# Optimizing a Trainium2 kernel written in Bass

```python
import numpy as np
import jax
import jax.numpy as jnp

def _softmax(x, axis=-1):
    return jax.nn.softmax(x, axis=axis)

def _gelu(x):
    return jax.nn.gelu(x, approximate=True)

def _silu(x):
    return jax.nn.silu(x)

def _sigmoid(x):
    return jax.nn.sigmoid(x)

def _layernorm(x, axis=-1, eps=1e-05):
    m = jnp.mean(x, axis=axis, keepdims=True)
    v = jnp.var(x, axis=axis, keepdims=True)
    return (x - m) / jnp.sqrt(v + eps)

def _scatter_add(tgt, idx, src, axis=0):
    return tgt.at[idx].add(src)

def _segment_sum(src, seg, n):
    return jax.ops.segment_sum(src, seg, n)
kernel_name = 'mk_gnn_preln_d4_gnn_r16_f88f90'

def setup_inputs(seed: int=0):
    np.random.seed(seed)
    _w = jnp.asarray

    def _rec_inputs():
        import jax
        import jax.numpy as jnp
        _gk = jax.random.key(seed)
        x = -0.0003713 + 1 * jax.random.normal(jax.random.fold_in(_gk, 1), (6250, 128), jnp.float32)
        _s = jax.random.randint(jax.random.fold_in(_gk, 2), (100000,), 0, 6250, jnp.int32)
        _d = jax.random.randint(jax.random.fold_in(_gk, 3), (100000,), 0, 6250, jnp.int32)
        _loop = jnp.arange(6250, dtype=jnp.int32)
        src = jnp.concatenate([_s, _d, _loop])
        dst = jnp.concatenate([_d, _s, _loop])
        _o = jnp.argsort(dst, stable=True)
        src = src[_o]
        dst = dst[_o]
        edge_weight = jax.random.uniform(jax.random.fold_in(_gk, 14), (206250,), jnp.float32, 0.0, 0.1)
        return (x, src, dst, edge_weight)
    x, src, dst, edge_weight = _rec_inputs()

    def _L0_gnn_setup():
        import jax, jax.numpy as jnp
        import numpy as np
        N_NODES = 6250
        N_EDGES = 200000
        D_IN = 128
        D_OUT = 128
        key = jax.random.key(seed)
        ks = jax.random.split(key, 8)
        x = jax.random.normal(ks[0], (N_NODES, D_IN), dtype=jnp.float32)
        scale = 1.0 / np.sqrt(D_IN)
        W1 = jax.random.normal(ks[1], (D_OUT, D_IN), dtype=jnp.float32) * scale
        b1 = jax.random.normal(ks[2], (D_OUT,), dtype=jnp.float32) * 0.01
        W2 = jax.random.normal(ks[3], (D_OUT, D_IN), dtype=jnp.float32) * scale
        b2 = jax.random.normal(ks[4], (D_OUT,), dtype=jnp.float32) * 0.01
        edge_val = jax.random.uniform(ks[5], (N_EDGES,), dtype=jnp.float32) * 0.1
        edge_src = jax.random.randint(ks[6], (N_EDGES,), 0, N_NODES, dtype=jnp.int32)
        edge_dst = jax.random.randint(ks[7], (N_EDGES,), 0, N_NODES, dtype=jnp.int32)
        return {'x': x, 'W1': W1, 'b1': b1, 'W2': W2, 'b2': b2, 'edge_val': edge_val, 'edge_src': edge_src, 'edge_dst': edge_dst}
    _L0_gnn_all = _L0_gnn_setup()
    _L0_gnn_in = {k: v for k, v in _L0_gnn_all.items() if k in ('W1', 'b1', 'W2', 'b2')}
    del _L0_gnn_all

    def _L1_gnn_setup():
        import jax, jax.numpy as jnp
        import numpy as np
        N = 3125
        E = 37500
        D = 128
        G = 8
        EPS = 1e-05
        key = jax.random.key(seed)
        ks = jax.random.split(key, 8)
        x = jax.random.normal(ks[0], (N, D), dtype=jnp.float32)
        edge_index = jax.random.randint(ks[1], (2, E), 0, N)
        batch = jnp.sort(jax.random.randint(ks[2], (N,), 0, G))
        s = 1.0 / np.sqrt(D)
        Wl = jax.random.normal(ks[3], (D, D), dtype=jnp.float32) * s
        bl = jax.random.normal(ks[4], (D,), dtype=jnp.float32) * s
        Wr = jax.random.normal(ks[5], (D, D), dtype=jnp.float32) * s
        return {'x': x, 'edge_index': edge_index, 'batch': batch, 'num_graphs': G, 'Wl': Wl, 'bl': bl, 'Wr': Wr, 'gn_weight': jnp.ones((D,), jnp.float32), 'gn_bias': jnp.zeros((D,), jnp.float32), 'mean_scale': jnp.ones((D,), jnp.float32)}
    _L1_gnn_all = _L1_gnn_setup()
    _L1_gnn_in = {k: v for k, v in _L1_gnn_all.items() if k in ('Wl', 'bl', 'Wr', 'gn_weight', 'gn_bias', 'mean_scale')}
    del _L1_gnn_all

    def _L2_gnn_setup():
        import jax, jax.numpy as jnp
        import numpy as np
        N_NODES = 6250
        N_CLIQUES = 3125
        N_EDGES = 100000
        D_IN = 128
        D_OUT = 128
        key = jax.random.key(seed)
        k1, k2, k3, k4, k5, k6 = jax.random.split(key, 6)
        x = jax.random.normal(k1, (N_NODES, D_IN), dtype=jnp.float32)
        x_clique = jax.random.normal(k2, (N_CLIQUES, D_IN), dtype=jnp.float32)
        node_idx = jax.random.randint(k3, (N_EDGES,), 0, N_NODES, dtype=jnp.int64)
        clique_idx = jax.random.randint(k4, (N_EDGES,), 0, N_CLIQUES, dtype=jnp.int64)
        node2clique_index = jnp.stack([node_idx, clique_idx], axis=0)
        W = jax.random.normal(k5, (D_OUT, D_IN), dtype=jnp.float32) * (1.0 / np.sqrt(D_IN))
        b = jax.random.normal(k6, (D_OUT,), dtype=jnp.float32) * 0.01
        return {'x': x, 'x_clique': x_clique, 'node2clique_index': node2clique_index, 'W': W, 'b': b}
    _L2_gnn_all = _L2_gnn_setup()
    _L2_gnn_in = {k: v for k, v in _L2_gnn_all.items() if k in ('x_clique', 'W', 'b')}
    del _L2_gnn_all

    def _L3_gnn_setup():
        import jax, jax.numpy as jnp
        import numpy as np
        N, E, D = (6250, 100000, 128)
        key = jax.random.key(seed)
        ks = jax.random.split(key, 10)
        s = 1.0 / np.sqrt(D)
        return {'x': jax.random.normal(ks[0], (N, D), dtype=jnp.float32), 'edge_index': jax.random.randint(ks[1], (2, E), 0, N, dtype=jnp.int64), 'W_in': jax.random.uniform(ks[2], (D, D), jnp.float32, -s, s), 'b_in': jnp.zeros((D,), jnp.float32), 'W_msg': jax.random.uniform(ks[3], (D, D), jnp.float32, -s, s), 'W_ih': jax.random.uniform(ks[4], (3 * D, D), jnp.float32, -s, s), 'b_ih': jax.random.uniform(ks[5], (3 * D,), jnp.float32, -s, s), 'W_hh': jax.random.uniform(ks[6], (3 * D, D), jnp.float32, -s, s), 'b_hh': jax.random.uniform(ks[7], (3 * D,), jnp.float32, -s, s), 'W_out': jax.random.uniform(ks[8], (D, D), jnp.float32, -s, s), 'b_out': jnp.zeros((D,), jnp.float32)}
    _L3_gnn_all = _L3_gnn_setup()
    _L3_gnn_in = {k: v for k, v in _L3_gnn_all.items() if k in ('W_in', 'b_in', 'W_msg', 'W_ih', 'b_ih', 'W_hh', 'b_hh', 'W_out', 'b_out')}
    del _L3_gnn_all
    return {'x': x, 'src': src, 'dst': dst, 'edge_weight': edge_weight, 'L0_gnn_W1': _L0_gnn_in['W1'], 'L0_gnn_b1': _L0_gnn_in['b1'], 'L0_gnn_W2': _L0_gnn_in['W2'], 'L0_gnn_b2': _L0_gnn_in['b2'], 'L1_gnn_Wl': _L1_gnn_in['Wl'], 'L1_gnn_bl': _L1_gnn_in['bl'], 'L1_gnn_Wr': _L1_gnn_in['Wr'], 'L1_gnn_gn_weight': _L1_gnn_in['gn_weight'], 'L1_gnn_gn_bias': _L1_gnn_in['gn_bias'], 'L1_gnn_mean_scale': _L1_gnn_in['mean_scale'], 'L2_gnn_x_clique': _L2_gnn_in['x_clique'], 'L2_gnn_W': _L2_gnn_in['W'], 'L2_gnn_b': _L2_gnn_in['b'], 'L3_gnn_W_in': _L3_gnn_in['W_in'], 'L3_gnn_b_in': _L3_gnn_in['b_in'], 'L3_gnn_W_msg': _L3_gnn_in['W_msg'], 'L3_gnn_W_ih': _L3_gnn_in['W_ih'], 'L3_gnn_b_ih': _L3_gnn_in['b_ih'], 'L3_gnn_W_hh': _L3_gnn_in['W_hh'], 'L3_gnn_b_hh': _L3_gnn_in['b_hh'], 'L3_gnn_W_out': _L3_gnn_in['W_out'], 'L3_gnn_b_out': _L3_gnn_in['b_out']}

def reference(x, src, dst, edge_weight, L0_gnn_W1, L0_gnn_b1, L0_gnn_W2, L0_gnn_b2, L1_gnn_Wl, L1_gnn_bl, L1_gnn_Wr, L1_gnn_gn_weight, L1_gnn_gn_bias, L1_gnn_mean_scale, L2_gnn_x_clique, L2_gnn_W, L2_gnn_b, L3_gnn_W_in, L3_gnn_b_in, L3_gnn_W_msg, L3_gnn_W_ih, L3_gnn_b_ih, L3_gnn_W_hh, L3_gnn_b_hh, L3_gnn_W_out, L3_gnn_b_out):
    import jax
    import jax.numpy as jnp

    def _L0_gnn_ref(x, W1, b1, W2, b2, edge_val, edge_src, edge_dst):
        import jax, jax.numpy as jnp
        import numpy as np
        N_NODES = 6250
        N_EDGES = 200000
        D_IN = 128
        D_OUT = 128
        msg = edge_val[:, None] * x[edge_src]
        neighbor = jax.ops.segment_sum(msg, edge_dst, num_segments=N_NODES)
        interaction = x * neighbor
        out = neighbor @ W1.T + b1 + interaction @ W2.T + b2
        return jax.nn.leaky_relu(out, negative_slope=0.2)

    def _L1_gnn_ref(x, edge_index, batch, num_graphs, Wl, bl, Wr, gn_weight, gn_bias, mean_scale):
        import jax, jax.numpy as jnp
        import numpy as np
        N = 3125
        E = 37500
        D = 128
        G = 8
        EPS = 1e-05
        n = x.shape[0]
        src, dst = (edge_index[0], edge_index[1])
        ones_e = jnp.ones(src.shape[0], dtype=x.dtype)
        deg = jax.ops.segment_sum(ones_e, dst, num_segments=n)
        agg = jax.ops.segment_sum(x[src], dst, num_segments=n)
        agg = agg / jnp.maximum(deg, 1.0)[:, None]
        f = agg @ Wl.T + bl + x @ Wr.T
        f = jax.nn.gelu(f, approximate=False)
        ones_n = jnp.ones(n, dtype=x.dtype)
        cnt = jax.ops.segment_sum(ones_n, batch, num_segments=num_graphs)[:, None]
        mean = jax.ops.segment_sum(f, batch, num_segments=num_graphs) / cnt
        out = f - mean_scale * mean[batch]
        var = jax.ops.segment_sum(out * out, batch, num_segments=num_graphs) / cnt
        out = out / jnp.sqrt(var[batch] + EPS) * gn_weight + gn_bias
        return out + x

    def _L2_gnn_ref(x, x_clique, node2clique_index, W, b):
        import jax, jax.numpy as jnp
        import numpy as np
        N_NODES = 6250
        N_CLIQUES = 3125
        N_EDGES = 100000
        D_IN = 128
        D_OUT = 128
        node_idx = node2clique_index[0]
        clique_idx = node2clique_index[1]
        n_nodes = x.shape[0]
        gathered = x_clique[clique_idx]
        summed = jax.ops.segment_sum(gathered, node_idx, num_segments=n_nodes)
        count = jax.ops.segment_sum(jnp.ones((gathered.shape[0],), dtype=x_clique.dtype), node_idx, num_segments=n_nodes)
        mean = summed / jnp.maximum(count, 1.0)[:, None]
        out = mean @ W.T + b
        return out

    def _L3_gnn_ref(x, edge_index, W_in, b_in, W_msg, W_ih, b_ih, W_hh, b_hh, W_out, b_out):
        import jax, jax.numpy as jnp
        import numpy as np
        N, E, D = (6250, 100000, 128)
        n_nodes = x.shape[0]
        src, dst = (edge_index[0], edge_index[1])
        h = x @ W_in.T + b_in
        m = h @ W_msg
        agg = jax.ops.segment_sum(m[src], dst, num_segments=n_nodes)
        gi = agg @ W_ih.T + b_ih
        gh = h @ W_hh.T + b_hh
        i_r, i_z, i_n = jnp.split(gi, 3, axis=-1)
        h_r, h_z, h_n = jnp.split(gh, 3, axis=-1)
        r = jax.nn.sigmoid(i_r + h_r)
        z = jax.nn.sigmoid(i_z + h_z)
        n = jnp.tanh(i_n + r * h_n)
        h_new = (1.0 - z) * n + z * h
        return h_new @ W_out.T + b_out
    edge_index = jnp.stack([src, dst])
    batch0 = jnp.zeros((6250,), jnp.int32)
    h = jnp.maximum(_layernorm(x, axis=-1), 0.0)
    x = x + _L0_gnn_ref(h, L0_gnn_W1, L0_gnn_b1, L0_gnn_W2, L0_gnn_b2, edge_weight, src, dst)
    h = jnp.maximum(_layernorm(x, axis=-1), 0.0)
    x = x + _L1_gnn_ref(h, edge_index, batch0, 8, L1_gnn_Wl, L1_gnn_bl, L1_gnn_Wr, L1_gnn_gn_weight, L1_gnn_gn_bias, L1_gnn_mean_scale)
    h = jnp.maximum(_layernorm(x, axis=-1), 0.0)
    x = x + _L2_gnn_ref(h, L2_gnn_x_clique, edge_index, L2_gnn_W, L2_gnn_b)
    h = jnp.maximum(_layernorm(x, axis=-1), 0.0)
    x = x + _L3_gnn_ref(h, edge_index, L3_gnn_W_in, L3_gnn_b_in, L3_gnn_W_msg, L3_gnn_W_ih, L3_gnn_b_ih, L3_gnn_W_hh, L3_gnn_b_hh, L3_gnn_W_out, L3_gnn_b_out)
    return x

_drawn_inputs = setup_inputs


def setup_inputs(seed=0):
    import zlib

    import numpy as np

    out = dict(_drawn_inputs(seed))
    spreads = {'L1_gnn_gn_weight': (1.0, 0.2),
     'L1_gnn_gn_bias': (0.0, 0.1),
     'L1_gnn_mean_scale': (1.0, 0.2),
     'L3_gnn_b_in': (0.0, 0.1),
     'L3_gnn_b_out': (0.0, 0.1)}
    factors = {'L0_gnn_b1': 8.0,
     'L0_gnn_b2': 7.451,
     'L2_gnn_b': 8.0,
     'L3_gnn_b_ih': 8.0,
     'L3_gnn_W_hh': 4.558,
     'L3_gnn_b_hh': 22.075}
    for name, (base, spread) in spreads.items():
        noise = np.random.default_rng([zlib.crc32(name.encode()), seed]).standard_normal(out[name].shape)
        drawn = base * np.exp(spread * noise) if base else spread * noise
        out[name] = jnp.asarray(drawn.astype(out[name].dtype))
    for name, factor in factors.items():
        out[name] = (out[name] * factor).astype(out[name].dtype)
    return out
```

```python
from contextlib import ExitStack

import concourse.bass as bass
from concourse import mybir

F32 = mybir.dt.float32
F16 = mybir.dt.float16
BF16 = mybir.dt.bfloat16
I32 = mybir.dt.int32
ALU = mybir.AluOpType
ACT = mybir.ActivationFunctionType
AX_X = mybir.AxisListType.X

P = 128
D = 128
N_NODES = 6250
N_CLIQUES = 3125
N_EDGES = 206250
EPS = 1e-5
SLOPE = 0.2

NB = -(-N_NODES // P)
NPAD = NB * P
SB = 7
NS = NB // SB
W = SB * P
LAST = N_NODES - (NB - 1) * P
TILE = 512
NT = -(-NPAD // TILE)
NCOL = NT * TILE

G = 6
K = 3
GS = 6
SUBS = 7
TD = G * GS * SUBS
HALF = TD // 2
NBLK = -(-N_NODES // TD)
BLK = NB * TD
CELLS = NB * G
NGT = -(-NBLK * GS * SUBS // P)
SHS = NB // SUBS
L2B = -(-N_CLIQUES // TD)
N_XC = L2B * TD

WIN = 32
WCH = 3
WPS = 3
CPS = WCH * WPS
STEPS = NBLK * SUBS
TAIL = 5
NCH = (STEPS + TAIL) * CPS
assert NCH * P >= N_EDGES and NCH % 2 == 0


def build_gnn(nc, A, out):
    with ExitStack() as ctx:
        def sb(name, shape, dt=F32):
            return ctx.enter_context(nc.sbuf_tensor(name, shape, dt))

        sems = {}

        def sem(name):
            if name not in sems:
                sems[name] = ctx.enter_context(nc.semaphore(name))
            return sems[name]

        x_dram = nc.dram_tensor("x_stream", (NPAD, D), F32).ap()
        rows_dram = nc.dram_tensor("node_rows", (NPAD, D), F32).ap()
        cells_dram = nc.dram_tensor("edge_counts", (NBLK, P, BLK), F16).ap()

        class Region:

            def __init__(self, name, words):
                self.t, self.words = sb(name, [P, words]), words

            def view(self, start, words, dt=F32):
                assert start + words <= self.words
                v = self.t[:, start:start + words]
                return v if dt == F32 else v.bitcast(dt)

        agg = sb("agg", [P, NCOL])
        carry = Region("carry", NPAD)
        big = Region("big", BLK)
        edge_area = Region("edge_area", 13600)

        at = 0

        def take(words, dt=F32):
            nonlocal at
            v = edge_area.view(at, words, dt)
            at += words
            return v

        keyT = take(K * NGT * P // 2, F16).rearrange("p (k g) -> p k g", k=K)
        slT = take(K * NGT * P // 2, F16).rearrange("p (k g) -> p k g", k=K)
        src_i = take(NCH, I32)
        rel = take(NCH)
        w_edge = take(NCH)
        oh_src = take(9 * P // 2, BF16).rearrange("p (s n) -> p s n", s=9)
        oh_cell = take(9 * CELLS // 2, BF16).rearrange("p (s n) -> p s n", s=9)
        gathered = take(CPS * D).rearrange("p (s n) -> p s n", s=CPS)
        oh_win = take(CPS * WIN).rearrange("p (s n) -> p s n", s=CPS)
        flipped_s = take(W // 2, F16)
        xc_plane = take(2 * 3 * D // 2, BF16).rearrange("p (c l n) -> p c l n", c=2, l=3)
        xc_in = take(2 * D)
        xc_r = take(2 * D)
        xc_r2 = take(2 * D)
        idx_slot = take(CPS, I32)
        planes = edge_area.view(0, 3 * NPAD // 2, BF16).rearrange("p (l b n) -> p l b n", l=3, b=NB)

        count_blk = big.view(0, BLK, F16)
        piece = big.view(0, BLK // 2, F16).rearrange("p (k n) -> p k n", k=SUBS)
        dmax_i, dmin_i = big.view(0, NCH, I32), big.view(NCH, NCH, I32)
        dmax_f, dmin_f = big.view(2 * NCH, NCH), big.view(3 * NCH, NCH)
        scr = big.view(4 * NCH, NCH)
        dst_i, next_i = big.view(5 * NCH, NCH, I32), big.view(6 * NCH, NCH, I32)
        NW3 = NGT * K * P
        dst_rows_i, src_rows_i = carry.view(0, NW3, I32), agg[:, 0:NW3].bitcast(I32)
        key_a, key_b, key_c = big.view(0, NW3), big.view(NW3, NW3), big.view(2 * NW3, NW3)
        key_ai = big.view(0, NW3, I32)
        f_all = big.view(0, NPAD).rearrange("p (b d) -> p b d", d=D)
        prod_s, r_s, z_s, n_s = (big.view(BLK - (n + 1) * W, W) for n in range(4))
        sq_all = agg[:, 0:NPAD].rearrange("p (b d) -> p b d", d=D)
        hidden_all = carry.view(0, NPAD)
        clique_sum = carry.view(0, NPAD)
        g_src, g_dst, g_idx = (edge_area.view(n * NCH, NCH, I32) for n in range(3))
        g_key, g_w = edge_area.view(3 * NCH, NCH), edge_area.view(4 * NCH, NCH)
        g_count = big.view(0, NCOL)
        g_onehot = big.view(NCOL, 2 * TILE).rearrange("p (s n) -> p s n", s=2)
        g_rows = big.view(NCOL + 2 * TILE, 2 * D).rearrange("p (s n) -> p s n", s=2)
        g_iota_i = big.view(NCOL + 2 * TILE + 2 * D, TILE, I32)
        g_iota = big.view(NCOL + 3 * TILE + 2 * D, TILE)

        xs = sb("xs", [P, SB, D])
        hs = sb("hs", [P, SB, D])
        agg_s = sb("agg_s", [P, W])
        hT_s = sb("hT_s", [P, W])
        stats = sb("stats", [P, SB, 6])
        mv = sb("mv", [P, SB, 2])
        rstd = sb("rstd", [P, SB])
        scaled_mean = sb("scaled_mean", [P, D])
        gain = sb("gain", [P, D])
        ones = sb("ones", [P, P])
        ident = sb("ident", [P, P])
        ones16 = sb("ones16", [P, P], BF16)
        ident16 = sb("ident16", [P, P], F16)
        iota_i = sb("iota_i", [P, CELLS], I32)
        iota16 = sb("iota16", [P, CELLS], F16)
        iota_win = sb("iota_win", [P, WIN])
        chunk_slot = sb("chunk_slot", [P, 2], I32)
        tile_off_i = sb("tile_off_i", [P, NT], I32)
        tile_off = sb("tile_off", [P, NT])
        tile_key = sb("tile_key", [P, NT])
        gbase_i = sb("gbase_i", [P, NGT], I32)
        gbase = sb("gbase", [P, NGT])
        glast = sb("glast", [P, NGT])
        first_chunk = sb("first_chunk", [P, NGT])
        chunk_end = sb("chunk_end", [P, NGT])
        chunk_idx = sb("chunk_idx", [P, K, NGT], I32)
        win_base = sb("win_base", [1, WPS + NCH // WCH], I32)
        win_sum = sb("win_sum", [P, WPS * WIN])
        bad3 = sb("bad3", [P, 3])
        bad = sb("bad", [P, 1])
        any_order = sb("any_order", [P, 1], I32)
        out_part = sb("out_part", [P, SHS])
        out_cnt = sb("out_cnt", [P, 2, NB])
        inv_cnt = sb("inv_cnt", [P, NB])
        last_col = sb("last_col", [P, 1])
        last_clique = sb("last_clique", [P, P])
        clique_out = sb("clique_out", [P, D])
        wt = {n: sb("w_" + n, [P, A[n].shape[1]]) for n in
              ("W1T", "W2T", "WlT", "WrT", "WcT", "WinT", "Wmsg", "WihT", "WhhT", "WoutT")}
        bias = {n: sb("b_" + n, [A[n].shape[0], A[n].shape[1]]) for n in ("b12", "bl", "bgru", "bhn", "bout")}
        b_in = sb("b_in", [P, 1])
        bcast = {n: sb("bc_" + n, [P, D]) for n in ("gn_weight", "gn_bias", "mean_scale", "bc")}
        N_CONST_LOADS = len(wt) + len(bias) + 2 + len(bcast)

        ps = ctx.enter_context(nc.psum_tensor("ps", [P, 8 * TILE], F32))
        pA, pB, pC, pD = (ps[:, n * 2 * TILE:(n + 1) * 2 * TILE] for n in range(4))
        p_cells = ps[:, 0:3 * TILE].rearrange("p (s n) -> p s n", s=3)
        p_flip = ps[:, 3 * TILE:3 * TILE + W]
        p_mix = ps[:, 5 * TILE:5 * TILE + W]
        p_win = ps[:, 7 * TILE:7 * TILE + WPS * WIN]

        def rows_of(t, i):
            return t[bass.ds(i * W, W), :].rearrange("(b p) d -> p b d", p=P)

        def steps_of(v, i):
            return v[:, bass.ds(i * W, W)]

        def flat(t):
            return t[:].rearrange("p b d -> p (b d)")

        def blocks(v):
            return v.rearrange("p (b d) -> p b d", d=D)

        GEN = {0: (rows_dram, True, False), 1: (rows_dram, False, True),
               2: (A["x_clique"], False, True), 3: (rows_dram, False, False)}
        MM_CREDIT = 2 * NT

        def mm_base(l):
            return l * (NCH * NT + MM_CREDIT)

        CELL_RING = 3
        WIN_RING = WPS

        block = ctx.enter_context(nc.Block())

        def branch(eng, order, general, sorted_):
            with eng.If(order > 0):
                general()
            with eng.Else():
                sorted_()

        @block.sync
        def _(sp):
            sp.dma_start(dmax_i, A["dstT"][P - 1:P, :].to_broadcast([P, NCH])).then_inc(sem("ends_in"), 16)
            sp.dma_start(dmin_i, A["dstT"][0:1, :].to_broadcast([P, NCH])).then_inc(sem("ends_in"), 16)
            sp.dma_start(win_base[:], A["win_base_src"]).then_inc(sem("ends_in"), 16)
            sp.dma_start(dst_i, A["dstT"]).then_inc(sem("dst_in"), 16)
            sp.dma_start(next_i[0:P - 1, :], A["dstT"][1:P, :]).then_inc(sem("next_in"), 16)
            sp.dma_start(next_i[P - 1:P, 0:NCH - 1], A["dstT"][0:1, 1:NCH]).then_inc(sem("next_in"), 16)
            sp.dma_start(next_i[P - 1:P, NCH - 1:NCH], A["dstT"][P - 1:P, NCH - 1:NCH]).then_inc(sem("next_in"), 16)

            def stage(s, source, new_x, with_h):
                with sp.Fori(0, NS) as i:
                    sp.wait_ge(sem(f"h_ready{s}"), i + 1)
                    sp.dma_start(xs[:], rows_of(source, i)).then_inc(sem(f"x_in{s}"), 16)
                    if with_h:
                        sp.dma_start(hs[:], rows_of(rows_dram, i)).then_inc(sem(f"h_in{s}"), 16)
                    if new_x:
                        sp.wait_ge(sem(f"x_new{s}"), i + 1)
                        sp.dma_start(rows_of(x_dram, i), xs[:]).then_inc(sem(f"x_out{s}"), 16)
                    sp.wait_ge(sem(f"h_rows{s}"), i + 1)
                    sp.dma_start(rows_of(rows_dram, i), hs[:]).then_inc(sem(f"rows_out{s}"), 16)
                    if new_x:
                        sp.wait_ge(sem(f"x_out{s}"), i * 16 + 16)
                        sp.sem_inc(sem(f"x_saved{s}"), 1)
                    sp.wait_ge(sem(f"rows_out{s}"), i * 16 + 16)
                    sp.sem_inc(sem(f"rows_saved{s}"), 1)
                sp.sem_inc(sem(f"rows_written{s}"), 1)

            stage(0, A["x"], False, False)
            sp.dma_start(src_i, A["srcT"]).then_inc(sem("edges_in"), 16)
            sp.dma_start(w_edge, A["wT"]).then_inc(sem("edges_in"), 16)
            for n, t in (*wt.items(), *bias.items()):
                sp.dma_start(t[:], A[n]).then_inc(sem("consts_in"), 16)
            sp.dma_start(b_in[:], A["b_in"]).then_inc(sem("consts_in"), 16)
            sp.dma_start(last_col[:], A["last_clique"]).then_inc(sem("consts_in"), 16)
            for n, t in bcast.items():
                sp.dma_start(t[:], A[n].to_broadcast([P, D])).then_inc(sem("consts_in"), 16)

            sp.wait_ge(sem("order_known"), 1)
            order = sp.value_load(any_order[0:1, 0:1], min_val=0, max_val=1)

            def edges_any(l):
                def f():
                    sp.wait_ge(sem(f"area_free{l}"), 1)
                    sp.wait_ge(sem("edges_in"), 32)
                    for t, n in ((g_src, "srcT"), (g_dst, "dstT"), (g_w, "wT")):
                        sp.dma_start(t, A[n]).then_inc(sem("g_edges"), 16)
                return f

            def store_block(b, with_clique):
                if with_clique:
                    sp.wait_ge(sem("xc_split"), b + 1)
                    sp.dma_start(xc_in[0:HALF, :].rearrange("p (c d) -> p c d", c=2),
                                 A["x_clique"][bass.ds(b * TD, TD), :].rearrange("(c p) d -> p c d", p=HALF)
                                 ).then_inc(sem("xc_loaded"), 16)
                sp.wait_ge(sem("stored"), b * (GS * SUBS) + GS * SUBS + CELL_RING)
                sp.dma_start(cells_dram[bass.ds(b, 1), :, :].rearrange("o p n -> p (o n)"),
                             count_blk[:, bass.ds((b % 2) * BLK, BLK)]).then_inc(sem("cells_out"), 16)
                sp.wait_ge(sem("cells_out"), b * 16 + 16)
                sp.sem_inc(sem("block_saved"), 1)

            def count_sorted():
                sp.sem_inc(sem("block_saved"), 1)
                with sp.Fori(0, L2B) as b:
                    store_block(b, True)
                with sp.Fori(L2B, NBLK) as b:
                    store_block(b, False)

            def load_pieces(l):
                before = 0 if l == 1 else 1

                def f():
                    if l == 1:
                        sp.wait_ge(sem("agg_done0"), 1)
                    else:
                        sp.wait_ge(sem("area_free3"), 1)
                    with sp.Fori(0, NBLK) as b:
                        for k in range(SUBS):
                            sp.wait_ge(sem("piece_used"), b * SUBS + before * (NBLK + 1) * SUBS + k + 1)
                            sp.dma_start(piece[:, k, :],
                                         cells_dram[bass.ds(b, 1), :, k * SHS * TD:(k + 1) * SHS * TD].rearrange(
                                             "o p n -> p (o n)")).then_inc(sem(f"piece{k}"), 16)
                return f

            branch(sp, order, edges_any(0), count_sorted)

            stage(1, A["x"], True, True)
            branch(sp, order, edges_any(1), load_pieces(1))
            with sp.Fori(0, NS) as i:
                sp.wait_ge(sem("h_free2"), i + 1)
                sp.dma_start(hs[:], rows_of(rows_dram, i)).then_inc(sem("h_in2a"), 16)
            stage(2, x_dram, True, True)
            branch(sp, order, edges_any(2), lambda: sp.sem_inc(sem("idle"), 1))
            stage(3, x_dram, True, False)
            with sp.Fori(0, NS) as i:
                sp.wait_ge(sem("msg_free"), i + 1)
                sp.dma_start(hs[:], rows_of(rows_dram, i)).then_inc(sem("h_in4"), 16)
                sp.wait_ge(sem("msg_rows"), i + 1)
                sp.dma_start(rows_of(rows_dram, i), hs[:]).then_inc(sem("msg_out"), 16)
                sp.wait_ge(sem("msg_out"), i * 16 + 16)
                sp.sem_inc(sem("msg_saved"), 1)
            branch(sp, order, edges_any(3), load_pieces(3))
            with sp.Fori(0, NS) as i:
                sp.wait_ge(sem("y_ready"), i + 1)
                sp.dma_start(xs[:], rows_of(x_dram, i)).then_inc(sem("x_in4"), 16)
                sp.wait_ge(sem("y_ready"), i + 2)
                sp.dma_start(rows_of(out, i), xs[:]).then_inc(sem("y_out"), 16)
                sp.wait_ge(sem("y_out"), i * 16 + 16)
                sp.sem_inc(sem("y_saved"), 1)

        @block.gpsimd
        def _(pool):
            nc.gpsimd.iota(iota_i[:], pattern=[[1, CELLS]], base=0, channel_multiplier=0).then_inc(sem("made"), 1)
            nc.gpsimd.iota(tile_off_i[:], pattern=[[-TILE, NT]], base=0, channel_multiplier=0).then_inc(sem("made"), 1)
            nc.gpsimd.iota(gbase_i[:], pattern=[[G * P, NGT]], base=0, channel_multiplier=G).then_inc(sem("made"), 1)
            nc.gpsimd.memset(ident[:], 0.0)
            nc.gpsimd.memset(ones16[:], 1.0)
            nc.gpsimd.memset(ones[:], 1.0).then_inc(sem("made"), 1)
            pool.drain()
            nc.gpsimd.affine_select(out=ident[:], in_=ident[:], compare_op=ALU.not_equal, fill=1.0, base=0,
                                    pattern=[[-1, P]], channel_multiplier=1).then_inc(sem("made"), 1)
            pool.wait_ge(sem("chunks_known"), 1)
            for g in range(NGT):
                for k in range(K):
                    for rows, table in ((dst_rows_i, A["dst_rows"]), (src_rows_i, A["src_rows"])):
                        n = (k * NGT + g) * P
                        pool.indirect_dma_start(
                            out=rows[:, n:n + P], out_offset=None, in_=table,
                            in_offset=bass.IndirectOffsetOnAxis(ap=chunk_idx[:, k, g:g + 1], axis=0),
                        ).then_inc(sem("chunk_rows"), 16)
            pool.wait_ge(sem("order_known"), 1)
            order = pool.value_load(any_order[0:1, 0:1], min_val=0, max_val=1)

            def gather_windows(t):
                pool.drain()
                nc.gpsimd.tensor_copy(idx_slot, src_i[:, bass.ds(t * CPS, CPS)])
                pool.drain()
                for w in range(WPS):
                    pool.wait_ge(sem("win_mm"), t * WPS + w + 1)
                    pool.sem_inc(sem("win_slot_taken"), 1)
                    for k in range(w * WCH, (w + 1) * WCH):
                        pool.indirect_dma_start(
                            out=gathered[:, k, :], out_offset=None, in_=rows_dram,
                            in_offset=bass.IndirectOffsetOnAxis(ap=idx_slot[:, k:k + 1], axis=0),
                        ).then_inc(sem(f"win_row{k}"), 16)

            def windows_sorted():
                pool.wait_ge(sem("edges_in"), 32)
                pool.wait_ge(sem("rows_written0"), 1)
                with pool.Fori(0, STEPS + TAIL) as t:
                    gather_windows(t)

            def gather_any(l):
                def f():
                    table = GEN[l][0]
                    index = g_idx if l == 2 else g_src
                    if l != 2:
                        pool.wait_ge(sem("msg_saved" if l == 3 else f"rows_saved{l}"), NS)
                    pool.wait_ge(sem("g_ready"), l + 1)
                    with pool.Fori(0, NCH // 2) as j:
                        pool.wait_ge(sem("g_mm"), j * (2 * NT) + mm_base(l) + 2 * NT)
                        pool.sem_inc(sem("g_slots_taken"), 1)
                        nc.gpsimd.tensor_copy(chunk_slot[:], index[:, bass.ds(j * 2, 2)])
                        pool.drain()
                        for k in range(2):
                            pool.indirect_dma_start(
                                out=g_rows[:, k, :], out_offset=None, in_=table,
                                in_offset=bass.IndirectOffsetOnAxis(ap=chunk_slot[:, k:k + 1], axis=0),
                            ).then_inc(sem(f"g_row{k}"), 16)
                return f

            def idle():
                pool.sem_inc(sem("idle"), 1)

            branch(pool, order, gather_any(0), windows_sorted)
            branch(pool, order, gather_any(1), idle)
            branch(pool, order, gather_any(2), idle)
            branch(pool, order, gather_any(3), idle)

        @block.tensor
        def _(pe):
            mm = nc.tensor.matmul
            pe.wait_ge(sem("made"), 5)
            pe.wait_ge(sem("keys_made"), 1)
            for n in range(K * NGT):
                last = nc.tensor.transpose(ps[:, n * P:(n + 1) * P], key_b[:, n * P:(n + 1) * P], ident[:])
            last.then_inc(sem("keys_flipped"), 1)
            pe.wait_ge(sem("keyT_ready"), 1)
            for n in range(K * NGT):
                last = nc.tensor.transpose(ps[:, n * P:(n + 1) * P], key_c[:, n * P:(n + 1) * P], ident[:])
            last.then_inc(sem("sources_flipped"), 1)
            pe.wait_ge(sem("slT_ready"), 1)
            mm(ps[:, 0:1], ones[:], bad[:], start=True, stop=True).then_inc(sem("bad_summed"), 1)
            pe.wait_ge(sem("consts_in"), 16 * N_CONST_LOADS)
            pe.wait_ge(sem("order_known"), 1)
            order = pe.value_load(any_order[0:1, 0:1], min_val=0, max_val=1)

            def sum_any(l):
                counted = GEN[l][2]

                def f():
                    pe.sem_inc(sem("g_mm"), MM_CREDIT)
                    with pe.Fori(0, NCH // 2) as j:
                        for k in range(2):
                            pe.wait_ge(sem(f"g_row{k}"), j * 16 + (l * (NCH // 2) + 1) * 16)
                            for t in range(NT):
                                n = k * NT + t
                                cols = slice((n % 2) * TILE, (n % 2 + 1) * TILE)
                                pe.wait_ge(sem("g_onehot"), j * (2 * NT) + l * NCH * NT + n + 1)
                                pe.wait_ge(sem("g_added"), j * (2 * NT) + l * (NCH * NT + 2) + n + 1)
                                last = mm(pA[:, cols], g_rows[:, k, :], g_onehot[:, n % 2, :], start=True, stop=True)
                                if counted:
                                    last = mm(pB[:, cols], ones[:], g_onehot[:, n % 2, :], start=True, stop=True)
                                last.then_inc(sem("g_mm"), 1)
                return f

            def count_group(t, g):
                pe.wait_ge(sem("onehots"), t * GS + g + 1)
                pe.wait_ge(sem("stored"), t * GS + g + 1)
                for k in range(K):
                    s = (g % 3) * K + k
                    last = mm(p_cells[:, g % 3, 0:CELLS], oh_src[:, s, :], oh_cell[:, s, :],
                              start=(k == 0), stop=(k == K - 1))
                last.then_inc(sem("cells"), 1)

            def flip(b, sub, c):
                pe.wait_ge(sem("flip_copied"), b * (2 * SUBS) + sub * 2 + c + 1)
                if c == 0:
                    pe.wait_ge(sem("stored"), b * (GS * SUBS) + GS * SUBS + CELL_RING)
                for j in range(SHS):
                    last = mm(p_flip[0:HALF, j * P:(j + 1) * P],
                              count_blk[:, bass.ds((b % 2) * BLK + (sub * SHS + j) * TD + c * HALF, HALF)],
                              ident16[:], start=True, stop=True)
                last.then_inc(sem("flips"), 1)

            def mix(b, sub, c):
                pe.wait_ge(sem("flip_copied"), b * (2 * SUBS) + sub * 2 + c + 2)
                if c == 0:
                    pe.wait_ge(sem("xc_split"), b + 2)
                    pe.wait_ge(sem("mix_added"), b * SUBS + sub + 1)
                for lo, n in ((0, TILE), (TILE, W - TILE)):
                    for l in range(3):
                        last = mm(p_mix[:, lo:lo + n], xc_plane[0:HALF, c, l, :], flipped_s[0:HALF, lo:lo + n],
                                  start=(c == 0 and l == 0), stop=(c == 1 and l == 2))
                last.then_inc(sem("mixed"), 1)

            def window(t, w):
                if w == 0:
                    pe.wait_ge(sem("win_copied"), t + 1)
                pe.wait_ge(sem("win_onehots"), t * WPS + w + 1)
                for k in range(WCH):
                    s = w * WCH + k
                    pe.wait_ge(sem(f"win_row{s}"), t * 16 + 16)
                    last = mm(p_win[:, w * WIN:(w + 1) * WIN], gathered[:, s, :], oh_win[:, s, :], start=(k == 0), stop=(k == WCH - 1))
                last.then_inc(sem("win_mm"), 1)

            def step(blk, sub, clique):
                t = blk * SUBS + sub
                b = blk - 1
                count_group(t, 0)
                if clique:
                    flip(b, sub, 0)
                count_group(t, 1)
                count_group(t, 2)
                if clique:
                    mix(b, sub, 0)
                    flip(b, sub, 1)
                count_group(t, 3)
                window(t, 0)
                count_group(t, 4)
                if clique:
                    mix(b, sub, 1)
                window(t, 1)
                count_group(t, 5)
                window(t, 2)

            def count_sorted():
                pe.sem_inc(sem("cells"), CELL_RING)
                pe.sem_inc(sem("win_mm"), WIN_RING)
                pe.sem_inc(sem("flips"), 2 * SUBS)
                pe.sem_inc(sem("mixed"), 1)
                with pe.Fori(0, SUBS) as sub:
                    step(0, sub, False)
                with pe.Fori(1, L2B + 1) as blk:
                    with pe.Fori(0, SUBS) as sub:
                        step(blk, sub, True)
                with pe.Fori(L2B + 1, NBLK) as blk:
                    with pe.Fori(0, SUBS) as sub:
                        step(blk, sub, False)
                with pe.Fori(STEPS, STEPS + TAIL) as t:
                    for w in range(WPS):
                        window(t, w)

            def multiply(l):
                def f():
                    before = 0 if l == 1 else 1
                    pe.sem_inc(sem("piece_used"), SUBS)
                    pe.wait_ge(sem(f"planes_ready{l}"), NS)
                    with pe.Fori(0, NBLK) as b:
                        slot = (b % 2) * (2 * TILE)
                        pe.wait_ge(sem("taken"), b + before * (NBLK + 2) + 1)
                        for k in range(SUBS):
                            pe.wait_ge(sem(f"piece{k}"), b * 16 + before * NBLK * 16 + 16)
                            for j in range(SHS):
                                sh = k * SHS + j
                                cells = piece[:, k, j * TD:(j + 1) * TD]
                                for p in range(3):
                                    last = mm(ps[:, bass.ds(slot, TD)], planes[:, p, sh, :], cells,
                                              start=(sh == 0 and p == 0), stop=(sh == NB - 1 and p == 2))
                                if l == 1:
                                    last = mm(ps[:, bass.ds(slot + TILE, TD)], ones16[:], cells, start=(sh == 0),
                                              stop=(sh == NB - 1))
                            last.then_inc(sem("piece_used"), 1)
                return f

            def transposes(dst_ps, source):
                for b in range(SB):
                    last = nc.tensor.transpose(dst_ps[:, b * P:(b + 1) * P], source[:, b * P:(b + 1) * P], ident[:])
                return last

            def product(dst_ps, terms):
                for b in range(SB):
                    for n, (lhs, rhs) in enumerate(terms):
                        k = rhs.shape[0]
                        lhsT = lhs[:, b * P:(b + 1) * P] if k == P else lhs[0:k, :]
                        last = mm(dst_ps[:, b * D:(b + 1) * D], lhsT, rhs, start=(n == 0), stop=(n == len(terms) - 1))
                return last

            def column_sums(source):
                mm(pC[:, 0:D], ones[0:LAST, :], source[0:LAST, NB - 1, :], start=True, stop=False)
                with pe.Fori(0, NB - 2) as b:
                    mm(pC[:, 0:D], ones[:], source[:, bass.ds(b, 1), :].rearrange("p b d -> p (b d)"),
                       start=False, stop=False)
                return mm(pC[:, 0:D], ones[:], source[:, NB - 2, :], start=False, stop=True)

            branch(pe, order, sum_any(0), count_sorted)
            with pe.Fori(0, NS) as i:
                pe.wait_ge(sem("h_in1"), i * 16 + 16)
                pe.wait_ge(sem("agg_done0"), 1)
                transposes(pA, flat(hs)).then_inc(sem("hT1"), 1)
                pe.wait_ge(sem("prod1"), i + 1)
                pe.wait_ge(sem("agg_staged1"), i + 1)
                product(pB, [(agg_s, wt["W1T"][:]), (prod_s, wt["W2T"][:]), (ones, bias["b12"][:])]).then_inc(
                    sem("lin1"), 1)
            pe.wait_ge(sem("h_ready1"), NS + 1)
            branch(pe, order, sum_any(1), multiply(1))
            with pe.Fori(0, NS) as i:
                pe.wait_ge(sem("h_in2a"), i * 16 + 16)
                pe.wait_ge(sem("agg_done1"), 1)
                transposes(pA, flat(hs)).then_inc(sem("hT2"), 1)
                pe.wait_ge(sem("hT_s2"), i + 1)
                pe.wait_ge(sem("agg_staged2"), i + 1)
                product(pB, [(agg_s, wt["WlT"][:]), (hT_s, wt["WrT"][:]), (ones, bias["bl"][:])]).then_inc(
                    sem("lin2"), 1)
            pe.wait_ge(sem("gelu"), NS)
            column_sums(f_all).then_inc(sem("mean_sum"), 1)
            pe.wait_ge(sem("squared"), 1)
            column_sums(sq_all).then_inc(sem("var_sum"), 1)
            pe.wait_ge(sem("h_ready2"), NS + 1)
            branch(pe, order, sum_any(2), lambda: pe.sem_inc(sem("idle"), 1))
            pe.wait_ge(sem("agg_done2"), 1)
            mm(pC[:, 0:D], last_clique[:], wt["WcT"][:], start=True, stop=True).then_inc(sem("clique_lin"), 1)
            with pe.Fori(0, NS) as i:
                pe.wait_ge(sem("agg_staged3"), i + 1)
                product(pB, [(agg_s, wt["WcT"][:])]).then_inc(sem("lin3"), 1)
            with pe.Fori(0, NS) as i:
                pe.wait_ge(sem("h_in4"), i * 16 + 16)
                transposes(pA, flat(hs)).then_inc(sem("hT4"), 1)
                pe.wait_ge(sem("hT_s4"), i + 1)
                mm(pB[:, 0:TILE], wt["WinT"][:], hT_s[:, 0:TILE], start=True, stop=True)
                mm(pB[:, TILE:W], wt["WinT"][:], hT_s[:, TILE:W], start=True, stop=True).then_inc(sem("hidden"), 1)
                pe.wait_ge(sem("hidden_s"), i + 1)
                product(pC, [(prod_s, wt["Wmsg"][:])]).then_inc(sem("msg"), 1)
            pe.wait_ge(sem("msg_free"), NS + 1)
            branch(pe, order, sum_any(3), multiply(3))
            with pe.Fori(0, NS) as i:
                ih, hh = wt["WihT"], wt["WhhT"]
                pe.wait_ge(sem("agg_done3"), 1)
                pe.wait_ge(sem("gru_staged"), i + 1)
                product(pA, [(agg_s, ih[:, 0:D]), (hT_s, hh[:, 0:D]), (ones, bias["bgru"][:, 0:D])])
                product(pB, [(agg_s, ih[:, D:2 * D]), (hT_s, hh[:, D:2 * D]), (ones, bias["bgru"][:, D:2 * D])])
                product(pC, [(agg_s, ih[:, 2 * D:]), (ones, bias["bgru"][0:1, 2 * D:])])
                product(pD, [(hT_s, hh[:, 2 * D:]), (ones, bias["bhn"][:])]).then_inc(sem("gates"), 1)
                pe.wait_ge(sem("tanh"), i + 1)
                transposes(pA, hT_s).then_inc(sem("hidden_rows"), 1)
                pe.wait_ge(sem("h_new"), i + 1)
                transposes(pB, prod_s).then_inc(sem("h_newT"), 1)
                pe.wait_ge(sem("h_newT_s"), i + 1)
                product(pC, [(r_s, wt["WoutT"][:]), (ones, bias["bout"][:])]).then_inc(sem("out_rows"), 1)

        @block.scalar
        def _(act):
            def ln_std(s, i):
                act.wait_ge(sem(f"ln_var{s}"), i + 1)
                nc.scalar.activation(rstd[:], rstd[:], ACT.Sqrt).then_inc(sem(f"ln_std{s}"), 1)

            def stage_agg(s, i):
                nc.scalar.copy(agg_s[:], agg[:, bass.ds(i * W, W)]).then_inc(sem(f"agg_staged{s}"), 1)

            with act.Fori(0, NS) as i:
                ln_std(0, i)
            act.wait_ge(sem("order_known"), 1)
            order = act.value_load(any_order[0:1, 0:1], min_val=0, max_val=1)

            def store_group(blk, sub, g):
                act.wait_ge(sem("cells"), (blk * SUBS + sub) * GS + g + 1 + CELL_RING)
                cells = count_blk[:, bass.ds((blk % 2) * BLK, BLK)].rearrange("p (s d) -> p s d", d=TD)
                nc.scalar.copy(cells[:, :, bass.ds((sub * GS + g) * G, G)],
                               p_cells[:, g % 3, 0:CELLS].rearrange("p (s d) -> p s d", d=G)).then_inc(
                    sem("stored"), 1)

            def copy_flip(b, sub, c):
                act.wait_ge(sem("flips"), b * (2 * SUBS) + sub * 2 + c + 1 + 2 * SUBS)
                act.wait_ge(sem("mixed"), b * (2 * SUBS) + sub * 2 + c + 1)
                nc.scalar.copy(flipped_s[0:HALF, :], p_flip[0:HALF, :]).then_inc(sem("flip_copied"), 1)

            def step(blk, sub, clique):
                for g in range(GS):
                    store_group(blk, sub, g)
                    if clique and g == 1:
                        copy_flip(blk - 1, sub, 0)
                    if clique and g == 3:
                        copy_flip(blk - 1, sub, 1)

            def slot_free(blk, flips):
                act.wait_ge(sem("flips"), flips)
                act.wait_ge(sem("reduced"), blk * SUBS)
                act.wait_ge(sem("block_saved"), blk)
                act.sem_inc(sem("block_begun"), 1)

            def count_sorted():
                act.sem_inc(sem("stored"), CELL_RING)
                act.sem_inc(sem("flip_copied"), 1)
                with act.Fori(0, SUBS) as sub:
                    step(0, sub, False)
                with act.Fori(1, L2B + 1) as blk:
                    slot_free(blk, blk * (2 * SUBS))
                    with act.Fori(0, SUBS) as sub:
                        step(blk, sub, True)
                with act.Fori(L2B + 1, NBLK) as blk:
                    slot_free(blk, (L2B + 1) * 2 * SUBS)
                    with act.Fori(0, SUBS) as sub:
                        step(blk, sub, False)

            branch(act, order, lambda: act.sem_inc(sem("idle"), 1), count_sorted)
            act.wait_ge(sem("agg_done0"), 1)
            with act.Fori(0, NS) as i:
                act.wait_ge(sem("h_ready1"), i + 1)
                stage_agg(1, i)
                ln_std(1, i)
            act.wait_ge(sem("agg_done1"), 1)
            with act.Fori(0, NS) as i:
                stage_agg(2, i)
                act.wait_ge(sem("lin2"), i + 1)
                nc.scalar.activation(f_all[:, bass.ds(i * SB, SB), :], blocks(pB[:, 0:W]), ACT.Gelu).then_inc(
                    sem("gelu"), 1)
            act.wait_ge(sem("centred"), 1)
            nc.scalar.activation(sq_all, f_all, ACT.Square).then_inc(sem("squared"), 1)
            act.wait_ge(sem("var_ready"), 1)
            nc.scalar.activation(gain[:], gain[:], ACT.Sqrt).then_inc(sem("std_ready"), 1)
            with act.Fori(0, NS) as i:
                ln_std(2, i)
            act.wait_ge(sem("agg_done2"), 1)
            with act.Fori(0, NS) as i:
                act.wait_ge(sem("h_ready3"), i + 1)
                stage_agg(3, i)
                ln_std(3, i)
            act.wait_ge(sem("agg_done3"), 1)
            with act.Fori(0, NS) as i:
                act.wait_ge(sem("y_ready"), i + 1)
                nc.scalar.copy(agg_s[:], agg[:, bass.ds(i * W, W)])
                nc.scalar.copy(hT_s[:], steps_of(hidden_all, i)).then_inc(sem("gru_staged"), 1)
                act.wait_ge(sem("gates"), i + 1)
                nc.scalar.activation(r_s, pA[:, 0:W], ACT.Sigmoid).then_inc(sem("r_ready"), 1)
                nc.scalar.activation(z_s, pB[:, 0:W], ACT.Sigmoid)
                act.wait_ge(sem("n_in"), i + 1)
                nc.scalar.activation(n_s, n_s, ACT.Tanh).then_inc(sem("tanh"), 1)

        @block.vector
        def _(dve):
            V = nc.vector
            dve.wait_ge(sem("made"), 5)
            V.tensor_copy(iota16[:], iota_i[:])
            V.tensor_copy(iota_win[:], iota_i[:, 0:WIN])
            V.tensor_copy(tile_off[:], tile_off_i[:])
            V.tensor_copy(ident16[:], ident[:])
            V.tensor_copy(gbase[:], gbase_i[:])
            dve.drain()
            V.tensor_scalar(glast[:], gbase[:], float(G - 1), float(N_NODES - 1), ALU.add, ALU.min)
            dve.wait_ge(sem("ends_in"), 48)
            V.tensor_copy(dmax_f, dmax_i)
            V.tensor_copy(dmin_f, dmin_i)
            dve.drain()
            for g in range(NGT):
                for ends, bound, op, count in ((dmax_f, gbase, ALU.is_lt, first_chunk),
                                               (dmin_f, glast, ALU.is_le, chunk_end)):
                    V.tensor_scalar(scr, ends, bound[:, g:g + 1], None, op)
                    dve.drain()
                    V.tensor_reduce(count[:, g:g + 1], scr, AX_X, ALU.add)
                    dve.drain()
            V.tensor_tensor(chunk_end[:], chunk_end[:], first_chunk[:], ALU.subtract)
            V.tensor_scalar(first_chunk[:], first_chunk[:], float(NCH - K), None, ALU.min)
            dve.drain()
            for k in range(K):
                V.tensor_scalar(chunk_idx[:, k, :], first_chunk[:], float(k), None, ALU.add)
            V.tensor_scalar(chunk_end[:], chunk_end[:], float(K), None, ALU.is_gt)
            dve.drain()
            dve.sem_inc(sem("chunks_known"), 1)
            V.tensor_reduce(bad3[:, 0:1], chunk_end[:], AX_X, ALU.add)
            spans = scr[:, 0:NCH // WCH]
            firsts = dmin_f.rearrange("p (n c) -> p n c", c=WCH)[:, :, 0]
            lasts = dmax_f.rearrange("p (n c) -> p n c", c=WCH)[:, :, WCH - 1]
            V.tensor_tensor(spans, lasts, firsts, ALU.subtract)
            dve.drain()
            V.tensor_scalar(spans, spans, float(WIN - 1), None, ALU.is_gt)
            dve.drain()
            V.tensor_reduce(bad3[:, 1:2], spans, AX_X, ALU.add)
            dve.wait_ge(sem("dst_in"), 16)
            V.tensor_copy(rel, dst_i)
            dve.drain()
            dve.wait_ge(sem("next_in"), 48)
            V.tensor_copy(scr, next_i)
            dve.drain()
            V.tensor_tensor(scr, rel, scr, ALU.is_gt)
            dve.drain()
            V.tensor_reduce(bad3[:, 2:3], scr, AX_X, ALU.add)
            V.tensor_tensor(rel.rearrange("p (n c) -> p n c", c=WCH), rel.rearrange("p (n c) -> p n c", c=WCH),
                            dmin_f.rearrange("p (n c) -> p n c", c=WCH)[:, :, 0:1].to_broadcast(
                                [P, NCH // WCH, WCH]), ALU.subtract)
            dve.drain()
            V.tensor_reduce(bad[:], bad3[:], AX_X, ALU.add)
            dve.drain()

            def layernorm(s, i, split=None):
                for b in range(SB):
                    V.bn_stats(stats[:, b, :], xs[:, b, :])
                dve.drain()
                for b in range(SB):
                    V.bn_aggr(mv[:, b, :], stats[:, b, :])
                dve.drain()
                V.tensor_scalar(rstd[:], mv[:, :, 1], EPS, None, ALU.add).then_inc(sem(f"ln_var{s}"), 1)
                dve.wait_ge(sem(f"ln_std{s}"), i + 1)
                V.reciprocal(rstd[:], rstd[:])
                dve.drain()
                for b in range(SB):
                    V.tensor_scalar(hT_s[:, b * P:(b + 1) * P], xs[:, b, :], mv[:, b, 0:1], rstd[:, b:b + 1],
                                    ALU.subtract, ALU.mult)
                dve.drain()
                V.tensor_scalar(flat(hs), hT_s[:], 0.0, None, ALU.max).then_inc(sem(f"h_rows{s}"), 1)
                if split is not None:
                    dve.drain()
                    split_rows(split, i)
                dve.drain()
                dve.wait_ge(sem(f"rows_saved{s}"), i + 1)
                if s:
                    dve.wait_ge(sem(f"x_saved{s}"), i + 1)
                dve.sem_inc(sem(f"h_ready{s}"), 1)

            def split_rows(l, i):
                part = [planes[:, n, bass.ds(i * SB, SB), :] for n in range(3)]
                V.tensor_copy(part[0], hs[:])
                dve.drain()
                V.tensor_tensor(blocks(r_s), hs[:], part[0], ALU.subtract)
                dve.drain()
                V.tensor_copy(part[1], blocks(r_s))
                dve.drain()
                V.tensor_tensor(blocks(z_s), blocks(r_s), part[1], ALU.subtract)
                dve.drain()
                V.tensor_copy(part[2], blocks(z_s)).then_inc(sem(f"planes_ready{l}"), 1)

            dve.sem_inc(sem("h_ready0"), 1)
            with dve.Fori(0, NS) as i:
                dve.wait_ge(sem("x_in0"), i * 16 + 16)
                layernorm(0, i)

            dve.wait_ge(sem("chunk_rows"), 16 * 2 * K * NGT)
            V.tensor_scalar(key_ai, src_rows_i, 7, None, ALU.arith_shift_right)
            V.tensor_copy(key_b, dst_rows_i)
            dve.drain()
            V.tensor_copy(key_c, key_ai)
            dve.drain()
            V.tensor_scalar(key_c, key_c, float(G), 1.0, ALU.mult, ALU.add)
            by_group = (lambda v: v.rearrange("p (k g e) -> p k g e", k=K, g=NGT))
            for k in range(K):
                V.tensor_tensor(by_group(key_b)[:, k], by_group(key_b)[:, k],
                                gbase[:].rearrange("p (g o) -> p g o", o=1).to_broadcast([P, NGT, P]), ALU.subtract)
            dve.drain()
            V.tensor_tensor(key_c, key_c, key_b, ALU.add)
            dve.drain()
            V.scalar_tensor_tensor(out=key_c, in0=key_b, scalar=0.0, in1=key_c, op0=ALU.is_ge, op1=ALU.mult)
            dve.drain()
            V.scalar_tensor_tensor(out=key_c, in0=key_b, scalar=float(G - 1), in1=key_c, op0=ALU.is_le, op1=ALU.mult)
            V.tensor_scalar(key_ai, src_rows_i, P - 1, None, ALU.bitwise_and)
            dve.drain()
            V.tensor_scalar(key_b, key_c, -1.0, None, ALU.add)
            dve.drain()
            V.tensor_copy(key_c, key_ai)
            dve.drain()
            dve.sem_inc(sem("keys_made"), 1)
            dve.wait_ge(sem("keys_flipped"), 1)
            V.tensor_copy(keyT, ps[:, 0:NW3].rearrange("p (k g) -> p k g", k=K)).then_inc(sem("keyT_ready"), 1)
            dve.wait_ge(sem("sources_flipped"), 1)
            V.tensor_copy(slT, ps[:, 0:NW3].rearrange("p (k g) -> p k g", k=K)).then_inc(sem("slT_ready"), 1)
            dve.wait_ge(sem("bad_summed"), 1)
            V.tensor_scalar(any_order[:], ps[:, 0:1], 1.0, None, ALU.min)
            dve.drain()
            dve.sem_inc(sem("area_free0"), 1)
            dve.sem_inc(sem("order_known"), 1)
            order = dve.value_load(any_order[0:1, 0:1], min_val=0, max_val=1)

            def sum_any(l):
                _, weighted, counted = GEN[l]

                def f():
                    dve.wait_ge(sem("g_edges"), 48 * (l + 1))
                    V.tensor_copy(g_key, g_src if l == 2 else g_dst)
                    V.tensor_scalar(g_idx, g_dst, N_CLIQUES - 1, None, ALU.min)
                    V.memset(agg[:], 0.0)
                    V.memset(g_iota, 0.0)
                    if counted:
                        V.memset(g_count, 0.0)
                    dve.drain()
                    for n in range(0, TILE, 2 * P):
                        V.tensor_scalar(g_iota[:, n:n + 2 * P], iota16[:, 0:2 * P], float(n), None, ALU.add)
                    dve.drain()
                    dve.sem_inc(sem("g_ready"), 1)
                    dve.sem_inc(sem("g_added"), 2)

                    def add(j, n):
                        t, s = n % NT, n % 2
                        dve.wait_ge(sem("g_mm"), j * (2 * NT) + mm_base(l) + n + 1 + MM_CREDIT)
                        cols, slot = slice(t * TILE, (t + 1) * TILE), slice(s * TILE, (s + 1) * TILE)
                        last = V.tensor_tensor(agg[:, cols], agg[:, cols], pA[:, slot], ALU.add)
                        if counted:
                            last = V.tensor_tensor(g_count[:, cols], g_count[:, cols], pB[:, slot], ALU.add)
                        last.then_inc(sem("g_added"), 1)

                    with dve.Fori(0, NCH // 2) as j:
                        for k in range(2):
                            dve.drain()
                            V.tensor_scalar(tile_key[:], tile_off[:], g_key[:, bass.ds(j * 2 + k, 1)], None, ALU.add)
                            dve.drain()
                            for t in range(NT):
                                n = k * NT + t
                                dve.wait_ge(sem("g_mm"), j * (2 * NT) + mm_base(l) + n - 1 + MM_CREDIT)
                                scale = (g_w[:, bass.ds(j * 2 + k, 1)], ALU.is_equal, ALU.mult) if weighted else (
                                    None, ALU.is_equal)
                                V.tensor_scalar(g_onehot[:, n % 2, :], g_iota, tile_key[:, t:t + 1],
                                                *scale).then_inc(sem("g_onehot"), 1)
                                if n:
                                    add(j, n - 1)
                        add(j, 2 * NT - 1)
                        dve.drain()
                    if counted:
                        V.tensor_scalar(g_count, g_count, 1.0, None, ALU.max)
                        dve.drain()
                        V.reciprocal(g_count, g_count)
                        dve.drain()
                        V.tensor_tensor(agg[:], agg[:], g_count, ALU.mult)
                        dve.drain()
                    if l == 2:
                        V.memset(inv_cnt[:], 1.0)
                        V.memset(out_cnt[:], 0.0)
                        dve.drain()
                    dve.sem_inc(sem(f"agg_done{l}"), 1)
                return f

            def window_onehots(t):
                for w in range(WPS):
                    dve.wait_ge(sem("win_mm"), t * WPS + w + 1)
                    for k in range(WCH):
                        c = w * WCH + k
                        last = V.tensor_scalar(oh_win[:, c, :], iota_win[:], rel[:, bass.ds(t * CPS + c, 1)],
                                               w_edge[:, bass.ds(t * CPS + c, 1)], ALU.is_equal, ALU.mult)
                    last.then_inc(sem("win_onehots"), 1)

            def window_copy(t):
                dve.wait_ge(sem("win_mm"), t * WPS + WIN_RING)
                V.tensor_copy(win_sum[:], p_win).then_inc(sem("win_copied"), 1)

            def window_adds(t, regs):
                dve.load(regs, win_base[0:1, bass.ds(t * WPS, WPS)])
                for w in range(WPS):
                    base = dve.snap(regs[w], min_val=0, max_val=NCOL - WIN)
                    dve.drain()
                    V.tensor_tensor(agg[:, bass.ds(base, WIN)], agg[:, bass.ds(base, WIN)],
                                    win_sum[:, w * WIN:(w + 1) * WIN], ALU.add)

            def group_onehots(t, g):
                dve.wait_ge(sem("cells"), t * GS + g + 1)
                for k in range(K):
                    s = (g % 3) * K + k
                    V.tensor_scalar(oh_src[:, s, :], iota16[:, 0:P], slT[:, k, bass.ds(t * GS + g, 1)], None,
                                    ALU.is_equal)
                    last = V.tensor_scalar(oh_cell[:, s, :], iota16[:], keyT[:, k, bass.ds(t * GS + g, 1)], None,
                                           ALU.is_equal)
                last.then_inc(sem("onehots"), 1)

            def reduce_step(b, sub, which):
                dve.wait_ge(sem("stored"), b * (GS * SUBS) + GS * SUBS + CELL_RING)
                cells = count_blk[:, bass.ds((b % 2) * BLK + sub * (SHS * TD), SHS * TD)]
                V.tensor_reduce(out_part[:], cells.rearrange("p (s d) -> p s d", d=TD), AX_X, ALU.add).then_inc(
                    sem("reduced"), 1)
                dve.drain()
                cnt = out_cnt[:, which, bass.ds(sub * SHS, SHS)]
                V.tensor_tensor(cnt, cnt, out_part[:], ALU.add)
                dve.drain()

            def split_cliques(b):
                dve.wait_ge(sem("mixed"), b * (2 * SUBS) + 1)
                dve.wait_ge(sem("xc_loaded"), b * 16 + 16)
                h = slice(0, HALF)
                rows, r, r2 = (v[h, :].rearrange("p (c d) -> p c d", c=2) for v in (xc_in, xc_r, xc_r2))
                V.tensor_copy(xc_plane[h, :, 0, :], rows)
                dve.drain()
                V.tensor_tensor(r, rows, xc_plane[h, :, 0, :], ALU.subtract)
                dve.drain()
                V.tensor_copy(xc_plane[h, :, 1, :], r)
                dve.drain()
                V.tensor_tensor(r2, r, xc_plane[h, :, 1, :], ALU.subtract)
                dve.drain()
                V.tensor_copy(xc_plane[h, :, 2, :], r2).then_inc(sem("xc_split"), 1)

            def add_mix(b, sub):
                dve.wait_ge(sem("mixed"), b * (2 * SUBS) + sub * 2 + 1)
                cols = clique_sum[:, bass.ds((sub + SUBS - 1) % SUBS * W, W)]
                V.tensor_tensor(cols, cols, p_mix, ALU.add).then_inc(sem("mix_added"), 1)

            def step(blk, sub, regs, counts, clique):
                t = blk * SUBS + sub
                group_onehots(t, 0)
                group_onehots(t, 1)
                window_copy(t)
                if clique:
                    add_mix(blk - 1, sub)
                group_onehots(t, 2)
                if counts is not None:
                    reduce_step(blk - 1, sub, counts)
                group_onehots(t, 3)
                window_onehots(t)
                group_onehots(t, 4)
                window_adds(t, regs)
                group_onehots(t, 5)

            def count_sorted():
                V.memset(agg[:], 0.0)
                V.memset(clique_sum, 0.0)
                V.memset(out_cnt[:], 0.0)
                V.memset(p_win, 0.0)
                V.memset(p_mix, 0.0)
                dve.drain()
                dve.sem_inc(sem("xc_split"), 1)
                dve.sem_inc(sem("reduced"), SUBS)
                dve.wait_ge(sem("edges_in"), 32)
                regs = [dve.alloc_register(f"win_base{w}") for w in range(WPS)]
                with dve.Fori(0, SUBS) as sub:
                    step(0, sub, regs, None, False)
                with dve.Fori(1, L2B + 1) as blk:
                    split_cliques(blk - 1)
                    with dve.Fori(0, SUBS) as sub:
                        step(blk, sub, regs, 0, True)
                add_mix(L2B, 0)
                with dve.Fori(L2B + 1, NBLK) as blk:
                    with dve.Fori(0, SUBS) as sub:
                        step(blk, sub, regs, 1, False)
                with dve.Fori(0, SUBS) as sub:
                    reduce_step(NBLK - 1, sub, 1)
                with dve.Fori(STEPS, STEPS + TAIL) as t:
                    window_onehots(t)
                    dve.drain()
                    window_copy(t)
                    window_adds(t, regs)
                dve.drain()
                window_copy(STEPS + TAIL)
                window_adds(STEPS + TAIL, regs)
                V.tensor_tensor(inv_cnt[:], out_cnt[:, 0, :], out_cnt[:, 1, :], ALU.add)
                dve.drain()
                V.tensor_scalar(inv_cnt[:], inv_cnt[:], 1.0, None, ALU.max)
                dve.drain()
                V.reciprocal(inv_cnt[:], inv_cnt[:])
                dve.wait_ge(sem("block_saved"), NBLK + 1)
                dve.drain()
                dve.sem_inc(sem("agg_done0"), 1)

            def multiply(l):
                def f():
                    before = 0 if l == 1 else 1
                    dve.sem_inc(sem("taken"), 2)
                    with dve.Fori(0, NBLK) as b:
                        slot = (b % 2) * (2 * TILE)
                        dve.wait_ge(sem("piece_used"), b * SUBS + before * (NBLK + 1) * SUBS + 2 * SUBS)
                        sums, cols = ps[:, bass.ds(slot, TD)], agg[:, bass.ds(b * TD, TD)]
                        if l == 1:
                            deg = r_s[:, 0:TD]
                            V.tensor_scalar(deg, ps[:, bass.ds(slot + TILE, TD)], 1.0, None, ALU.max)
                            dve.drain()
                            V.reciprocal(deg, deg)
                            dve.drain()
                            V.tensor_tensor(cols, sums, deg, ALU.mult).then_inc(sem("taken"), 1)
                        else:
                            V.tensor_copy(cols, sums).then_inc(sem("taken"), 1)
                        dve.drain()
                    dve.sem_inc(sem(f"agg_done{l}"), 1)
                return f

            branch(dve, order, sum_any(0), count_sorted)

            dve.sem_inc(sem("h_ready1"), 1)
            with dve.Fori(0, NS) as i:
                dve.wait_ge(sem("hT1"), i + 1)
                dve.wait_ge(sem("agg_staged1"), i + 1)
                V.tensor_tensor(prod_s, pA[:, 0:W], agg_s[:], ALU.mult).then_inc(sem("prod1"), 1)
                dve.wait_ge(sem("lin1"), i + 1)
                V.tensor_copy(z_s, pB[:, 0:W])
                dve.drain()
                V.scalar_tensor_tensor(out=r_s, in0=z_s, scalar=SLOPE, in1=z_s, op0=ALU.mult, op1=ALU.max)
                dve.drain()
                dve.wait_ge(sem("x_in1"), i * 16 + 16)
                V.tensor_tensor(flat(xs), flat(xs), r_s, ALU.add).then_inc(sem("x_new1"), 1)
                dve.drain()
                layernorm(1, i, split=1)
            dve.sem_inc(sem("area_free1"), 1)
            branch(dve, order, sum_any(1), multiply(1))

            dve.sem_inc(sem("h_free2"), 1)
            with dve.Fori(0, NS) as i:
                dve.wait_ge(sem("hT2"), i + 1)
                V.tensor_copy(hT_s[:], pA[:, 0:W]).then_inc(sem("hT_s2"), 1)
                dve.wait_ge(sem("lin2"), i + 1)
                dve.sem_inc(sem("h_free2"), 1)
            dve.wait_ge(sem("mean_sum"), 1)
            V.scalar_tensor_tensor(out=scaled_mean[:], in0=pC[:, 0:D], scalar=1.0 / N_NODES, in1=bcast["mean_scale"][:],
                                   op0=ALU.mult, op1=ALU.mult)
            dve.drain()
            V.tensor_tensor(f_all, f_all, scaled_mean[:].rearrange("p (o d) -> p o d", o=1).to_broadcast([P, NB, D]),
                            ALU.subtract).then_inc(sem("centred"), 1)
            dve.wait_ge(sem("var_sum"), 1)
            V.tensor_scalar(gain[:], pC[:, 0:D], 1.0 / N_NODES, EPS, ALU.mult, ALU.add).then_inc(sem("var_ready"), 1)
            dve.wait_ge(sem("std_ready"), 1)
            V.reciprocal(scaled_mean[:], gain[:])
            dve.drain()
            V.tensor_tensor(gain[:], scaled_mean[:], bcast["gn_weight"][:], ALU.mult)
            dve.drain()
            dve.sem_inc(sem("h_ready2"), 1)

            def over_blocks(t):
                return t[:].rearrange("p (o d) -> p o d", o=1).to_broadcast([P, SB, D])

            z3 = blocks(z_s)
            with dve.Fori(0, NS) as i:
                V.tensor_tensor(z3, f_all[:, bass.ds(i * SB, SB), :], over_blocks(gain), ALU.mult)
                dve.drain()
                V.tensor_tensor(z3, z3, over_blocks(bcast["gn_bias"]), ALU.add)
                dve.drain()
                dve.wait_ge(sem("h_in2"), i * 16 + 16)
                V.tensor_tensor(z3, z3, hs[:], ALU.add)
                dve.drain()
                dve.wait_ge(sem("x_in2"), i * 16 + 16)
                V.tensor_tensor(xs[:], xs[:], z3, ALU.add).then_inc(sem("x_new2"), 1)
                dve.drain()
                layernorm(2, i)
            dve.sem_inc(sem("area_free2"), 1)

            def cliques_sorted():
                V.tensor_copy(agg[:, 0:NPAD], clique_sum)
                dve.drain()
                dve.sem_inc(sem("agg_done2"), 1)

            V.tensor_copy(last_clique[:], last_col[:].to_broadcast([P, P]))
            dve.drain()
            branch(dve, order, sum_any(2), cliques_sorted)
            dve.wait_ge(sem("clique_lin"), 1)
            V.tensor_copy(clique_out[:], pC[:, 0:D])
            dve.drain()
            dve.sem_inc(sem("h_ready3"), 1)
            with dve.Fori(0, NS) as i:
                dve.wait_ge(sem("lin3"), i + 1)
                for b in range(SB):
                    V.scalar_tensor_tensor(out=z3[:, b, :], in0=clique_out[:], scalar=out_cnt[:, 1, bass.ds(i * SB + b, 1)],
                                           in1=blocks(pB[:, 0:W])[:, b, :], op0=ALU.mult, op1=ALU.add)
                dve.drain()
                for b in range(SB):
                    V.scalar_tensor_tensor(out=z3[:, b, :], in0=z3[:, b, :], scalar=inv_cnt[:, bass.ds(i * SB + b, 1)],
                                           in1=bcast["bc"][:], op0=ALU.mult, op1=ALU.add)
                dve.drain()
                dve.wait_ge(sem("x_in3"), i * 16 + 16)
                V.tensor_tensor(xs[:], xs[:], z3, ALU.add).then_inc(sem("x_new3"), 1)
                dve.drain()
                layernorm(3, i)

            dve.sem_inc(sem("msg_free"), 1)
            with dve.Fori(0, NS) as i:
                dve.wait_ge(sem("hT4"), i + 1)
                V.tensor_copy(hT_s[:], pA[:, 0:W]).then_inc(sem("hT_s4"), 1)
                dve.wait_ge(sem("hidden"), i + 1)
                V.tensor_scalar(prod_s, pB[:, 0:W], b_in[:, 0:1], None, ALU.add).then_inc(sem("hidden_s"), 1)
                dve.drain()
                V.tensor_copy(steps_of(hidden_all, i), prod_s)
                dve.wait_ge(sem("msg"), i + 1)
                V.tensor_copy(flat(hs), pC[:, 0:W]).then_inc(sem("msg_rows"), 1)
                dve.drain()
                split_rows(3, i)
                dve.drain()
                dve.wait_ge(sem("msg_saved"), i + 1)
                dve.sem_inc(sem("msg_free"), 1)
            dve.sem_inc(sem("area_free3"), 1)
            branch(dve, order, sum_any(3), multiply(3))

            dve.sem_inc(sem("y_ready"), 1)
            with dve.Fori(0, NS) as i:
                dve.wait_ge(sem("r_ready"), i + 1)
                V.tensor_tensor(n_s, r_s, pD[:, 0:W], ALU.mult)
                dve.drain()
                V.tensor_tensor(n_s, n_s, pC[:, 0:W], ALU.add).then_inc(sem("n_in"), 1)
                dve.wait_ge(sem("tanh"), i + 1)
                dve.wait_ge(sem("hidden_rows"), i + 1)
                V.tensor_tensor(r_s, pA[:, 0:W], n_s, ALU.subtract)
                dve.drain()
                V.tensor_tensor(r_s, r_s, z_s, ALU.mult)
                dve.drain()
                V.tensor_tensor(prod_s, r_s, n_s, ALU.add).then_inc(sem("h_new"), 1)
                dve.wait_ge(sem("h_newT"), i + 1)
                V.tensor_copy(r_s, pB[:, 0:W]).then_inc(sem("h_newT_s"), 1)
                dve.wait_ge(sem("out_rows"), i + 1)
                dve.wait_ge(sem("x_in4"), i * 16 + 16)
                V.tensor_tensor(flat(xs), flat(xs), pC[:, 0:W], ALU.add).then_inc(sem("y_ready"), 1)
                dve.drain()


def kernel(**inputs):
    import numpy as np
    import concourse.bacc as bacc
    from concourse.bass_utils import run_bass_kernel_spmd as run

    def edges(name, fill):
        a = np.ascontiguousarray(inputs[name])
        pad = np.full((NCH * P - N_EDGES,), fill, a.dtype)
        return np.concatenate([a, pad]).reshape(NCH, P)

    def wT(name):
        return np.ascontiguousarray(np.asarray(inputs[name]).T)

    def row(*names):
        return np.ascontiguousarray(np.stack([np.asarray(inputs[n]) for n in names]))

    x = np.ascontiguousarray(inputs["x"])
    xc = np.ascontiguousarray(inputs["L2_gnn_x_clique"])
    src, dst, w = edges("src", N_NODES), edges("dst", N_NODES), edges("edge_weight", 0)
    bhh = row("L3_gnn_b_hh")
    arrays = {
        "x": np.concatenate([x, np.zeros((NPAD - N_NODES, D), x.dtype)]),
        "src_rows": src, "dst_rows": dst,
        "srcT": np.ascontiguousarray(src.T), "dstT": np.ascontiguousarray(dst.T), "wT": np.ascontiguousarray(w.T),
        "win_base_src": np.concatenate([np.zeros((1, WPS), dst.dtype), dst[::WCH, 0:1].T], axis=1),
        "x_clique": np.concatenate([xc, np.repeat(xc[-1:], N_XC - N_CLIQUES, axis=0)]),
        "last_clique": np.ascontiguousarray(xc[-1:].T),
        "W1T": wT("L0_gnn_W1"), "W2T": wT("L0_gnn_W2"), "WlT": wT("L1_gnn_Wl"), "WrT": wT("L1_gnn_Wr"),
        "WcT": wT("L2_gnn_W"), "WinT": wT("L3_gnn_W_in"), "Wmsg": np.ascontiguousarray(inputs["L3_gnn_W_msg"]),
        "WihT": wT("L3_gnn_W_ih"), "WhhT": wT("L3_gnn_W_hh"), "WoutT": wT("L3_gnn_W_out"),
        "b12": row("L0_gnn_b1", "L0_gnn_b2"), "bl": row("L1_gnn_bl"), "bc": row("L2_gnn_b"),
        "bgru": row("L3_gnn_b_ih", "L3_gnn_b_hh"), "bhn": np.ascontiguousarray(bhh[:, 2 * D:]),
        "bout": row("L3_gnn_b_out"), "b_in": np.ascontiguousarray(row("L3_gnn_b_in").T),
        "gn_weight": row("L1_gnn_gn_weight"), "gn_bias": row("L1_gnn_gn_bias"), "mean_scale": row("L1_gnn_mean_scale"),
    }
    nc = bacc.Bacc("TRN2", target_bir_lowering=False, num_devices=1)
    A, fed = {}, {}
    for name, a in arrays.items():
        A[name] = nc.dram_tensor(f"in_{name}", a.shape, mybir.dt.from_np(a.dtype), kind="ExternalInput").ap()
        fed[f"in_{name}"] = a
    out = nc.dram_tensor("out_rows_padded", (NPAD, D), F32, kind="ExternalOutput").ap()
    build_gnn(nc, A, out)
    r = run(nc, [fed], core_ids=[0])
    return r.results[0]["out_rows_padded"][:N_NODES]
```

```python
from contextlib import ExitStack

import concourse.bass as bass
from concourse import mybir

F32 = mybir.dt.float32
F16 = mybir.dt.float16
BF16 = mybir.dt.bfloat16
I32 = mybir.dt.int32
ALU = mybir.AluOpType
ACT = mybir.ActivationFunctionType
AX_X = mybir.AxisListType.X

P = 128
D = 128
N_NODES = 6250
N_CLIQUES = 3125
N_EDGES = 206250
EPS = 1e-5
SLOPE = 0.2
SCALE = 4096.0

NB = -(-N_NODES // P)
NPAD = NB * P
SB = 7
NS = NB // SB
W = SB * P
LAST = N_NODES - (NB - 1) * P
TILE = 512
NT = -(-NPAD // TILE)
NCOL = NT * TILE

G = 6
K = 2
GS = 6
SUBS = 7
TD = G * GS * SUBS
HALF = TD // 2
NBLK = -(-N_NODES // TD)
BLK = NB * TD
CELLS = NB * G
NGT = -(-NBLK * GS * SUBS // P)
KD = 4
SHS = NB // SUBS
L2B = -(-N_CLIQUES // TD)
N_XC = L2B * TD

WIN = 32
WCH = 3
WPS = 3
CPS = WCH * WPS
STEPS = NBLK * SUBS
TAIL = 5
NCH = (STEPS + TAIL) * CPS
assert NCH * P >= N_EDGES and NCH % 2 == 0


def build_gnn(nc, A, out):
    with ExitStack() as ctx:
        def sb(name, shape, dt=F32):
            return ctx.enter_context(nc.sbuf_tensor(name, shape, dt))

        sems = {}

        def sem(name):
            if name not in sems:
                sems[name] = ctx.enter_context(nc.semaphore(name))
            return sems[name]

        x_dram = nc.dram_tensor("x_stream", (NPAD, D), F32).ap()
        rows_dram = nc.dram_tensor("node_rows", (NPAD, D), F32).ap()
        deg_dram = nc.dram_tensor("in_degrees", (1, NGT * P * G), F32).ap()
        cells_dram = nc.dram_tensor("edge_counts", (NBLK, P, BLK), F16).ap()

        class Region:

            def __init__(self, name, words):
                self.t, self.words = sb(name, [P, words]), words

            def view(self, start, words, dt=F32):
                assert start + words <= self.words
                v = self.t[:, start:start + words]
                return v if dt == F32 else v.bitcast(dt)

        agg = sb("agg", [P, NCOL])
        carry = Region("carry", NPAD)
        big = Region("big", BLK)
        edge_area = Region("edge_area", 13600)

        at = 0

        def take(words, dt=F32):
            nonlocal at
            v = edge_area.view(at, words, dt)
            at += words
            return v

        keyT = take(K * NGT * P // 2, F16).rearrange("p (k g) -> p k g", k=K)
        slT = take(K * NGT * P // 2, F16).rearrange("p (k g) -> p k g", k=K)
        src_i = take(NCH, I32)
        rel = take(NCH)
        w_edge = take(NCH)
        oh_src = take(3 * K * P // 2, BF16).rearrange("p (s n) -> p s n", s=3 * K)
        oh_cell = take(3 * K * CELLS // 2, BF16).rearrange("p (s n) -> p s n", s=3 * K)
        gathered = take(CPS * D).rearrange("p (s n) -> p s n", s=CPS)
        oh_win = take(CPS * WIN).rearrange("p (s n) -> p s n", s=CPS)
        flipped_s = take(W // 2, F16)
        xc_plane = take(2 * 3 * D // 2, BF16).rearrange("p (c l n) -> p c l n", c=2, l=3)
        xc_in = take(2 * D)
        xc_r = take(2 * D)
        xc_r2 = take(2 * D)
        idx_slot = take(CPS, I32)
        planes = edge_area.view(0, NPAD, F16).rearrange("p (l b n) -> p l b n", l=2, b=NB)
        deg_s = edge_area.view(NPAD, 2 * TD)
        inv_deg = edge_area.view(NPAD + 2 * TD, TD)
        unused = edge_area.view(NPAD + 3 * TD, SHS * TD // 2, F16)
        deg_row = edge_area.view(0, NPAD)
        xs2 = edge_area.view(NPAD, 2 * W)
        am_s, ah_s, t_s, newT_s = (edge_area.view(NPAD + (2 + n) * W, W) for n in range(4))
        hid2 = big.view(0, 2 * W)

        count_blk = big.view(0, BLK, F16)
        piece = big.view(0, BLK // 2, F16).rearrange("p (k n) -> p k n", k=SUBS)
        dmax_i, dmin_i = big.view(0, NCH, I32), big.view(NCH, NCH, I32)
        dmax_f, dmin_f = big.view(2 * NCH, NCH), big.view(3 * NCH, NCH)
        scr = big.view(4 * NCH, NCH)
        dst_i, next_i = big.view(5 * NCH, NCH, I32), big.view(6 * NCH, NCH, I32)
        GE = K * P
        NKEY = NGT * GE
        group_dst_i = carry.view(0, NGT * (GE + 1), I32).rearrange("p (g e) -> p g e", g=NGT)
        chunk_dst_i = carry.view(NGT * (GE + 1), NGT * P, I32).rearrange("p (g e) -> p g e", g=NGT)
        chunk_dst = carry.view(NGT * (GE + 1 + P), NGT * P).rearrange("p (g e) -> p g e", g=NGT)
        group_src_i = agg[:, 0:NKEY].bitcast(I32)
        key_b, key_c = big.view(NKEY, NKEY), big.view(2 * NKEY, NKEY)
        key_ai = big.view(0, NKEY, I32)
        deg_tmp = big.view(3 * NKEY, 5 * GE).rearrange("p (s e) -> p s e", s=5)
        f_all = big.view(0, NPAD).rearrange("p (b d) -> p b d", d=D)
        prod_s, r_s, z_s, n_s = (big.view(BLK - (n + 1) * W, W) for n in range(4))
        sq_all = agg[:, 0:NPAD].rearrange("p (b d) -> p b d", d=D)
        hidden_all = carry.view(0, NPAD)
        clique_sum = carry.view(0, NPAD)
        g_src, g_dst, g_idx = (edge_area.view(n * NCH, NCH, I32) for n in range(3))
        g_key, g_w = edge_area.view(3 * NCH, NCH), edge_area.view(4 * NCH, NCH)
        g_count = big.view(0, NCOL)
        g_onehot = big.view(NCOL, 2 * TILE).rearrange("p (s n) -> p s n", s=2)
        g_rows = big.view(NCOL + 2 * TILE, 2 * D).rearrange("p (s n) -> p s n", s=2)
        g_iota_i = big.view(NCOL + 2 * TILE + 2 * D, TILE, I32)
        g_iota = big.view(NCOL + 3 * TILE + 2 * D, TILE)

        xs = sb("xs", [P, SB, D])
        hs = sb("hs", [P, SB, D])
        agg_s = sb("agg_s", [P, W])
        hT_s = sb("hT_s", [P, W])
        stats = sb("stats", [P, SB, 6])
        mv = sb("mv", [P, SB, 2])
        rstd = sb("rstd", [P, SB])
        scaled_mean = sb("scaled_mean", [P, D])
        gain = sb("gain", [P, D])
        ones = sb("ones", [P, P])
        ident = sb("ident", [P, P])
        ones16 = sb("ones16", [P, P], BF16)
        ident16 = sb("ident16", [P, P], F16)
        iota_i = sb("iota_i", [P, CELLS], I32)
        iota16 = sb("iota16", [P, CELLS], F16)
        iota_win = sb("iota_win", [P, WIN])
        chunk_slot = sb("chunk_slot", [P, 2], I32)
        tile_off_i = sb("tile_off_i", [P, NT], I32)
        tile_off = sb("tile_off", [P, NT])
        tile_key = sb("tile_key", [P, NT])
        gbase_i = sb("gbase_i", [P, NGT], I32)
        gbase = sb("gbase", [P, NGT])
        glast = sb("glast", [P, NGT])
        first_chunk = sb("first_chunk", [P, NGT])
        in_chunk = sb("in_chunk", [P, NGT])
        past_group = sb("past_group", [P, NGT])
        edge_idx = sb("edge_idx", [P, NGT], I32)
        deg_g = sb("deg_g", [P, NGT, G])
        chunk_idx = sb("chunk_idx", [P, NGT], I32)
        win_base = sb("win_base", [1, WPS + NCH // WCH], I32)
        win_sum = sb("win_sum", [P, WPS * WIN])
        bad3 = sb("bad3", [P, 3])
        bad = sb("bad", [P, 1])
        any_order = sb("any_order", [P, 1], I32)
        out_part = sb("out_part", [P, NB])
        out_cnt = sb("out_cnt", [P, 2, NB])
        inv_cnt = sb("inv_cnt", [P, NB])
        last_col = sb("last_col", [P, 1])
        last_clique = sb("last_clique", [P, P])
        clique_out = sb("clique_out", [P, D])
        wt = {n: sb("w_" + n, [P, A[n].shape[1]]) for n in
              ("W1T", "W2T", "WlT", "WrT", "WcT", "WinT", "Wmsg", "WihT", "WhhT", "WoutT")}
        bias = {n: sb("b_" + n, [A[n].shape[0], A[n].shape[1]]) for n in ("b12", "bl", "b_in_row")}
        b_gates = {n: sb("b_" + n, [P, 3]) for n in ("b_ih", "b_hh")}
        b_rz = sb("b_rz", [P, 2])
        b_in = sb("b_in", [P, 1])
        bcast = {n: sb("bc_" + n, [P, D]) for n in ("gn_weight", "gn_bias", "mean_scale", "bc", "bout")}
        N_CONST_LOADS = len(wt) + len(bias) + len(b_gates) + 2 + len(bcast)

        ps = ctx.enter_context(nc.psum_tensor("ps", [P, 8 * TILE], F32))
        pA, pB, pC, pD = (ps[:, n * 2 * TILE:(n + 1) * 2 * TILE] for n in range(4))
        p_cells = ps[:, 0:3 * TILE].rearrange("p (s n) -> p s n", s=3)
        p_flip = ps[:, 3 * TILE:3 * TILE + W]
        p_mix = ps[:, 5 * TILE:5 * TILE + W]
        p_win = ps[:, 7 * TILE:7 * TILE + WPS * WIN]

        def rows_of(t, i):
            return t[bass.ds(i * W, W), :].rearrange("(b p) d -> p b d", p=P)

        def steps_of(v, i):
            return v[:, bass.ds(i * W, W)]

        def flat(t):
            return t[:].rearrange("p b d -> p (b d)")

        def blocks(v):
            return v.rearrange("p (b d) -> p b d", d=D)

        GEN = {0: (rows_dram, True, False), 1: (rows_dram, False, True),
               2: (A["x_clique"], False, True), 3: (rows_dram, False, False)}
        MM_CREDIT = 2 * NT

        def mm_base(l):
            return l * (NCH * NT + MM_CREDIT)

        CELL_RING = 3
        WIN_RING = WPS

        block = ctx.enter_context(nc.Block())

        def branch(eng, order, general, sorted_):
            with eng.If(order > 0):
                general()
            with eng.Else():
                sorted_()

        @block.sync
        def _(sp):
            sp.dma_start(dmax_i, A["dstT"][P - 1:P, :].to_broadcast([P, NCH])).then_inc(sem("ends_in"), 16)
            sp.dma_start(dmin_i, A["dstT"][0:1, :].to_broadcast([P, NCH])).then_inc(sem("ends_in"), 16)
            sp.dma_start(win_base[:], A["win_base_src"]).then_inc(sem("ends_in"), 16)
            sp.dma_start(dst_i, A["dstT"]).then_inc(sem("dst_in"), 16)
            sp.dma_start(next_i[0:P - 1, :], A["dstT"][1:P, :]).then_inc(sem("next_in"), 16)
            sp.dma_start(next_i[P - 1:P, 0:NCH - 1], A["dstT"][0:1, 1:NCH]).then_inc(sem("next_in"), 16)
            sp.dma_start(next_i[P - 1:P, NCH - 1:NCH], A["dstT"][P - 1:P, NCH - 1:NCH]).then_inc(sem("next_in"), 16)

            def stage(s, source, new_x, with_h):
                with sp.Fori(0, NS) as i:
                    sp.wait_ge(sem(f"h_ready{s}"), i + 1)
                    sp.dma_start(xs[:], rows_of(source, i)).then_inc(sem("x_in"), 16)
                    if with_h:
                        sp.dma_start(hs[:], rows_of(rows_dram, i)).then_inc(sem(f"h_in{s}"), 16)
                    if new_x:
                        sp.wait_ge(sem("x_new"), i + 1 + (s - 1) * NS)
                        sp.dma_start(rows_of(x_dram, i), xs[:]).then_inc(sem("x_out"), 16)
                    sp.wait_ge(sem("h_rows"), i + 1 + s * NS)
                    sp.dma_start(rows_of(rows_dram, i), hs[:]).then_inc(sem("rows_out"), 16)
                    if new_x:
                        sp.wait_ge(sem("x_out"), i * 16 + 16 + (s - 1) * NS * 16)
                        sp.sem_inc(sem("x_saved"), 1)
                    sp.wait_ge(sem("rows_out"), i * 16 + 16 + s * NS * 16)
                    sp.sem_inc(sem("rows_saved"), 1)
                sp.sem_inc(sem(f"rows_written{s}"), 1)

            stage(0, A["x"], False, False)
            sp.dma_start(src_i, A["srcT"]).then_inc(sem("edges_in"), 16)
            sp.dma_start(w_edge, A["wT"]).then_inc(sem("edges_in"), 16)
            for n, t in (*wt.items(), *bias.items(), *b_gates.items()):
                sp.dma_start(t[:], A[n]).then_inc(sem("consts_in"), 16)
            sp.dma_start(b_in[:], A["b_in"]).then_inc(sem("consts_in"), 16)
            sp.dma_start(last_col[:], A["last_clique"]).then_inc(sem("consts_in"), 16)
            for n, t in bcast.items():
                sp.dma_start(t[:], A[n].to_broadcast([P, D])).then_inc(sem("consts_in"), 16)

            sp.wait_ge(sem("deg_counted"), 1)
            sp.dma_start(deg_dram.rearrange("o (g p j) -> p (o g) j", g=NGT, p=P), deg_g[:]).then_inc(sem("deg_out"), 16)
            sp.wait_ge(sem("deg_out"), 16)
            sp.wait_ge(sem("order_known"), 1)
            order = sp.value_load(any_order[0:1, 0:1], min_val=0, max_val=1)

            def edges_any(l):
                def f():
                    sp.wait_ge(sem(f"area_free{l}"), 1)
                    sp.wait_ge(sem("edges_in"), 32)
                    for t, n in ((g_src, "srcT"), (g_dst, "dstT"), (g_w, "wT")):
                        sp.dma_start(t, A[n]).then_inc(sem("g_edges"), 16)
                    if l == 1:
                        sp.wait_ge(sem("g_counted"), 1)
                        sp.dma_start(deg_dram[:, 0:NCOL], g_count[0:1, :]).then_inc(sem("deg_out"), 16)
                return f

            def load_cliques(b):
                sp.wait_ge(sem("xc_split"), b + 1)
                sp.dma_start(xc_in[0:HALF, :].rearrange("p (c d) -> p c d", c=2),
                             A["x_clique"][bass.ds(b * TD, TD), :].rearrange("(c p) d -> p c d", p=HALF)
                             ).then_inc(sem("xc_loaded"), 16)

            def store_piece(b, k, steps):
                sp.wait_ge(sem("stored"), b * (GS * SUBS) + (SUBS + steps) * GS + CELL_RING)
                cols = k * (SHS * TD)
                sp.dma_start(cells_dram[bass.ds(b, 1), :, cols:cols + SHS * TD].rearrange("o p n -> p (o n)"),
                             count_blk[:, bass.ds((b % 2) * BLK + cols, SHS * TD)]).then_inc(sem("cells_out"), 16)

            def store_block(b, paced):
                for k in range(SUBS):
                    store_piece(b, k, k if paced else 0)
                sp.wait_ge(sem("cells_out"), b * (16 * SUBS) + 16 * SUBS)
                sp.sem_inc(sem("block_saved"), 1)

            def count_sorted():
                sp.sem_inc(sem("block_saved"), 1)
                with sp.Fori(0, L2B) as b:
                    load_cliques(b)
                    store_block(b, True)
                with sp.Fori(L2B, NBLK - 1) as b:
                    store_block(b, True)
                store_block(NBLK - 1, False)

            def load_pieces(l):
                before = 0 if l == 1 else 1

                def f():
                    if l == 1:
                        sp.wait_ge(sem("agg_done0"), 1)
                    else:
                        sp.wait_ge(sem("area_free3"), 1)
                    with sp.Fori(0, NBLK) as b:
                        if l == 1:
                            sp.wait_ge(sem("taken"), b + 1)
                            sp.dma_start(deg_s[:, bass.ds((b % 2) * TD, TD)],
                                         deg_dram[:, bass.ds(b * TD, TD)].to_broadcast([P, TD])).then_inc(sem("deg_in"), 16)
                        for k in range(SUBS):
                            sp.wait_ge(sem("piece_used"), b * SUBS + before * (NBLK + 1) * SUBS + k + 1)
                            if l == 1:
                                sp.sem_inc(sem("piece_multiplied"), 1)
                            if l == 1 and k < KD:
                                sp.wait_ge(sem("piece_counted"), b * KD + k + 1)
                            elif l == 1:
                                sp.wait_ge(sem("piece_counted_act"), b * (SUBS - KD) + k - KD + 1)
                            sp.dma_start(piece[:, k, :],
                                         cells_dram[bass.ds(b, 1), :, k * SHS * TD:(k + 1) * SHS * TD].rearrange(
                                             "o p n -> p (o n)")).then_inc(sem(f"piece{k}"), 16)
                return f

            branch(sp, order, edges_any(0), count_sorted)

            stage(1, A["x"], True, True)
            branch(sp, order, edges_any(1), load_pieces(1))
            with sp.Fori(0, NS) as i:
                sp.wait_ge(sem("h_free2"), i + 1)
                sp.dma_start(hs[:], rows_of(rows_dram, i)).then_inc(sem("h_in2a"), 16)
            stage(2, x_dram, True, True)
            branch(sp, order, edges_any(2), lambda: sp.sem_inc(sem("idle"), 1))
            stage(3, x_dram, True, False)
            branch(sp, order, edges_any(3), load_pieces(3))
            sp.wait_ge(sem("agg_done3"), 1)
            sp.dma_start(deg_row[0:1, :], deg_dram[:, 0:NPAD]).then_inc(sem("deg_row_in"), 16)
            sp.dma_start(hs[:], rows_of(rows_dram, 0)).then_inc(sem("h_in4"), 16)
            sp.dma_start(xs2[:, 0:W].rearrange("p (b d) -> p b d", d=D), rows_of(x_dram, 0)).then_inc(sem("x_in4"), 16)

            def store_y(i):
                sp.wait_ge(sem("y_ready"), i + 2)
                sp.dma_start(rows_of(out, i), xs2[:, bass.ds((i % 2) * W, W)].rearrange("p (b d) -> p b d", d=D)
                             ).then_inc(sem("y_out"), 16)

            sp.sem_inc(sem("y_out"), 16)
            with sp.Fori(0, NS - 1) as i:
                sp.wait_ge(sem("hT4"), i + 1)
                sp.dma_start(hs[:], rows_of(rows_dram, i + 1)).then_inc(sem("h_in4"), 16)
                sp.wait_ge(sem("y_out"), i * 16 + 16)
                sp.sem_inc(sem("piece_multiplied"), 1)
                sp.wait_ge(sem("x_biased"), i + 1)
                sp.dma_start(xs2[:, bass.ds(((i + 1) % 2) * W, W)].rearrange("p (b d) -> p b d", d=D),
                             rows_of(x_dram, i + 1)).then_inc(sem("x_in4"), 16)
                store_y(i)
            store_y(NS - 1)
            sp.wait_ge(sem("y_out"), 16 * NS + 16)

        @block.gpsimd
        def _(pool):
            nc.gpsimd.iota(iota_i[:], pattern=[[1, CELLS]], base=0, channel_multiplier=0).then_inc(sem("made"), 1)
            nc.gpsimd.iota(tile_off_i[:], pattern=[[-TILE, NT]], base=0, channel_multiplier=0).then_inc(sem("made"), 1)
            nc.gpsimd.iota(gbase_i[:], pattern=[[G * P, NGT]], base=0, channel_multiplier=G).then_inc(sem("made"), 1)
            nc.gpsimd.memset(ident[:], 0.0)
            nc.gpsimd.memset(ones16[:], 1.0)
            nc.gpsimd.memset(ones[:], 1.0).then_inc(sem("made"), 1)
            pool.drain()
            nc.gpsimd.affine_select(out=ident[:], in_=ident[:], compare_op=ALU.not_equal, fill=1.0, base=0,
                                    pattern=[[-1, P]], channel_multiplier=1).then_inc(sem("made"), 1)
            for g in range(NGT):
                pool.wait_ge(sem("chunk_known"), g + 1)
                pool.indirect_dma_start(
                    out=chunk_dst_i[:, g, :], out_offset=None, in_=A["dst_rows"],
                    in_offset=bass.IndirectOffsetOnAxis(ap=chunk_idx[:, g:g + 1], axis=0),
                ).then_inc(sem("chunk_rows"), 16)
            pool.wait_ge(sem("edge_known"), 1)
            for rows, table, n, got in ((group_dst_i, "dst_flat", GE + 1, "group_dst"), (None, "src_flat", GE, "group_src")):
                for g in range(NGT):
                    pool.indirect_dma_start(
                        out=rows[:, g, :] if rows is not None else group_src_i[:, g * GE:(g + 1) * GE],
                        out_offset=None, in_=A[table],
                        in_offset=bass.IndirectOffsetOnAxis(ap=edge_idx[:, g:g + 1], axis=1),
                    ).then_inc(sem(got), 16)
            pool.wait_ge(sem("order_known"), 1)
            order = pool.value_load(any_order[0:1, 0:1], min_val=0, max_val=1)

            def gather_windows(t):
                for w in range(WPS):
                    pool.wait_ge(sem("indices_ready"), t * WPS + w + 1)
                    pool.sem_inc(sem("win_slot_taken"), 1)
                    for k in range(w * WCH, (w + 1) * WCH):
                        pool.indirect_dma_start(
                            out=gathered[:, k, :], out_offset=None, in_=rows_dram,
                            in_offset=bass.IndirectOffsetOnAxis(ap=idx_slot[:, k:k + 1], axis=0),
                        ).then_inc(sem(f"win_row{k}"), 16)

            def windows_sorted():
                pool.wait_ge(sem("edges_in"), 32)
                pool.wait_ge(sem("rows_written0"), 1)
                with pool.Fori(0, STEPS + TAIL) as t:
                    gather_windows(t)

            def gather_any(l):
                def f():
                    table = GEN[l][0]
                    index = g_idx if l == 2 else g_src
                    if l != 2:
                        pool.wait_ge(sem("rows_saved"), (l + 1) * NS)
                    pool.wait_ge(sem("g_ready"), l + 1)
                    with pool.Fori(0, NCH // 2) as j:
                        pool.wait_ge(sem("g_mm"), j * (2 * NT) + mm_base(l) + 2 * NT)
                        pool.sem_inc(sem("g_slots_taken"), 1)
                        nc.gpsimd.tensor_copy(chunk_slot[:], index[:, bass.ds(j * 2, 2)])
                        pool.drain()
                        for k in range(2):
                            pool.indirect_dma_start(
                                out=g_rows[:, k, :], out_offset=None, in_=table,
                                in_offset=bass.IndirectOffsetOnAxis(ap=chunk_slot[:, k:k + 1], axis=0),
                            ).then_inc(sem(f"g_row{k}"), 16)
                return f

            def idle():
                pool.sem_inc(sem("idle"), 1)

            branch(pool, order, gather_any(0), windows_sorted)
            branch(pool, order, gather_any(1), idle)
            branch(pool, order, gather_any(2), idle)
            branch(pool, order, gather_any(3), idle)
            with pool.Fori(0, NS) as i:
                pool.wait_ge(sem("x_in4"), i * 16 + 16)
                rows = blocks(xs2[:, bass.ds((i % 2) * W, W)])
                nc.gpsimd.tensor_tensor(rows, rows, bcast["bout"][:].rearrange("p (o d) -> p o d", o=1).to_broadcast(
                    [P, SB, D]), ALU.add).then_inc(sem("x_biased"), 1)

        @block.tensor
        def _(pe):
            mm = nc.tensor.matmul
            pe.wait_ge(sem("made"), 5)
            pe.wait_ge(sem("keys_made"), 1)
            for n in range(K * NGT):
                last = nc.tensor.transpose(ps[:, n * P:(n + 1) * P], key_b[:, n * P:(n + 1) * P], ident[:])
            last.then_inc(sem("keys_flipped"), 1)
            pe.wait_ge(sem("keyT_ready"), 1)
            for n in range(K * NGT):
                last = nc.tensor.transpose(ps[:, n * P:(n + 1) * P], key_c[:, n * P:(n + 1) * P], ident[:])
            last.then_inc(sem("sources_flipped"), 1)
            pe.wait_ge(sem("slT_ready"), 1)
            mm(ps[:, 0:1], ones[:], bad[:], start=True, stop=True).then_inc(sem("bad_summed"), 1)
            pe.wait_ge(sem("consts_in"), 16 * N_CONST_LOADS)
            pe.wait_ge(sem("order_known"), 1)
            order = pe.value_load(any_order[0:1, 0:1], min_val=0, max_val=1)

            def sum_any(l):
                counted = GEN[l][2]

                def f():
                    pe.sem_inc(sem("g_mm"), MM_CREDIT)
                    with pe.Fori(0, NCH // 2) as j:
                        for k in range(2):
                            pe.wait_ge(sem(f"g_row{k}"), j * 16 + (l * (NCH // 2) + 1) * 16)
                            for t in range(NT):
                                n = k * NT + t
                                cols = slice((n % 2) * TILE, (n % 2 + 1) * TILE)
                                pe.wait_ge(sem("g_onehot"), j * (2 * NT) + l * NCH * NT + n + 1)
                                pe.wait_ge(sem("g_added"), j * (2 * NT) + l * (NCH * NT + 2) + n + 1)
                                last = mm(pA[:, cols], g_rows[:, k, :], g_onehot[:, n % 2, :], start=True, stop=True)
                                if counted:
                                    last = mm(pB[:, cols], ones[:], g_onehot[:, n % 2, :], start=True, stop=True)
                                last.then_inc(sem("g_mm"), 1)
                return f

            def count_group(t, g):
                pe.wait_ge(sem("onehots"), t * GS + g + 1)
                pe.wait_ge(sem("stored"), t * GS + g + 1)
                for k in range(K):
                    s = (g % 3) * K + k
                    last = mm(p_cells[:, g % 3, 0:CELLS], oh_src[:, s, :], oh_cell[:, s, :],
                              start=(k == 0), stop=(k == K - 1))
                last.then_inc(sem("cells"), 1)

            def flip(b, sub, c):
                pe.wait_ge(sem("flip_copied"), b * (2 * SUBS) + sub * 2 + c + 1)
                if c == 0:
                    pe.wait_ge(sem("stored"), b * (GS * SUBS) + GS * SUBS + CELL_RING)
                for j in range(SHS):
                    last = mm(p_flip[0:HALF, j * P:(j + 1) * P],
                              count_blk[:, bass.ds((b % 2) * BLK + (sub * SHS + j) * TD + c * HALF, HALF)],
                              ident16[:], start=True, stop=True)
                last.then_inc(sem("flips"), 1)

            def mix(b, sub, c):
                pe.wait_ge(sem("flip_copied"), b * (2 * SUBS) + sub * 2 + c + 2)
                if c == 0:
                    pe.wait_ge(sem("xc_split"), b + 2)
                    pe.wait_ge(sem("mix_added"), b * SUBS + sub + 1)
                for lo, n in ((0, TILE), (TILE, W - TILE)):
                    for l in range(3):
                        last = mm(p_mix[:, lo:lo + n], xc_plane[0:HALF, c, l, :], flipped_s[0:HALF, lo:lo + n],
                                  start=(c == 0 and l == 0), stop=(c == 1 and l == 2))
                last.then_inc(sem("mixed"), 1)

            def window(t, w):
                if w == 0:
                    pe.wait_ge(sem("win_copied"), t + 1)
                pe.wait_ge(sem("win_onehots"), t * WPS + w + 1)
                for k in range(WCH):
                    s = w * WCH + k
                    pe.wait_ge(sem(f"win_row{s}"), t * 16 + 16)
                    last = mm(p_win[:, w * WIN:(w + 1) * WIN], gathered[:, s, :], oh_win[:, s, :], start=(k == 0), stop=(k == WCH - 1))
                last.then_inc(sem("win_mm"), 1)

            def step(blk, sub, clique):
                t = blk * SUBS + sub
                b = blk - 1
                count_group(t, 0)
                if clique:
                    flip(b, sub, 0)
                count_group(t, 1)
                window(t, 0)
                count_group(t, 2)
                if clique:
                    mix(b, sub, 0)
                    flip(b, sub, 1)
                count_group(t, 3)
                window(t, 1)
                count_group(t, 4)
                if clique:
                    mix(b, sub, 1)
                count_group(t, 5)
                window(t, 2)

            def count_sorted():
                pe.sem_inc(sem("cells"), CELL_RING)
                pe.sem_inc(sem("win_mm"), WIN_RING)
                pe.sem_inc(sem("flips"), 2 * SUBS)
                pe.sem_inc(sem("mixed"), 1)
                with pe.Fori(0, SUBS) as sub:
                    step(0, sub, False)
                with pe.Fori(1, L2B + 1) as blk:
                    with pe.Fori(0, SUBS) as sub:
                        step(blk, sub, True)
                with pe.Fori(L2B + 1, NBLK) as blk:
                    with pe.Fori(0, SUBS) as sub:
                        step(blk, sub, False)
                with pe.Fori(STEPS, STEPS + TAIL) as t:
                    for w in range(WPS):
                        window(t, w)

            def multiply(l):
                def f():
                    before = 0 if l == 1 else 1
                    pe.sem_inc(sem("piece_used"), SUBS)
                    pe.wait_ge(sem(f"planes_ready{l}"), NS)
                    with pe.Fori(0, NBLK) as b:
                        slot = (b % 2) * (2 * TILE)
                        pe.wait_ge(sem("taken"), b + before * (NBLK + 2) + 1)
                        for k in range(SUBS):
                            pe.wait_ge(sem(f"piece{k}"), b * 16 + before * NBLK * 16 + 16)
                            for j in range(SHS):
                                sh = k * SHS + j
                                cells = piece[:, k, j * TD:(j + 1) * TD]
                                for p in range(2):
                                    last = mm(ps[:, bass.ds(slot, TD)], planes[:, p, sh, :], cells,
                                              start=(sh == 0 and p == 0), stop=(sh == NB - 1 and p == 1))
                            last.then_inc(sem("piece_used"), 1)
                return f

            def transposes(dst_ps, source):
                for b in range(SB):
                    last = nc.tensor.transpose(dst_ps[:, b * P:(b + 1) * P], source[:, b * P:(b + 1) * P], ident[:])
                return last

            def product(dst_ps, terms):
                for b in range(SB):
                    for n, (lhs, rhs) in enumerate(terms):
                        k = rhs.shape[0]
                        lhsT = lhs[:, b * P:(b + 1) * P] if k == P else lhs[0:k, :]
                        last = mm(dst_ps[:, b * D:(b + 1) * D], lhsT, rhs, start=(n == 0), stop=(n == len(terms) - 1))
                return last

            def column_sums(source):
                mm(pC[:, 0:D], ones[0:LAST, :], source[0:LAST, NB - 1, :], start=True, stop=False)
                with pe.Fori(0, NB - 2) as b:
                    mm(pC[:, 0:D], ones[:], source[:, bass.ds(b, 1), :].rearrange("p b d -> p (b d)"),
                       start=False, stop=False)
                return mm(pC[:, 0:D], ones[:], source[:, NB - 2, :], start=False, stop=True)

            branch(pe, order, sum_any(0), count_sorted)
            with pe.Fori(0, NS) as i:
                pe.wait_ge(sem("h_in1"), i * 16 + 16)
                pe.wait_ge(sem("agg_done0"), 1)
                transposes(pA, flat(hs)).then_inc(sem("hT1"), 1)
                pe.wait_ge(sem("prod1"), i + 1)
                pe.wait_ge(sem("agg_staged1"), i + 1)
                product(pB, [(agg_s, wt["W1T"][:]), (prod_s, wt["W2T"][:]), (ones, bias["b12"][:])]).then_inc(
                    sem("lin1"), 1)
            pe.wait_ge(sem("h_ready1"), NS + 1)
            branch(pe, order, sum_any(1), multiply(1))
            with pe.Fori(0, NS) as i:
                pe.wait_ge(sem("h_in2a"), i * 16 + 16)
                pe.wait_ge(sem("agg_done1"), 1)
                transposes(pA, flat(hs)).then_inc(sem("hT2"), 1)
                pe.wait_ge(sem("hT_s2"), i + 1)
                pe.wait_ge(sem("agg_staged2"), i + 1)
                product(pB, [(agg_s, wt["WlT"][:]), (hT_s, wt["WrT"][:]), (ones, bias["bl"][:])]).then_inc(
                    sem("lin2"), 1)
            pe.wait_ge(sem("gelu"), NS)
            column_sums(f_all).then_inc(sem("mean_sum"), 1)
            pe.wait_ge(sem("squared"), 1)
            column_sums(sq_all).then_inc(sem("var_sum"), 1)
            pe.wait_ge(sem("h_ready2"), NS + 1)
            branch(pe, order, sum_any(2), lambda: pe.sem_inc(sem("idle"), 1))
            pe.wait_ge(sem("agg_done2"), 1)
            mm(pC[:, 0:D], last_clique[:], wt["WcT"][:], start=True, stop=True).then_inc(sem("clique_lin"), 1)
            with pe.Fori(0, NS) as i:
                pe.wait_ge(sem("agg_staged3"), i + 1)
                product(pB, [(agg_s, wt["WcT"][:])]).then_inc(sem("lin3"), 1)
            branch(pe, order, sum_any(3), multiply(3))

            def wide(dst_ps, terms):
                for lo, hi in ((0, TILE), (TILE, W)):
                    for n, (lhs, rhs) in enumerate(terms):
                        last = mm(dst_ps[:, lo:hi], lhs, rhs(lo, hi - lo), start=(n == 0), stop=(n == len(terms) - 1))
                return last

            def step_view(v, i, rows=slice(0, P)):
                return lambda lo, n: v[rows, bass.ds(i * W + lo, n)]

            def fixed_view(v):
                return lambda lo, n: v[:, lo:lo + n]

            def messages(i):
                pe.wait_ge(sem("h_in4"), i * 16 + 16)
                pe.wait_ge(sem("r_ready"), i + 1)
                transposes(pA, flat(hs)).then_inc(sem("hT4"), 1)
                pe.wait_ge(sem("n_in"), i + 1)
                wide(pC, [(wt["WinT"][:], step_view(agg, i)),
                          (bias["b_in_row"][:], step_view(deg_row, i, slice(0, 1)))]).then_inc(sem("hid_sum"), 1)
                pe.wait_ge(sem("hT_s4"), i + 1)
                pe.wait_ge(sem("z_ready"), i + 1)
                wide(pB, [(wt["WinT"][:], fixed_view(hT_s))]).then_inc(sem("hidden"), 1)
                pe.wait_ge(sem("hid_sum_s"), i + 1)
                wide(pD, [(wt["Wmsg"][:], fixed_view(ah_s))]).then_inc(sem("msg_sum"), 1)

            def gates(i):
                ih, hh = wt["WihT"], wt["WhhT"]
                pe.wait_ge(sem("hidden_s"), i + 1)
                pe.wait_ge(sem("msg_sum_s"), i + 1)
                pe.wait_ge(sem("y_ready"), i + 1)
                msg, hid = fixed_view(am_s), step_view(hid2, i % 2)
                wide(pA, [(ih[:, 0:D], msg), (hh[:, 0:D], hid)]).then_inc(sem("r_gate"), 1)
                wide(pB, [(ih[:, D:2 * D], msg), (hh[:, D:2 * D], hid)]).then_inc(sem("z_gate"), 1)
                wide(pC, [(ih[:, 2 * D:], msg)])
                wide(pD, [(hh[:, 2 * D:], hid)]).then_inc(sem("n_gate"), 1)

            def output(i):
                pe.wait_ge(sem("hT_s4"), i + 2)
                pe.wait_ge(sem("h_new"), i + 1)
                product(pA, [(newT_s, wt["WoutT"][:])]).then_inc(sem("out_rows"), 1)

            pe.wait_ge(sem("agg_done3"), 1)
            pe.wait_ge(sem("deg_row_in"), 16)
            for name in ("r_ready", "z_ready", "n_in", "y_ready"):
                pe.sem_inc(sem(name), 1)
            messages(0)
            with pe.Fori(0, NS - 1) as i:
                gates(i)
                messages(i + 1)
                output(i)
            gates(NS - 1)
            pe.wait_ge(sem("h_new"), NS)
            pe.wait_ge(sem("r_ready"), NS + 1)
            product(pA, [(newT_s, wt["WoutT"][:])]).then_inc(sem("out_rows"), 1)

        @block.scalar
        def _(act):
            def ln_std(s, i):
                act.wait_ge(sem("ln_var"), i + 1 + s * NS)
                nc.scalar.activation(rstd[:], rstd[:], ACT.Sqrt).then_inc(sem("ln_std"), 1)

            def stage_agg(s, i):
                nc.scalar.copy(agg_s[:], agg[:, bass.ds(i * W, W)]).then_inc(sem(f"agg_staged{s}"), 1)

            with act.Fori(0, NS) as i:
                ln_std(0, i)
            act.wait_ge(sem("order_known"), 1)
            order = act.value_load(any_order[0:1, 0:1], min_val=0, max_val=1)

            def store_group(blk, sub, g):
                act.wait_ge(sem("cells"), (blk * SUBS + sub) * GS + g + 1 + CELL_RING)
                cells = count_blk[:, bass.ds((blk % 2) * BLK, BLK)].rearrange("p (s d) -> p s d", d=TD)
                nc.scalar.copy(cells[:, :, bass.ds((sub * GS + g) * G, G)],
                               p_cells[:, g % 3, 0:CELLS].rearrange("p (s d) -> p s d", d=G)).then_inc(
                    sem("stored"), 1)

            def copy_flip(b, sub, c):
                act.wait_ge(sem("flips"), b * (2 * SUBS) + sub * 2 + c + 1 + 2 * SUBS)
                act.wait_ge(sem("mixed"), b * (2 * SUBS) + sub * 2 + c + 1)
                nc.scalar.copy(flipped_s[0:HALF, :], p_flip[0:HALF, :]).then_inc(sem("flip_copied"), 1)

            def copy_indices(t, w):
                act.wait_ge(sem("win_mm"), t * WPS + w + 1)
                nc.scalar.copy(idx_slot[:, w * WCH:(w + 1) * WCH],
                               src_i[:, bass.ds(t * CPS + w * WCH, WCH)]).then_inc(sem("indices_ready"), 1)

            def step(blk, sub, clique):
                t = blk * SUBS + sub
                for g in range(GS):
                    store_group(blk, sub, g)
                    if clique and g == 1:
                        copy_flip(blk - 1, sub, 0)
                    if clique and g == 3:
                        copy_flip(blk - 1, sub, 1)
                    if g % 2:
                        copy_indices(t + 1, g // 2)

            def slot_free(blk, flips):
                act.wait_ge(sem("flips"), flips)
                act.wait_ge(sem("block_saved"), blk)
                act.sem_inc(sem("block_begun"), 1)

            def count_sorted():
                act.sem_inc(sem("stored"), CELL_RING)
                act.sem_inc(sem("flip_copied"), 1)
                act.wait_ge(sem("edges_in"), 32)
                for w in range(WPS):
                    copy_indices(0, w)
                with act.Fori(0, SUBS) as sub:
                    step(0, sub, False)
                with act.Fori(1, L2B + 1) as blk:
                    slot_free(blk, blk * (2 * SUBS))
                    with act.Fori(0, SUBS) as sub:
                        step(blk, sub, True)
                with act.Fori(L2B + 1, NBLK) as blk:
                    slot_free(blk, (L2B + 1) * 2 * SUBS)
                    with act.Fori(0, SUBS) as sub:
                        step(blk, sub, False)
                with act.Fori(STEPS + 1, STEPS + TAIL) as t:
                    for w in range(WPS):
                        copy_indices(t, w)

            def idle():
                act.sem_inc(sem("idle"), 1)

            def count_pieces():
                act.sem_inc(sem("piece_counted_act"), SUBS - KD)
                act.sem_inc(sem("part_added"), 1)
                with act.Fori(0, NBLK) as b:
                    act.wait_ge(sem("part_added"), b + 1)
                    for k in range(KD, SUBS):
                        act.wait_ge(sem(f"piece{k}"), b * 16 + 16)
                        for j in range(SHS):
                            last = nc.scalar.activation(unused[:, j * TD:(j + 1) * TD], piece[:, k, j * TD:(j + 1) * TD], ACT.Copy,
                                                        accum_out=out_part[:, k * SHS + j:k * SHS + j + 1])
                        last.then_inc(sem("piece_counted_act"), 1)
                        act.drain()

            branch(act, order, idle, count_sorted)
            act.wait_ge(sem("agg_done0"), 1)
            with act.Fori(0, NS) as i:
                act.wait_ge(sem("h_ready1"), i + 1)
                stage_agg(1, i)
                ln_std(1, i)
            branch(act, order, idle, count_pieces)
            act.wait_ge(sem("agg_done1"), 1)
            with act.Fori(0, NS) as i:
                stage_agg(2, i)
                act.wait_ge(sem("lin2"), i + 1)
                nc.scalar.activation(f_all[:, bass.ds(i * SB, SB), :], blocks(pB[:, 0:W]), ACT.Gelu).then_inc(
                    sem("gelu"), 1)
            act.wait_ge(sem("centred"), 1)
            nc.scalar.activation(sq_all, f_all, ACT.Square).then_inc(sem("squared"), 1)
            act.wait_ge(sem("var_ready"), 1)
            nc.scalar.activation(gain[:], gain[:], ACT.Sqrt).then_inc(sem("std_ready"), 1)
            with act.Fori(0, NS) as i:
                ln_std(2, i)
            act.wait_ge(sem("agg_done2"), 1)
            with act.Fori(0, NS) as i:
                act.wait_ge(sem("h_ready3"), i + 1)
                stage_agg(3, i)
                ln_std(3, i)
            act.wait_ge(sem("agg_done3"), 1)
            act.wait_ge(sem("b_rz_ready"), 1)
            b_in_gate = b_gates["b_ih"][:, 2:3]

            def copy_messages(i):
                act.wait_ge(sem("hT4"), i + 1)
                nc.scalar.copy(hT_s[:], pA[:, 0:W]).then_inc(sem("hT_s4"), 1)
                act.wait_ge(sem("hid_sum"), i + 1)
                nc.scalar.copy(ah_s, pC[:, 0:W]).then_inc(sem("hid_sum_s"), 1)
                act.wait_ge(sem("hidden"), i + 1)
                nc.scalar.activation(steps_of(hid2, i % 2), pB[:, 0:W], ACT.Identity, bias=b_in[:]).then_inc(
                    sem("hidden_s"), 1)
                act.wait_ge(sem("msg_sum"), i + 1)
                nc.scalar.copy(am_s, pD[:, 0:W]).then_inc(sem("msg_sum_s"), 1)

            def gates(i):
                act.wait_ge(sem("r_gate"), i + 1)
                nc.scalar.activation(r_s, pA[:, 0:W], ACT.Sigmoid, bias=b_rz[:, 0:1]).then_inc(sem("r_ready"), 1)
                act.wait_ge(sem("z_gate"), i + 1)
                nc.scalar.activation(z_s, pB[:, 0:W], ACT.Sigmoid, bias=b_rz[:, 1:2]).then_inc(sem("z_ready"), 1)
                act.wait_ge(sem("n_in"), i + 2)
                nc.scalar.activation(n_s, t_s, ACT.Tanh, bias=b_in_gate).then_inc(sem("tanh"), 1)

            copy_messages(0)
            with act.Fori(0, NS - 1) as i:
                gates(i)
                copy_messages(i + 1)
            gates(NS - 1)

        @block.vector
        def _(dve):
            V = nc.vector
            dve.wait_ge(sem("made"), 5)
            V.tensor_copy(iota16[:], iota_i[:])
            V.tensor_copy(iota_win[:], iota_i[:, 0:WIN])
            V.tensor_copy(tile_off[:], tile_off_i[:])
            V.tensor_copy(ident16[:], ident[:])
            V.tensor_copy(gbase[:], gbase_i[:])
            dve.drain()
            V.tensor_scalar(glast[:], gbase[:], float(G - 1), float(N_NODES - 1), ALU.add, ALU.min)
            dve.wait_ge(sem("ends_in"), 48)
            V.tensor_copy(dmax_f, dmax_i)
            V.tensor_copy(dmin_f, dmin_i)
            dve.drain()
            for g in range(NGT):
                V.tensor_scalar(scr, dmax_f, gbase[:, g:g + 1], None, ALU.is_lt, ALU.add,
                                accum_out=first_chunk[:, g:g + 1])
                dve.drain()
                V.tensor_scalar(first_chunk[:, g:g + 1], first_chunk[:, g:g + 1], float(NCH - 1), None, ALU.min)
                dve.drain()
                V.tensor_copy(chunk_idx[:, g:g + 1], first_chunk[:, g:g + 1]).then_inc(sem("chunk_known"), 1)
            dve.wait_ge(sem("chunk_rows"), 16 * NGT)
            V.tensor_copy(chunk_dst, chunk_dst_i)
            dve.drain()
            V.tensor_tensor(chunk_dst, chunk_dst, gbase[:].rearrange("p (g o) -> p g o", o=1).to_broadcast(
                [P, NGT, P]), ALU.is_lt)
            dve.drain()
            V.tensor_reduce(in_chunk[:], chunk_dst, AX_X, ALU.add)
            dve.drain()
            V.scalar_tensor_tensor(out=in_chunk[:], in0=first_chunk[:], scalar=float(P), in1=in_chunk[:],
                                   op0=ALU.mult, op1=ALU.add)
            dve.drain()
            V.tensor_scalar(edge_idx[:], in_chunk[:], float(NCH * P - GE - 1), None, ALU.min).then_inc(
                sem("edge_known"), 1)
            spans = scr[:, 0:NCH // WCH]
            firsts = dmin_f.rearrange("p (n c) -> p n c", c=WCH)[:, :, 0]
            lasts = dmax_f.rearrange("p (n c) -> p n c", c=WCH)[:, :, WCH - 1]
            V.tensor_tensor(spans, lasts, firsts, ALU.subtract)
            dve.drain()
            V.tensor_scalar(spans, spans, float(WIN - 1), None, ALU.is_gt)
            dve.drain()
            V.tensor_reduce(bad3[:, 1:2], spans, AX_X, ALU.add)
            dve.wait_ge(sem("dst_in"), 16)
            V.tensor_copy(rel, dst_i)
            dve.drain()
            dve.wait_ge(sem("next_in"), 48)
            V.tensor_copy(scr, next_i)
            dve.drain()
            V.tensor_tensor(scr, rel, scr, ALU.is_gt)
            dve.drain()
            V.tensor_reduce(bad3[:, 2:3], scr, AX_X, ALU.add)
            V.tensor_tensor(rel.rearrange("p (n c) -> p n c", c=WCH), rel.rearrange("p (n c) -> p n c", c=WCH),
                            dmin_f.rearrange("p (n c) -> p n c", c=WCH)[:, :, 0:1].to_broadcast(
                                [P, NCH // WCH, WCH]), ALU.subtract)
            dve.drain()

            def layernorm(s, i, split=None):
                for b in range(SB):
                    V.bn_stats(stats[:, b, :], xs[:, b, :])
                dve.drain()
                for b in range(SB):
                    V.bn_aggr(mv[:, b, :], stats[:, b, :])
                dve.drain()
                V.tensor_scalar(rstd[:], mv[:, :, 1], EPS, None, ALU.add).then_inc(sem("ln_var"), 1)
                dve.wait_ge(sem("ln_std"), i + 1 + s * NS)
                V.reciprocal(rstd[:], rstd[:])
                dve.drain()
                for b in range(SB):
                    V.tensor_scalar(hT_s[:, b * P:(b + 1) * P], xs[:, b, :], mv[:, b, 0:1], rstd[:, b:b + 1],
                                    ALU.subtract, ALU.mult)
                dve.drain()
                V.tensor_scalar(flat(hs), hT_s[:], 0.0, None, ALU.max).then_inc(sem("h_rows"), 1)
                if split is not None:
                    dve.drain()
                    split_rows(split, i)
                dve.drain()
                dve.wait_ge(sem("rows_saved"), i + 1 + s * NS)
                if s:
                    dve.wait_ge(sem("x_saved"), i + 1 + (s - 1) * NS)
                dve.sem_inc(sem(f"h_ready{s}"), 1)

            def split_rows(l, i):
                part = [planes[:, n, bass.ds(i * SB, SB), :] for n in range(2)]
                V.tensor_scalar(part[0], hs[:], SCALE, None, ALU.mult)
                dve.drain()
                V.scalar_tensor_tensor(out=part[1], in0=hs[:], scalar=SCALE, in1=part[0], op0=ALU.mult,
                                       op1=ALU.subtract).then_inc(sem(f"planes_ready{l}"), 1)

            dve.sem_inc(sem("h_ready0"), 1)
            with dve.Fori(0, NS) as i:
                dve.wait_ge(sem("x_in"), i * 16 + 16 + 0 * NS * 16)
                layernorm(0, i)

            by_group = (lambda v: v.rearrange("p (g e) -> p g e", g=NGT))
            dve.wait_ge(sem("group_dst"), 16 * NGT)
            V.tensor_copy(past_group[:], group_dst_i[:, :, GE])
            V.tensor_copy(by_group(key_b), group_dst_i[:, :, 0:GE])
            dve.drain()
            V.tensor_tensor(past_group[:], past_group[:], glast[:], ALU.is_le)
            V.tensor_tensor(by_group(key_b), by_group(key_b), gbase[:].rearrange("p (g o) -> p g o", o=1).to_broadcast(
                [P, NGT, GE]), ALU.subtract)
            dve.drain()
            V.tensor_reduce(bad3[:, 0:1], past_group[:], AX_X, ALU.add)
            for g in range(NGT):
                for j in range(G):
                    n = (g * G + j) % 5
                    V.tensor_scalar(deg_tmp[:, n], by_group(key_b)[:, g, :], float(j), None,
                                    ALU.is_equal, ALU.add, accum_out=deg_g[:, g, j:j + 1])
                    if n == 4:
                        dve.drain()
            dve.drain()
            dve.sem_inc(sem("deg_counted"), 1)
            V.tensor_reduce(bad[:], bad3[:], AX_X, ALU.add)
            dve.wait_ge(sem("group_src"), 16 * NGT)
            V.tensor_scalar(key_ai, group_src_i, 7, None, ALU.arith_shift_right)
            dve.drain()
            V.tensor_copy(key_c, key_ai)
            dve.drain()
            V.tensor_scalar(key_c, key_c, float(G), 1.0, ALU.mult, ALU.add)
            dve.drain()
            V.tensor_tensor(key_c, key_c, key_b, ALU.add)
            dve.drain()
            V.scalar_tensor_tensor(out=key_c, in0=key_b, scalar=0.0, in1=key_c, op0=ALU.is_ge, op1=ALU.mult)
            dve.drain()
            V.scalar_tensor_tensor(out=key_c, in0=key_b, scalar=float(G - 1), in1=key_c, op0=ALU.is_le, op1=ALU.mult)
            V.tensor_scalar(key_ai, group_src_i, P - 1, None, ALU.bitwise_and)
            dve.drain()
            V.tensor_scalar(key_b, key_c, -1.0, None, ALU.add)
            dve.drain()
            V.tensor_copy(key_c, key_ai)
            dve.drain()
            dve.sem_inc(sem("keys_made"), 1)
            dve.wait_ge(sem("keys_flipped"), 1)
            V.tensor_copy(keyT.rearrange("p k (g e) -> p k g e", g=NGT),
                          ps[:, 0:NKEY].rearrange("p (g k e) -> p k g e", g=NGT, k=K)).then_inc(sem("keyT_ready"), 1)
            dve.wait_ge(sem("sources_flipped"), 1)
            V.tensor_copy(slT.rearrange("p k (g e) -> p k g e", g=NGT),
                          ps[:, 0:NKEY].rearrange("p (g k e) -> p k g e", g=NGT, k=K)).then_inc(sem("slT_ready"), 1)
            dve.wait_ge(sem("bad_summed"), 1)
            V.tensor_scalar(any_order[:], ps[:, 0:1], 1.0, None, ALU.min)
            dve.drain()
            dve.sem_inc(sem("area_free0"), 1)
            dve.sem_inc(sem("order_known"), 1)
            order = dve.value_load(any_order[0:1, 0:1], min_val=0, max_val=1)

            def sum_any(l):
                _, weighted, counted = GEN[l]

                def f():
                    dve.wait_ge(sem("g_edges"), 48 * (l + 1))
                    V.tensor_copy(g_key, g_src if l == 2 else g_dst)
                    V.tensor_scalar(g_idx, g_dst, N_CLIQUES - 1, None, ALU.min)
                    V.memset(agg[:], 0.0)
                    V.memset(g_iota, 0.0)
                    if counted:
                        V.memset(g_count, 0.0)
                    dve.drain()
                    for n in range(0, TILE, 2 * P):
                        V.tensor_scalar(g_iota[:, n:n + 2 * P], iota16[:, 0:2 * P], float(n), None, ALU.add)
                    dve.drain()
                    dve.sem_inc(sem("g_ready"), 1)
                    dve.sem_inc(sem("g_added"), 2)

                    def add(j, n):
                        t, s = n % NT, n % 2
                        dve.wait_ge(sem("g_mm"), j * (2 * NT) + mm_base(l) + n + 1 + MM_CREDIT)
                        cols, slot = slice(t * TILE, (t + 1) * TILE), slice(s * TILE, (s + 1) * TILE)
                        last = V.tensor_tensor(agg[:, cols], agg[:, cols], pA[:, slot], ALU.add)
                        if counted:
                            last = V.tensor_tensor(g_count[:, cols], g_count[:, cols], pB[:, slot], ALU.add)
                        last.then_inc(sem("g_added"), 1)

                    with dve.Fori(0, NCH // 2) as j:
                        for k in range(2):
                            dve.drain()
                            V.tensor_scalar(tile_key[:], tile_off[:], g_key[:, bass.ds(j * 2 + k, 1)], None, ALU.add)
                            dve.drain()
                            for t in range(NT):
                                n = k * NT + t
                                dve.wait_ge(sem("g_mm"), j * (2 * NT) + mm_base(l) + n - 1 + MM_CREDIT)
                                scale = (g_w[:, bass.ds(j * 2 + k, 1)], ALU.is_equal, ALU.mult) if weighted else (
                                    None, ALU.is_equal)
                                V.tensor_scalar(g_onehot[:, n % 2, :], g_iota, tile_key[:, t:t + 1],
                                                *scale).then_inc(sem("g_onehot"), 1)
                                if n:
                                    add(j, n - 1)
                        add(j, 2 * NT - 1)
                        dve.drain()
                    if l == 1:
                        dve.sem_inc(sem("g_counted"), 1)
                        dve.wait_ge(sem("deg_out"), 32)
                    if counted:
                        V.tensor_scalar(g_count, g_count, 1.0, None, ALU.max)
                        dve.drain()
                        V.reciprocal(g_count, g_count)
                        dve.drain()
                        V.tensor_tensor(agg[:], agg[:], g_count, ALU.mult)
                        dve.drain()
                    if l == 2:
                        V.memset(inv_cnt[:], 1.0)
                        V.memset(out_cnt[:], 0.0)
                        dve.drain()
                    dve.sem_inc(sem(f"agg_done{l}"), 1)
                return f

            def window_onehots(t, w):
                dve.wait_ge(sem("win_mm"), t * WPS + w + 1)
                for c in range(w * WCH, (w + 1) * WCH):
                    last = V.tensor_scalar(oh_win[:, c, :], iota_win[:], rel[:, bass.ds(t * CPS + c, 1)],
                                           w_edge[:, bass.ds(t * CPS + c, 1)], ALU.is_equal, ALU.mult)
                last.then_inc(sem("win_onehots"), 1)

            def window_copy(t):
                dve.wait_ge(sem("win_mm"), t * WPS + WIN_RING)
                V.tensor_copy(win_sum[:], p_win).then_inc(sem("win_copied"), 1)

            def window_adds(t, regs):
                dve.load(regs, win_base[0:1, bass.ds(t * WPS, WPS)])
                for w in range(WPS):
                    base = dve.snap(regs[w], min_val=0, max_val=NCOL - WIN)
                    dve.drain()
                    V.tensor_tensor(agg[:, bass.ds(base, WIN)], agg[:, bass.ds(base, WIN)],
                                    win_sum[:, w * WIN:(w + 1) * WIN], ALU.add)

            def group_onehots(t, g):
                dve.wait_ge(sem("cells"), t * GS + g + 1)
                for k in range(K):
                    s = (g % 3) * K + k
                    V.tensor_scalar(oh_src[:, s, :], iota16[:, 0:P], slT[:, k, bass.ds(t * GS + g, 1)], None,
                                    ALU.is_equal)
                    last = V.tensor_scalar(oh_cell[:, s, :], iota16[:], keyT[:, k, bass.ds(t * GS + g, 1)], None,
                                           ALU.is_equal)
                last.then_inc(sem("onehots"), 1)

            def split_cliques(b):
                dve.wait_ge(sem("mixed"), b * (2 * SUBS) + 1)
                dve.wait_ge(sem("xc_loaded"), b * 16 + 16)
                h = slice(0, HALF)
                rows, r, r2 = (v[h, :].rearrange("p (c d) -> p c d", c=2) for v in (xc_in, xc_r, xc_r2))
                V.tensor_copy(xc_plane[h, :, 0, :], rows)
                dve.drain()
                V.tensor_tensor(r, rows, xc_plane[h, :, 0, :], ALU.subtract)
                dve.drain()
                V.tensor_copy(xc_plane[h, :, 1, :], r)
                dve.drain()
                V.tensor_tensor(r2, r, xc_plane[h, :, 1, :], ALU.subtract)
                dve.drain()
                V.tensor_copy(xc_plane[h, :, 2, :], r2).then_inc(sem("xc_split"), 1)

            def add_mix(b, sub):
                dve.wait_ge(sem("mixed"), b * (2 * SUBS) + sub * 2 + 1)
                cols = clique_sum[:, bass.ds((sub + SUBS - 1) % SUBS * W, W)]
                V.tensor_tensor(cols, cols, p_mix, ALU.add).then_inc(sem("mix_added"), 1)

            def step(blk, sub, regs, clique):
                t = blk * SUBS + sub
                group_onehots(t, 0)
                group_onehots(t, 1)
                window_copy(t)
                window_onehots(t, 0)
                group_onehots(t, 2)
                if clique:
                    add_mix(blk - 1, sub)
                group_onehots(t, 3)
                window_onehots(t, 1)
                group_onehots(t, 4)
                window_adds(t, regs)
                group_onehots(t, 5)
                window_onehots(t, 2)

            def count_sorted():
                V.memset(agg[:], 0.0)
                V.memset(clique_sum, 0.0)
                V.memset(out_cnt[:], 0.0)
                V.memset(p_win, 0.0)
                V.memset(p_mix, 0.0)
                dve.drain()
                dve.sem_inc(sem("xc_split"), 1)
                dve.wait_ge(sem("edges_in"), 32)
                regs = [dve.alloc_register(f"win_base{w}") for w in range(WPS)]
                with dve.Fori(0, SUBS) as sub:
                    step(0, sub, regs, False)
                with dve.Fori(1, L2B + 1) as blk:
                    split_cliques(blk - 1)
                    with dve.Fori(0, SUBS) as sub:
                        step(blk, sub, regs, True)
                add_mix(L2B, 0)
                with dve.Fori(L2B + 1, NBLK) as blk:
                    with dve.Fori(0, SUBS) as sub:
                        step(blk, sub, regs, False)
                with dve.Fori(STEPS, STEPS + TAIL) as t:
                    for w in range(WPS):
                        window_onehots(t, w)
                    dve.drain()
                    window_copy(t)
                    window_adds(t, regs)
                dve.drain()
                window_copy(STEPS + TAIL)
                window_adds(STEPS + TAIL, regs)
                dve.wait_ge(sem("block_saved"), NBLK + 1)
                dve.drain()
                dve.sem_inc(sem("agg_done0"), 1)

            def multiply(l):
                def f():
                    before = 0 if l == 1 else 1
                    dve.sem_inc(sem("taken"), 2)
                    if l == 1:
                        dve.sem_inc(sem("piece_counted"), KD)

                    def take_out(b, which):
                        slot = (b % 2) * (2 * TILE)
                        if l == 1:
                            for k in range(KD):
                                dve.wait_ge(sem(f"piece{k}"), b * 16 + 16)
                                V.tensor_reduce(out_part[:, k * SHS:(k + 1) * SHS],
                                                piece[:, k, :].rearrange("p (s d) -> p s d", d=TD), AX_X,
                                                ALU.add).then_inc(sem("piece_counted"), 1)
                            dve.wait_ge(sem("deg_in"), b * 16 + 16)
                            V.tensor_scalar(inv_deg, deg_s[:, bass.ds((b % 2) * TD, TD)], 1.0, None, ALU.max)
                            dve.drain()
                            V.reciprocal(inv_deg, inv_deg)
                            dve.wait_ge(sem("piece_counted_act"), b * (SUBS - KD) + 2 * (SUBS - KD))
                            V.tensor_tensor(out_cnt[:, which, :], out_cnt[:, which, :], out_part[:], ALU.add).then_inc(
                                sem("part_added"), 1)
                            dve.drain()
                        dve.wait_ge(sem("piece_used"), b * SUBS + before * (NBLK + 1) * SUBS + 2 * SUBS)
                        sums, cols = ps[:, bass.ds(slot, TD)], agg[:, bass.ds(b * TD, TD)]
                        if l == 1:
                            V.scalar_tensor_tensor(out=cols, in0=sums, scalar=1.0 / SCALE, in1=inv_deg, op0=ALU.mult,
                                                   op1=ALU.mult).then_inc(sem("taken"), 1)
                        else:
                            V.tensor_scalar(cols, sums, 1.0 / SCALE, None, ALU.mult).then_inc(sem("taken"), 1)
                        dve.drain()

                    with dve.Fori(0, L2B) as b:
                        take_out(b, 0)
                    with dve.Fori(L2B, NBLK) as b:
                        take_out(b, 1)
                    if l == 1:
                        V.tensor_tensor(inv_cnt[:], out_cnt[:, 0, :], out_cnt[:, 1, :], ALU.add)
                        dve.drain()
                        V.tensor_scalar(inv_cnt[:], inv_cnt[:], 1.0, None, ALU.max)
                        dve.drain()
                        V.reciprocal(inv_cnt[:], inv_cnt[:])
                        dve.drain()
                    dve.sem_inc(sem(f"agg_done{l}"), 1)
                return f

            branch(dve, order, sum_any(0), count_sorted)

            dve.sem_inc(sem("h_ready1"), 1)
            with dve.Fori(0, NS) as i:
                dve.wait_ge(sem("hT1"), i + 1)
                dve.wait_ge(sem("agg_staged1"), i + 1)
                V.tensor_tensor(prod_s, pA[:, 0:W], agg_s[:], ALU.mult).then_inc(sem("prod1"), 1)
                dve.wait_ge(sem("lin1"), i + 1)
                V.tensor_copy(z_s, pB[:, 0:W])
                dve.drain()
                V.scalar_tensor_tensor(out=r_s, in0=z_s, scalar=SLOPE, in1=z_s, op0=ALU.mult, op1=ALU.max)
                dve.drain()
                dve.wait_ge(sem("x_in"), i * 16 + 16 + 1 * NS * 16)
                V.tensor_tensor(flat(xs), flat(xs), r_s, ALU.add).then_inc(sem("x_new"), 1)
                dve.drain()
                layernorm(1, i, split=1)
            dve.sem_inc(sem("area_free1"), 1)
            branch(dve, order, sum_any(1), multiply(1))

            dve.sem_inc(sem("h_free2"), 1)
            with dve.Fori(0, NS) as i:
                dve.wait_ge(sem("hT2"), i + 1)
                V.tensor_copy(hT_s[:], pA[:, 0:W]).then_inc(sem("hT_s2"), 1)
                dve.wait_ge(sem("lin2"), i + 1)
                dve.sem_inc(sem("h_free2"), 1)
            dve.wait_ge(sem("mean_sum"), 1)
            V.scalar_tensor_tensor(out=scaled_mean[:], in0=pC[:, 0:D], scalar=1.0 / N_NODES, in1=bcast["mean_scale"][:],
                                   op0=ALU.mult, op1=ALU.mult)
            dve.drain()
            V.tensor_tensor(f_all, f_all, scaled_mean[:].rearrange("p (o d) -> p o d", o=1).to_broadcast([P, NB, D]),
                            ALU.subtract).then_inc(sem("centred"), 1)
            dve.wait_ge(sem("var_sum"), 1)
            V.tensor_scalar(gain[:], pC[:, 0:D], 1.0 / N_NODES, EPS, ALU.mult, ALU.add).then_inc(sem("var_ready"), 1)
            dve.wait_ge(sem("std_ready"), 1)
            V.reciprocal(scaled_mean[:], gain[:])
            dve.drain()
            V.tensor_tensor(gain[:], scaled_mean[:], bcast["gn_weight"][:], ALU.mult)
            dve.drain()
            dve.sem_inc(sem("h_ready2"), 1)

            def over_blocks(t):
                return t[:].rearrange("p (o d) -> p o d", o=1).to_broadcast([P, SB, D])

            z3 = blocks(z_s)
            with dve.Fori(0, NS) as i:
                V.tensor_tensor(z3, f_all[:, bass.ds(i * SB, SB), :], over_blocks(gain), ALU.mult)
                dve.drain()
                V.tensor_tensor(z3, z3, over_blocks(bcast["gn_bias"]), ALU.add)
                dve.drain()
                dve.wait_ge(sem("h_in2"), i * 16 + 16)
                V.tensor_tensor(z3, z3, hs[:], ALU.add)
                dve.drain()
                dve.wait_ge(sem("x_in"), i * 16 + 16 + 2 * NS * 16)
                V.tensor_tensor(xs[:], xs[:], z3, ALU.add).then_inc(sem("x_new"), 1)
                dve.drain()
                layernorm(2, i)
            dve.sem_inc(sem("area_free2"), 1)

            def cliques_sorted():
                V.tensor_copy(agg[:, 0:NPAD], clique_sum)
                dve.drain()
                dve.sem_inc(sem("agg_done2"), 1)

            V.tensor_copy(last_clique[:], last_col[:].to_broadcast([P, P]))
            dve.drain()
            branch(dve, order, sum_any(2), cliques_sorted)
            dve.wait_ge(sem("clique_lin"), 1)
            V.tensor_copy(clique_out[:], pC[:, 0:D])
            dve.drain()
            dve.sem_inc(sem("h_ready3"), 1)
            with dve.Fori(0, NS) as i:
                dve.wait_ge(sem("lin3"), i + 1)
                for b in range(SB):
                    V.scalar_tensor_tensor(out=z3[:, b, :], in0=clique_out[:], scalar=out_cnt[:, 1, bass.ds(i * SB + b, 1)],
                                           in1=blocks(pB[:, 0:W])[:, b, :], op0=ALU.mult, op1=ALU.add)
                dve.drain()
                for b in range(SB):
                    V.scalar_tensor_tensor(out=z3[:, b, :], in0=z3[:, b, :], scalar=inv_cnt[:, bass.ds(i * SB + b, 1)],
                                           in1=bcast["bc"][:], op0=ALU.mult, op1=ALU.add)
                dve.drain()
                dve.wait_ge(sem("x_in"), i * 16 + 16 + 3 * NS * 16)
                V.tensor_tensor(xs[:], xs[:], z3, ALU.add).then_inc(sem("x_new"), 1)
                dve.drain()
                layernorm(3, i, split=3)

            V.tensor_tensor(b_rz[:], b_gates["b_ih"][:, 0:2], b_gates["b_hh"][:, 0:2], ALU.add)
            dve.drain()
            dve.sem_inc(sem("b_rz_ready"), 1)
            dve.sem_inc(sem("area_free3"), 1)
            branch(dve, order, sum_any(3), multiply(3))

            b_hn = b_gates["b_hh"][:, 2:3]
            with dve.Fori(0, NS) as i:
                dve.wait_ge(sem("n_gate"), i + 1)
                dve.wait_ge(sem("r_ready"), i + 2)
                V.scalar_tensor_tensor(out=t_s, in0=pD[:, 0:W], scalar=b_hn, in1=r_s, op0=ALU.add, op1=ALU.mult)
                dve.drain()
                V.tensor_tensor(t_s, t_s, pC[:, 0:W], ALU.add).then_inc(sem("n_in"), 1)
                dve.wait_ge(sem("tanh"), i + 1)
                V.tensor_tensor(r_s, steps_of(hid2, i % 2), n_s, ALU.subtract)
                dve.drain()
                V.tensor_tensor(r_s, r_s, z_s, ALU.mult)
                dve.drain()
                V.tensor_tensor(newT_s, r_s, n_s, ALU.add).then_inc(sem("h_new"), 1)
                dve.wait_ge(sem("out_rows"), i + 1)
                dve.wait_ge(sem("x_biased"), i + 1)
                rows = steps_of(xs2, i % 2)
                V.tensor_tensor(rows, rows, pA[:, 0:W], ALU.add).then_inc(sem("y_ready"), 1)
                dve.drain()


def kernel(**inputs):
    import numpy as np
    import concourse.bacc as bacc
    from concourse.bass_utils import run_bass_kernel_spmd as run

    def edges(name, fill):
        a = np.ascontiguousarray(inputs[name])
        pad = np.full((NCH * P - N_EDGES,), fill, a.dtype)
        return np.concatenate([a, pad]).reshape(NCH, P)

    def wT(name):
        return np.ascontiguousarray(np.asarray(inputs[name]).T)

    def row(*names):
        return np.ascontiguousarray(np.stack([np.asarray(inputs[n]) for n in names]))

    x = np.ascontiguousarray(inputs["x"])
    xc = np.ascontiguousarray(inputs["L2_gnn_x_clique"])
    src, dst, w = edges("src", N_NODES), edges("dst", N_NODES), edges("edge_weight", 0)

    def gates(name):
        return np.ascontiguousarray(np.asarray(inputs[name]).reshape(3, D).T)

    arrays = {
        "x": np.concatenate([x, np.zeros((NPAD - N_NODES, D), x.dtype)]),
        "dst_rows": dst, "src_flat": src.reshape(1, -1), "dst_flat": dst.reshape(1, -1),
        "srcT": np.ascontiguousarray(src.T), "dstT": np.ascontiguousarray(dst.T), "wT": np.ascontiguousarray(w.T),
        "win_base_src": np.concatenate([np.zeros((1, WPS), dst.dtype), dst[::WCH, 0:1].T], axis=1),
        "x_clique": np.concatenate([xc, np.repeat(xc[-1:], N_XC - N_CLIQUES, axis=0)]),
        "last_clique": np.ascontiguousarray(xc[-1:].T),
        "W1T": wT("L0_gnn_W1"), "W2T": wT("L0_gnn_W2"), "WlT": wT("L1_gnn_Wl"), "WrT": wT("L1_gnn_Wr"),
        "WcT": wT("L2_gnn_W"), "WinT": wT("L3_gnn_W_in"), "Wmsg": np.ascontiguousarray(inputs["L3_gnn_W_msg"]),
        "WihT": wT("L3_gnn_W_ih"), "WhhT": wT("L3_gnn_W_hh"), "WoutT": wT("L3_gnn_W_out"),
        "b12": row("L0_gnn_b1", "L0_gnn_b2"), "bl": row("L1_gnn_bl"), "bc": row("L2_gnn_b"),
        "b_ih": gates("L3_gnn_b_ih"), "b_hh": gates("L3_gnn_b_hh"), "b_in_row": row("L3_gnn_b_in"),
        "bout": row("L3_gnn_b_out"), "b_in": np.ascontiguousarray(row("L3_gnn_b_in").T),
        "gn_weight": row("L1_gnn_gn_weight"), "gn_bias": row("L1_gnn_gn_bias"), "mean_scale": row("L1_gnn_mean_scale"),
    }
    nc = bacc.Bacc("TRN2", target_bir_lowering=False, num_devices=1)
    A, fed = {}, {}
    for name, a in arrays.items():
        A[name] = nc.dram_tensor(f"in_{name}", a.shape, mybir.dt.from_np(a.dtype), kind="ExternalInput").ap()
        fed[f"in_{name}"] = a
    out = nc.dram_tensor("out_rows_padded", (NPAD, D), F32, kind="ExternalOutput").ap()
    build_gnn(nc, A, out)
    r = run(nc, [fed], core_ids=[0])
    return r.results[0]["out_rows_padded"][:N_NODES]
```

```python
from contextlib import ExitStack

import concourse.bass as bass
from concourse import mybir

F32 = mybir.dt.float32
F16 = mybir.dt.float16
BF16 = mybir.dt.bfloat16
I32 = mybir.dt.int32
ALU = mybir.AluOpType
ACT = mybir.ActivationFunctionType
AX_X = mybir.AxisListType.X

P = 128
D = 128
N_NODES = 6250
N_CLIQUES = 3125
N_EDGES = 206250
EPS = 1e-5
SLOPE = 0.2
SCALE = 4096.0

NB = -(-N_NODES // P)
NPAD = NB * P
SB = 7
NS = NB // SB
W = SB * P
LAST = N_NODES - (NB - 1) * P
TILE = 512
NT = -(-NPAD // TILE)
NCOL = NT * TILE

G = 6
K = 2
GS = 6
SUBS = 7
TD = G * GS * SUBS
HALF = TD // 2
NBLK = -(-N_NODES // TD)
BLK = NB * TD
CELLS = NB * G
NGT = -(-NBLK * GS * SUBS // P)
KD = 4
SHS = NB // SUBS
L2B = -(-N_CLIQUES // TD)
N_XC = L2B * TD

WIN = 32
WCH = 3
WPS = 3
CPS = WCH * WPS
STEPS = NBLK * SUBS
TAIL = 5
NCH = (STEPS + TAIL) * CPS
assert NCH * P >= N_EDGES and NCH % 2 == 0


def build_gnn(nc, A, out):
    with ExitStack() as ctx:
        def sb(name, shape, dt=F32):
            return ctx.enter_context(nc.sbuf_tensor(name, shape, dt))

        sems = {}

        def sem(name):
            if name not in sems:
                sems[name] = ctx.enter_context(nc.semaphore(name))
            return sems[name]

        x_dram = nc.dram_tensor("x_stream", (NPAD, D), F32).ap()
        rows_dram = nc.dram_tensor("node_rows", (NPAD, D), F32).ap()
        deg_dram = nc.dram_tensor("in_degrees", (1, NGT * P * G), F32).ap()
        inv_deg_dram = nc.dram_tensor("one_over_in_degrees", (1, NGT * P * G), F32).ap()
        cells_dram = nc.dram_tensor("edge_counts", (NBLK, P, BLK), F16).ap()

        class Region:

            def __init__(self, name, words):
                self.t, self.words = sb(name, [P, words]), words

            def view(self, start, words, dt=F32):
                assert start + words <= self.words
                v = self.t[:, start:start + words]
                return v if dt == F32 else v.bitcast(dt)

        agg = sb("agg", [P, NCOL])
        carry = Region("carry", NPAD)
        big = Region("big", BLK)
        edge_area = Region("edge_area", 13600)

        GE = K * P

        at = 0

        def take(words, dt=F32):
            nonlocal at
            v = edge_area.view(at, words, dt)
            at += words
            return v

        keyT = take(K * NGT * P // 2, F16).rearrange("p (k g) -> p k g", k=K)
        slT = take(K * NGT * P // 2, F16).rearrange("p (k g) -> p k g", k=K)
        src_i = take(NCH, I32)
        rel = take(NCH)
        w_edge = take(NCH)
        oh_src = take(3 * K * P // 2, BF16).rearrange("p (s n) -> p s n", s=3 * K)
        deg_unused = edge_area.view(at, G * GE // 2, F16).rearrange("p (s e) -> p s e", s=G)
        oh_cell = take(3 * K * CELLS // 2, BF16).rearrange("p (s n) -> p s n", s=3 * K)
        gathered = take(CPS * D).rearrange("p (s n) -> p s n", s=CPS)
        oh_win = take(CPS * WIN).rearrange("p (s n) -> p s n", s=CPS)
        flipped_s = take(W // 2, F16)
        xc_plane = take(2 * 2 * 3 * D // 2, BF16).rearrange("p (s c l n) -> p s c l n", s=2, c=2, l=3)
        xc_in = take(2 * D)
        xc_r = take(2 * D)
        xc_r2 = take(2 * D)
        idx_slot = take(CPS, I32)
        group_rel = take(2 * TAIL * GE // 2, F16)
        planes = edge_area.view(0, NPAD, F16).rearrange("p (l b n) -> p l b n", l=2, b=NB)
        inv_deg_s = edge_area.view(NPAD, 2 * TD)
        unused = edge_area.view(NPAD + 3 * TD, SHS * TD // 2, F16)
        deg_row = edge_area.view(0, NPAD)
        am_s, ah_s, t_s, newT_s = (edge_area.view(NPAD + n * W, W) for n in range(4))
        xs2 = edge_area.view(NPAD + 4 * W, 2 * W)
        hid2 = big.view(0, 2 * W)

        count_blk = big.view(0, BLK, F16)
        piece = big.view(0, BLK // 2, F16).rearrange("p (k n) -> p k n", k=SUBS)
        dmax_i, dmin_i = big.view(0, NCH, I32), big.view(NCH, NCH, I32)
        dmax_f, dmin_f = big.view(2 * NCH, NCH), big.view(3 * NCH, NCH)
        scr = big.view(4 * NCH, NCH)
        dst_i, next_i = big.view(5 * NCH, NCH, I32), big.view(6 * NCH, NCH, I32)
        NKEY = NGT * GE
        group_dst_i = carry.view(0, NGT * (GE + 1), I32).rearrange("p (g e) -> p g e", g=NGT)
        chunk_dst_i = carry.view(NGT * (GE + 1), NGT * P, I32).rearrange("p (g e) -> p g e", g=NGT)
        chunk_dst = carry.view(NGT * (GE + 1 + P), NGT * P).rearrange("p (g e) -> p g e", g=NGT)
        group_src_i = agg[:, 0:NKEY].bitcast(I32)
        key_b, key_c, key_a = big.view(NKEY, NKEY), big.view(2 * NKEY, NKEY), big.view(3 * NKEY, NKEY)
        key_ai = big.view(0, NKEY, I32)
        f_all = big.view(0, NPAD).rearrange("p (b d) -> p b d", d=D)
        prod_s, r_s, z_s, n_s = (big.view(BLK - (n + 1) * W, W) for n in range(4))
        sq_all = agg[:, 0:NPAD].rearrange("p (b d) -> p b d", d=D)
        hidden_all = carry.view(0, NPAD)
        clique_sum = carry.view(0, NPAD)
        g_src, g_dst, g_idx = (edge_area.view(n * NCH, NCH, I32) for n in range(3))
        g_key, g_w = edge_area.view(3 * NCH, NCH), edge_area.view(4 * NCH, NCH)
        g_count = big.view(0, NCOL)
        g_onehot = big.view(NCOL, 2 * TILE).rearrange("p (s n) -> p s n", s=2)
        g_rows = big.view(NCOL + 2 * TILE, 2 * D).rearrange("p (s n) -> p s n", s=2)
        g_iota_i = big.view(NCOL + 2 * TILE + 2 * D, TILE, I32)
        g_iota = big.view(NCOL + 3 * TILE + 2 * D, TILE)

        row_slots = {0: (agg[:, 2400:2400 + 2 * W], agg[:, 2400 + 2 * W:2400 + 4 * W])}
        for s in (1, 2):
            row_slots[s] = (edge_area.view(9000, 2 * W), edge_area.view(9000 + 2 * W, 2 * W))
        hs = sb("hs", [P, SB, D])
        agg_s = sb("agg_s", [P, W])
        hT_s = sb("hT_s", [P, W])
        stats = sb("stats", [P, SB, 6])
        mv = sb("mv", [P, SB, 2])
        rstd = sb("rstd", [P, SB])
        scaled_mean = sb("scaled_mean", [P, D])
        gain = sb("gain", [P, D])
        ones = sb("ones", [P, P])
        ident = sb("ident", [P, P])
        ones16 = sb("ones16", [P, P], BF16)
        ident16 = sb("ident16", [P, P], F16)
        iota_i = sb("iota_i", [P, CELLS], I32)
        iota16 = sb("iota16", [P, CELLS], F16)
        iota_win = sb("iota_win", [P, WIN])
        chunk_slot = sb("chunk_slot", [P, 2], I32)
        tile_off_i = sb("tile_off_i", [P, NT], I32)
        tile_off = sb("tile_off", [P, NT])
        tile_key = sb("tile_key", [P, NT])
        gbase_i = sb("gbase_i", [P, NGT], I32)
        gbase = sb("gbase", [P, NGT])
        glast = sb("glast", [P, NGT])
        first_chunk = sb("first_chunk", [P, NGT])
        in_chunk = sb("in_chunk", [P, NGT])
        past_group = sb("past_group", [P, NGT])
        edge_idx = sb("edge_idx", [P, NGT], I32)
        inv_deg_g = sb("inv_deg_g", [P, 2 * TAIL * G])
        deg_g = sb("deg_g", [P, 2 * TAIL * G])
        chunk_idx = sb("chunk_idx", [P, NGT], I32)
        win_base = sb("win_base", [1, WPS + NCH // WCH], I32)
        win_sum = sb("win_sum", [P, WPS * WIN])
        bad3 = sb("bad3", [P, 3])
        bad = sb("bad", [P, 1])
        any_order = sb("any_order", [P, 1], I32)
        out_part = sb("out_part", [P, NB])
        out_cnt = sb("out_cnt", [P, 2, NB])
        inv_cnt = sb("inv_cnt", [P, NB])
        last_share = sb("last_share", [P, NB])
        shift = sb("shift", [P, D])
        last_col = sb("last_col", [P, 1])
        last_clique = sb("last_clique", [P, P])
        clique_out = sb("clique_out", [P, D])
        wt = {n: sb("w_" + n, [P, A[n].shape[1]]) for n in
              ("W1T", "W2T", "WlT", "WrT", "WcT", "WinT", "Wmsg", "WihT", "WhhT", "WoutT")}
        bias = {n: sb("b_" + n, [A[n].shape[0], A[n].shape[1]]) for n in ("b12", "b_in_row")}
        b_gates = {n: sb("b_" + n, [P, 3]) for n in ("b_ih", "b_hh")}
        b_rz = sb("b_rz", [P, 2])
        b_in = sb("b_in", [P, 1])
        bcast = {n: sb("bc_" + n, [P, D]) for n in ("gn_weight", "gn_bias", "mean_scale", "bc", "bout", "bl")}
        N_CONST_LOADS = len(wt) + len(bias) + len(b_gates) + 2 + len(bcast)

        ps = ctx.enter_context(nc.psum_tensor("ps", [P, 8 * TILE], F32))
        pA, pB, pC, pD = (ps[:, n * 2 * TILE:(n + 1) * 2 * TILE] for n in range(4))
        p_cells = ps[:, 0:3 * TILE].rearrange("p (s n) -> p s n", s=3)
        p_flip = ps[:, 3 * TILE:3 * TILE + W]
        p_mix = ps[:, 5 * TILE:5 * TILE + W]
        p_win = ps[:, 7 * TILE:7 * TILE + WPS * WIN]


        def rows_of(t, i):
            return t[bass.ds(i * W, W), :].rearrange("(b p) d -> p b d", p=P)

        def steps_of(v, i):
            return v[:, bass.ds(i * W, W)]

        def flat(t):
            return t[:].rearrange("p b d -> p (b d)")

        def blocks(v):
            return v.rearrange("p (b d) -> p b d", d=D)

        LAYER_0, CLIQUES, LAYER_1, LAYER_3 = range(4)
        GEN = {LAYER_0: (rows_dram, True, False), CLIQUES: (A["x_clique"], False, True),
               LAYER_1: (rows_dram, False, True), LAYER_3: (rows_dram, False, False)}
        ROWS_FROM = {LAYER_0: 0, LAYER_1: 1, LAYER_3: 2}


        def both(f, g):
            def run():
                f()
                g()
            return run

        MM_CREDIT = 2 * NT

        def mm_base(l):
            return l * (NCH * NT + MM_CREDIT)

        CELL_RING = 3
        WIN_RING = WPS

        block = ctx.enter_context(nc.Block())

        def branch(eng, order, general, sorted_):
            with eng.If(order > 0):
                general()
            with eng.Else():
                sorted_()

        @block.sync
        def _(sp):
            sp.dma_start(dmax_i, A["dstT"][P - 1:P, :].to_broadcast([P, NCH])).then_inc(sem("ends_in"), 16)
            sp.dma_start(dmin_i, A["dstT"][0:1, :].to_broadcast([P, NCH])).then_inc(sem("ends_in"), 16)
            sp.dma_start(win_base[:], A["win_base_src"]).then_inc(sem("ends_in"), 16)
            sp.dma_start(dst_i, A["dstT"]).then_inc(sem("dst_in"), 16)
            sp.dma_start(next_i[0:P - 1, :], A["dstT"][1:P, :]).then_inc(sem("next_in"), 16)
            sp.dma_start(next_i[P - 1:P, 0:NCH - 1], A["dstT"][0:1, 1:NCH]).then_inc(sem("next_in"), 16)
            sp.dma_start(next_i[P - 1:P, NCH - 1:NCH], A["dstT"][P - 1:P, NCH - 1:NCH]).then_inc(sem("next_in"), 16)

            def slot(t, i):
                return blocks(steps_of(t, i % 2))

            def stage(s, source):
                x2, h2 = row_slots[s]
                new_x = s > 0
                sp.dma_start(slot(x2, 0), rows_of(source, 0)).then_inc(sem("x_in"), 16)

                def step(i, more):
                    sp.wait_ge(sem("x_seen"), i + 1 + s * NS)
                    sp.sem_inc(sem("sp_passed"), 1)
                    sp.wait_ge(sem("rows_out"), i * 16 + 16 + s * NS * 16)
                    if new_x:
                        sp.sem_inc(sem("sp_passed"), 1)
                        sp.wait_ge(sem("x_out"), i * 16 + 16 + (s - 1) * NS * 16)
                    if more:
                        sp.dma_start(slot(x2, i + 1), rows_of(source, i + 1)).then_inc(sem("x_in"), 16)
                    if new_x:
                        sp.wait_ge(sem("x_new"), i + 1 + (s - 1) * NS)
                        sp.dma_start(rows_of(x_dram, i), slot(x2, i)).then_inc(sem("x_out"), 16)
                    sp.wait_ge(sem("h_rows"), i + 1 + s * NS)
                    sp.dma_start(rows_of(rows_dram, i), slot(h2, i)).then_inc(sem("rows_out"), 16)

                with sp.Fori(0, NS - 1) as i:
                    step(i, True)
                step(NS - 1, False)
                sp.wait_ge(sem("rows_out"), (s + 1) * NS * 16 + 16)
                if new_x:
                    sp.wait_ge(sem("x_out"), s * NS * 16 + 16)
                sp.sem_inc(sem(f"rows_written{s}"), 1)

            sp.dma_start(src_i, A["srcT"]).then_inc(sem("edges_in"), 16)
            sp.dma_start(w_edge, A["wT"]).then_inc(sem("edges_in"), 16)
            for n, t in (*wt.items(), *bias.items(), *b_gates.items()):
                sp.dma_start(t[:], A[n]).then_inc(sem("consts_in"), 16)
            sp.dma_start(b_in[:], A["b_in"]).then_inc(sem("consts_in"), 16)
            sp.dma_start(last_col[:], A["last_clique"]).then_inc(sem("consts_in"), 16)
            for n, t in bcast.items():
                sp.dma_start(t[:], A[n].to_broadcast([P, D])).then_inc(sem("consts_in"), 16)
            sp.sem_inc(sem("rows_out"), 16)
            sp.sem_inc(sem("x_out"), 16)
            stage(0, A["x"])
            sp.wait_ge(sem("order_known"), 1)
            order = sp.value_load(any_order[0:1, 0:1], min_val=0, max_val=1)

            def edges_any(l):
                def f():
                    sp.wait_ge(sem(f"area_free{l}"), 1)
                    sp.wait_ge(sem("edges_in"), 32)
                    for t, n in ((g_src, "srcT"), (g_dst, "dstT"), (g_w, "wT")):
                        sp.dma_start(t, A[n]).then_inc(sem("g_edges"), 16)
                    if l == LAYER_1:
                        sp.wait_ge(sem("g_counted"), 1)
                        sp.dma_start(deg_dram[:, 0:NCOL], g_count[0:1, :]).then_inc(sem("deg_out"), 16)
                return f

            def load_cliques(b):
                sp.wait_ge(sem("xc_split"), b + 1)
                sp.sem_inc(sem("sp_passed"), 1)
                sp.dma_start(xc_in[0:HALF, :].rearrange("p (c d) -> p c d", c=2),
                             A["x_clique"][bass.ds(b * TD, TD), :].rearrange("(c p) d -> p c d", p=HALF)
                             ).then_inc(sem("xc_loaded"), 16)

            def store_piece(b, k, steps):
                sp.wait_ge(sem("stored"), b * (GS * SUBS) + (SUBS + steps) * GS + CELL_RING)
                cols = k * (SHS * TD)
                sp.dma_start(cells_dram[bass.ds(b, 1), :, cols:cols + SHS * TD].rearrange("o p n -> p (o n)"),
                             count_blk[:, bass.ds((b % 2) * BLK + cols, SHS * TD)]).then_inc(sem("cells_out"), 16)

            def store_block(b, paced):
                for k in range(SUBS):
                    store_piece(b, k, k if paced else 0)
                sp.wait_ge(sem("cells_out"), b * (16 * SUBS) + 16 * SUBS)
                sp.sem_inc(sem("block_saved"), 1)

            def count_sorted():
                sp.sem_inc(sem("block_saved"), 1)
                load_cliques(0)
                with sp.Fori(0, L2B - 1) as b:
                    load_cliques(b + 1)
                    store_block(b, True)
                with sp.Fori(L2B - 1, NBLK - 1) as b:
                    store_block(b, True)
                store_block(NBLK - 1, False)
                sp.wait_ge(sem("deg_counted"), 1)
                sp.dma_start(deg_dram.rearrange("o (g p j) -> p (o g) j", g=NGT, p=P),
                             deg_g[:, 0:NGT * G].rearrange("p (g j) -> p g j", j=G)).then_inc(
                    sem("deg_out"), 16)
                sp.dma_start(inv_deg_dram.rearrange("o (g p j) -> p (o g) j", g=NGT, p=P),
                             inv_deg_g[:, 0:NGT * G].rearrange("p (g j) -> p g j", j=G)).then_inc(sem("deg_out"), 16)
                sp.wait_ge(sem("deg_out"), 32)

            def load_pieces(l):
                before = 0 if l == 1 else 1

                def f():
                    if l == 1:
                        sp.wait_ge(sem("agg_done0"), 1)
                    else:
                        sp.wait_ge(sem("area_free3"), 1)
                    with sp.Fori(0, NBLK) as b:
                        if l == 1:
                            sp.wait_ge(sem("taken"), b + 1)
                            sp.dma_start(inv_deg_s[:, bass.ds((b % 2) * TD, TD)],
                                         inv_deg_dram[:, bass.ds(b * TD, TD)].to_broadcast([P, TD])).then_inc(sem("deg_in"), 16)
                        for k in range(SUBS):
                            sp.wait_ge(sem("piece_used"), b * SUBS + before * (NBLK + 1) * SUBS + k + 1)
                            if l == 1:
                                sp.sem_inc(sem("sp_passed"), 1)
                            if l == 1 and k < KD:
                                sp.wait_ge(sem("piece_counted"), b * KD + k + 1)
                            elif l == 1:
                                sp.wait_ge(sem("piece_counted_act"), b * (SUBS - KD) + k - KD + 1)
                            sp.dma_start(piece[:, k, :],
                                         cells_dram[bass.ds(b, 1), :, k * SHS * TD:(k + 1) * SHS * TD].rearrange(
                                             "o p n -> p (o n)")).then_inc(sem(f"piece{k}"), 16)
                return f

            branch(sp, order, edges_any(0), count_sorted)

            sp.wait_ge(sem("agg_done0"), 1)
            stage(1, A["x"])
            branch(sp, order, both(edges_any(CLIQUES), edges_any(LAYER_1)), load_pieces(1))
            sp.wait_ge(sem("agg_done1"), 1)
            stage(2, x_dram)
            branch(sp, order, edges_any(3), load_pieces(3))
            sp.dma_start(hs[:], rows_of(rows_dram, 0)).then_inc(sem("h_in4"), 16)
            sp.dma_start(xs2[:, 0:W].rearrange("p (b d) -> p b d", d=D), rows_of(x_dram, 0)).then_inc(sem("x_in4"), 16)
            sp.wait_ge(sem("agg_done3"), 1)
            sp.dma_start(deg_row[0:1, :], deg_dram[:, 0:NPAD]).then_inc(sem("deg_row_in"), 16)

            def store_y(i):
                sp.wait_ge(sem("y_ready"), i + 2)
                sp.dma_start(rows_of(out, i), xs2[:, bass.ds((i % 2) * W, W)].rearrange("p (b d) -> p b d", d=D)
                             ).then_inc(sem("y_out"), 16)

            sp.sem_inc(sem("y_out"), 16)
            with sp.Fori(0, NS - 1) as i:
                sp.wait_ge(sem("hT4"), i + 1)
                sp.dma_start(hs[:], rows_of(rows_dram, i + 1)).then_inc(sem("h_in4"), 16)
                sp.wait_ge(sem("y_out"), i * 16 + 16)
                sp.sem_inc(sem("sp_passed"), 1)
                sp.wait_ge(sem("x_biased"), i + 1)
                sp.dma_start(xs2[:, bass.ds(((i + 1) % 2) * W, W)].rearrange("p (b d) -> p b d", d=D),
                             rows_of(x_dram, i + 1)).then_inc(sem("x_in4"), 16)
                store_y(i)
            store_y(NS - 1)
            sp.wait_ge(sem("y_out"), 16 * NS + 16)

        @block.gpsimd
        def _(pool):
            nc.gpsimd.iota(iota_i[:], pattern=[[1, CELLS]], base=0, channel_multiplier=0).then_inc(sem("made"), 1)
            nc.gpsimd.iota(tile_off_i[:], pattern=[[-TILE, NT]], base=0, channel_multiplier=0).then_inc(sem("made"), 1)
            nc.gpsimd.iota(gbase_i[:], pattern=[[G * P, NGT]], base=0, channel_multiplier=G).then_inc(sem("made"), 1)
            nc.gpsimd.memset(ident[:], 0.0)
            nc.gpsimd.memset(ones16[:], 1.0)
            nc.gpsimd.memset(ones[:], 1.0).then_inc(sem("made"), 1)
            pool.drain()
            nc.gpsimd.affine_select(out=ident[:], in_=ident[:], compare_op=ALU.not_equal, fill=1.0, base=0,
                                    pattern=[[-1, P]], channel_multiplier=1).then_inc(sem("made"), 1)
            for g in range(NGT):
                pool.wait_ge(sem("chunk_known"), g + 1)
                pool.indirect_dma_start(
                    out=chunk_dst_i[:, g, :], out_offset=None, in_=A["dst_rows"],
                    in_offset=bass.IndirectOffsetOnAxis(ap=chunk_idx[:, g:g + 1], axis=0),
                ).then_inc(sem("chunk_rows"), 16)
            pool.wait_ge(sem("edge_known"), 1)
            group_src_rows = group_src_i.rearrange("p (g e) -> p g e", g=NGT)
            for rows, table, got in ((group_dst_i, "dst_flat", "group_dst"), (group_src_rows, "src_flat", "group_src")):
                for g in range(NGT):
                    pool.indirect_dma_start(
                        out=rows[:, g, :], out_offset=None, in_=A[table],
                        in_offset=bass.IndirectOffsetOnAxis(ap=edge_idx[:, g:g + 1], axis=1),
                    ).then_inc(sem(got), 16)
            pool.wait_ge(sem("order_known"), 1)
            order = pool.value_load(any_order[0:1, 0:1], min_val=0, max_val=1)

            def gather_windows(t):
                for w in range(WPS):
                    pool.wait_ge(sem("indices_ready"), t * WPS + w + 1)
                    pool.sem_inc(sem("win_slot_taken"), 1)
                    for k in range(w * WCH, (w + 1) * WCH):
                        pool.indirect_dma_start(
                            out=gathered[:, k, :], out_offset=None, in_=rows_dram,
                            in_offset=bass.IndirectOffsetOnAxis(ap=idx_slot[:, k:k + 1], axis=0),
                        ).then_inc(sem(f"win_row{k}"), 16)

            def windows_sorted():
                pool.wait_ge(sem("edges_in"), 32)
                pool.wait_ge(sem("rows_written0"), 1)
                with pool.Fori(0, STEPS + TAIL) as t:
                    gather_windows(t)

            def gather_any(l):
                def f():
                    table = GEN[l][0]
                    index = g_idx if l == CLIQUES else g_src
                    if l in ROWS_FROM:
                        pool.wait_ge(sem(f"rows_written{ROWS_FROM[l]}"), 1)
                    pool.wait_ge(sem("g_ready"), l + 1)
                    with pool.Fori(0, NCH // 2) as j:
                        pool.wait_ge(sem("g_mm"), j * (2 * NT) + mm_base(l) + 2 * NT)
                        pool.sem_inc(sem("g_slots_taken"), 1)
                        nc.gpsimd.tensor_copy(chunk_slot[:], index[:, bass.ds(j * 2, 2)])
                        pool.drain()
                        for k in range(2):
                            pool.indirect_dma_start(
                                out=g_rows[:, k, :], out_offset=None, in_=table,
                                in_offset=bass.IndirectOffsetOnAxis(ap=chunk_slot[:, k:k + 1], axis=0),
                            ).then_inc(sem(f"g_row{k}"), 16)
                return f

            def idle():
                pool.sem_inc(sem("idle"), 1)

            def load_rows(name, used):
                pool.dma_start(hs[:], rows_of(rows_dram, 0)).then_inc(sem(name), 16)
                with pool.Fori(0, NS - 1) as i:
                    pool.wait_ge(sem(used), i + 1)
                    pool.sem_inc(sem("rows_used"), 1)
                    pool.dma_start(hs[:], rows_of(rows_dram, i + 1)).then_inc(sem(name), 16)
                pool.wait_ge(sem(used), NS)

            branch(pool, order, gather_any(0), windows_sorted)
            pool.wait_ge(sem("rows_written0"), 1)
            load_rows("h_in1", "hT1")
            branch(pool, order, both(gather_any(CLIQUES), gather_any(LAYER_1)), idle)
            pool.wait_ge(sem("rows_written1"), 1)
            load_rows("h_in2a", "hT2")
            over_rows = (lambda t: t[:].rearrange("p (o d) -> p o d", o=1).to_broadcast([P, SB, D]))
            norm = blocks(z_s)
            pool.dma_start(hs[:], rows_of(rows_dram, 0)).then_inc(sem("h_in2"), 16)
            pool.wait_ge(sem("gain_ready"), 1)

            def normalise(i):
                pool.wait_ge(sem("x_new"), i + NS)
                pool.sem_inc(sem("norm_begun"), 1)
                nc.gpsimd.tensor_tensor(norm, f_all[:, bass.ds(i * SB, SB), :], over_rows(gain), ALU.mult)
                pool.drain()
                nc.gpsimd.tensor_tensor(norm, norm, over_rows(shift), ALU.add)
                pool.drain()
                pool.wait_ge(sem("h_in2"), i * 16 + 16)
                nc.gpsimd.tensor_tensor(norm, norm, hs[:], ALU.add).then_inc(sem("norm_rows"), 1)

            with pool.Fori(0, NS - 1) as i:
                normalise(i)
                pool.wait_ge(sem("norm_rows"), i + 1)
                pool.sem_inc(sem("rows_used"), 1)
                pool.dma_start(hs[:], rows_of(rows_dram, i + 1)).then_inc(sem("h_in2"), 16)
            normalise(NS - 1)
            branch(pool, order, gather_any(3), idle)
            with pool.Fori(0, NS) as i:
                pool.wait_ge(sem("x_in4"), i * 16 + 16)
                rows = blocks(xs2[:, bass.ds((i % 2) * W, W)])
                nc.gpsimd.tensor_tensor(rows, rows, bcast["bout"][:].rearrange("p (o d) -> p o d", o=1).to_broadcast(
                    [P, SB, D]), ALU.add).then_inc(sem("x_biased"), 1)

        @block.tensor
        def _(pe):
            mm = nc.tensor.matmul
            pe.wait_ge(sem("made"), 5)
            for name, source, done in (("sources_made", key_a, "sources_flipped"), ("keys_made", key_c, "keys_flipped")):
                pe.wait_ge(sem(name), 1)
                for n in range(K * NGT):
                    last = nc.tensor.transpose(ps[:, n * P:(n + 1) * P], source[:, n * P:(n + 1) * P], ident[:])
                last.then_inc(sem(done), 1)
                if source is key_a:
                    pe.wait_ge(sem("slT_ready"), 1)
            pe.wait_ge(sem("keyT_ready"), 1)
            mm(ps[:, 0:1], ones[:], bad[:], start=True, stop=True).then_inc(sem("bad_summed"), 1)
            pe.wait_ge(sem("consts_in"), 16 * N_CONST_LOADS)
            pe.wait_ge(sem("order_known"), 1)
            order = pe.value_load(any_order[0:1, 0:1], min_val=0, max_val=1)

            def sum_any(l):
                counted = GEN[l][2]

                def f():
                    if l == LAYER_1:
                        pe.wait_ge(sem("area_free2"), 1)
                    pe.sem_inc(sem("g_mm"), MM_CREDIT)
                    with pe.Fori(0, NCH // 2) as j:
                        for k in range(2):
                            pe.wait_ge(sem(f"g_row{k}"), j * 16 + (l * (NCH // 2) + 1) * 16)
                            for t in range(NT):
                                n = k * NT + t
                                cols = slice((n % 2) * TILE, (n % 2 + 1) * TILE)
                                pe.wait_ge(sem("g_onehot"), j * (2 * NT) + l * NCH * NT + n + 1)
                                pe.wait_ge(sem("g_added"), j * (2 * NT) + l * (NCH * NT + 2) + n + 1)
                                last = mm(pA[:, cols], g_rows[:, k, :], g_onehot[:, n % 2, :], start=True, stop=True)
                                if counted:
                                    last = mm(pB[:, cols], ones[:], g_onehot[:, n % 2, :], start=True, stop=True)
                                last.then_inc(sem("g_mm"), 1)
                return f

            def count_group(t, g):
                pe.wait_ge(sem("onehots"), t * GS + g + 1)
                pe.wait_ge(sem("stored"), t * GS + g + 1)
                for k in range(K):
                    s = (g % 3) * K + k
                    last = mm(p_cells[:, g % 3, 0:CELLS], oh_src[:, s, :], oh_cell[:, s, :],
                              start=(k == 0), stop=(k == K - 1))
                last.then_inc(sem("cells"), 1)

            def flip(b, sub, c):
                pe.wait_ge(sem("flip_copied"), b * (2 * SUBS) + sub * 2 + c + 1)
                if c == 0:
                    pe.wait_ge(sem("stored"), b * (GS * SUBS) + GS * SUBS + CELL_RING)
                for j in range(SHS):
                    last = mm(p_flip[0:HALF, j * P:(j + 1) * P],
                              count_blk[:, bass.ds((b % 2) * BLK + (sub * SHS + j) * TD + c * HALF, HALF)],
                              ident16[:], start=True, stop=True)
                last.then_inc(sem("flips"), 1)

            def mix(b, sub, c):
                pe.wait_ge(sem("flip_copied"), b * (2 * SUBS) + sub * 2 + c + 2)
                if c == 0:
                    pe.wait_ge(sem("xc_split"), b + 2)
                    pe.wait_ge(sem("mix_added"), b * SUBS + sub + 1)
                for lo, n in ((0, TILE), (TILE, W - TILE)):
                    for l in range(3):
                        plane = xc_plane[0:HALF, bass.ds(b % 2, 1), c, l, :].rearrange("p s n -> p (s n)")
                        last = mm(p_mix[:, lo:lo + n], plane, flipped_s[0:HALF, lo:lo + n],
                                  start=(c == 0 and l == 0), stop=(c == 1 and l == 2))
                last.then_inc(sem("mixed"), 1)

            def window(t, w):
                if w == 0:
                    pe.wait_ge(sem("win_copied"), t + 1)
                pe.wait_ge(sem("win_onehots"), t * WPS + w + 1)
                for k in range(WCH):
                    s = w * WCH + k
                    pe.wait_ge(sem(f"win_row{s}"), t * 16 + 16)
                    last = mm(p_win[:, w * WIN:(w + 1) * WIN], gathered[:, s, :], oh_win[:, s, :],
                              start=(k == 0), stop=(k == WCH - 1))
                last.then_inc(sem("win_mm"), 1)

            def step(blk, sub, clique):
                t = blk * SUBS + sub
                b = blk - 1
                count_group(t, 0)
                if clique:
                    flip(b, sub, 0)
                count_group(t, 1)
                window(t, 0)
                count_group(t, 2)
                if clique:
                    mix(b, sub, 0)
                    flip(b, sub, 1)
                count_group(t, 3)
                window(t, 1)
                count_group(t, 4)
                if clique:
                    mix(b, sub, 1)
                count_group(t, 5)
                window(t, 2)

            def count_sorted():
                pe.sem_inc(sem("cells"), CELL_RING)
                pe.sem_inc(sem("win_mm"), WIN_RING)
                pe.sem_inc(sem("flips"), 2 * SUBS)
                pe.sem_inc(sem("mixed"), 1)
                with pe.Fori(0, SUBS) as sub:
                    step(0, sub, False)
                with pe.Fori(1, L2B + 1) as blk:
                    with pe.Fori(0, SUBS) as sub:
                        step(blk, sub, True)
                with pe.Fori(L2B + 1, NBLK) as blk:
                    with pe.Fori(0, SUBS) as sub:
                        step(blk, sub, False)
                with pe.Fori(STEPS, STEPS + TAIL) as t:
                    for w in range(WPS):
                        window(t, w)

            def multiply(l):
                def f():
                    before = 0 if l == 1 else 1
                    pe.sem_inc(sem("piece_used"), SUBS)
                    pe.wait_ge(sem(f"planes_ready{l}"), NS)
                    with pe.Fori(0, NBLK) as b:
                        slot = (b % 2) * (2 * TILE)
                        pe.wait_ge(sem("taken"), b + before * (NBLK + 2) + 1)
                        for k in range(SUBS):
                            pe.wait_ge(sem(f"piece{k}"), b * 16 + before * NBLK * 16 + 16)
                            for j in range(SHS):
                                sh = k * SHS + j
                                cells = piece[:, k, j * TD:(j + 1) * TD]
                                for p in range(2):
                                    last = mm(ps[:, bass.ds(slot, TD)], planes[:, p, sh, :], cells,
                                              start=(sh == 0 and p == 0), stop=(sh == NB - 1 and p == 1))
                            last.then_inc(sem("piece_used"), 1)
                return f

            def transposes(dst_ps, source):
                for b in range(SB):
                    last = nc.tensor.transpose(dst_ps[:, b * P:(b + 1) * P], source[:, b * P:(b + 1) * P], ident[:])
                return last

            def product(dst_ps, terms):
                for b in range(SB):
                    for n, (lhs, rhs) in enumerate(terms):
                        k = rhs.shape[0]
                        lhsT = lhs[:, b * P:(b + 1) * P] if k == P else lhs[0:k, :]
                        last = mm(dst_ps[:, b * D:(b + 1) * D], lhsT, rhs, start=(n == 0), stop=(n == len(terms) - 1))
                return last

            def column_sums(source, i, first, last_step):
                for b in range(SB):
                    k = LAST if last_step and b == SB - 1 else P
                    last = mm(pC[:, 0:D], ones[0:k, :], source[0:k, bass.ds(i * SB + b, 1), :].rearrange(
                        "p b d -> p (b d)"), start=first and b == 0, stop=last_step and b == SB - 1)
                return last

            def summed(source, name, inc):
                def f(i, first=False, last_step=False):
                    pe.wait_ge(sem(name), i + 1)
                    last = column_sums(source, i, first, last_step)
                    if last_step:
                        last.then_inc(sem(inc), 1)
                return f

            branch(pe, order, sum_any(0), count_sorted)

            def lin1(i):
                pe.wait_ge(sem("prod1"), i + 1)
                pe.wait_ge(sem("lin1_read"), i + 1)
                product(pB, [(agg_s, wt["W1T"][:]), (prod_s, wt["W2T"][:]), (ones, bias["b12"][:])]).then_inc(
                    sem("lin1"), 1)

            def rows_T(s, name, i):
                pe.wait_ge(sem(name), i * 16 + 16)
                transposes(pA, flat(hs)).then_inc(sem(f"hT{s}"), 1)

            pe.wait_ge(sem("agg_done0"), 1)
            pe.sem_inc(sem("lin1_read"), 1)
            rows_T(1, "h_in1", 0)
            with pe.Fori(0, NS - 1) as i:
                lin1(i)
                rows_T(1, "h_in1", i + 1)
            lin1(NS - 1)
            pe.wait_ge(sem("x_new"), NS)
            branch(pe, order, both(sum_any(CLIQUES), sum_any(LAYER_1)), multiply(1))

            def lin2(i):
                pe.wait_ge(sem("agg_staged2"), i + 1)
                pe.wait_ge(sem("hT_s2"), i + 1)
                pe.wait_ge(sem("biased"), i + 1)
                product(pB, [(agg_s, wt["WlT"][:]), (hT_s, wt["WrT"][:])]).then_inc(sem("lin2"), 1)

            pe.sem_inc(sem("biased"), 1)
            pe.wait_ge(sem("agg_done1"), 1)
            rows_T(2, "h_in2a", 0)

            def layer_1(i):
                pe.wait_ge(sem("hT_s2"), i + 1)
                rows_T(2, "h_in2a", i + 1)
                lin2(i)

            mean_sums = summed(f_all, "gelu", "mean_sum")
            layer_1(0)
            layer_1(1)
            mean_sums(0, first=True)
            with pe.Fori(2, NS - 1) as i:
                layer_1(i)
                mean_sums(i - 1)
            lin2(NS - 1)
            mean_sums(NS - 2)
            mean_sums(NS - 1, last_step=True)
            square_sums = summed(sq_all, "squared", "var_sum")
            square_sums(0, first=True)
            with pe.Fori(1, NS - 1) as i:
                square_sums(i)
            square_sums(NS - 1, last_step=True)

            mm(pA[:, 0:D], last_clique[:], wt["WcT"][:], start=True, stop=True).then_inc(sem("clique_lin"), 1)
            pe.sem_inc(sem("lin3"), 1)
            with pe.Fori(0, NS) as i:
                pe.wait_ge(sem("agg_staged3"), i + 1)
                pe.wait_ge(sem("x_new"), i + NS)
                product(pB, [(agg_s, wt["WcT"][:])]).then_inc(sem("lin3"), 1)
            pe.wait_ge(sem("x_new"), 2 * NS)
            branch(pe, order, sum_any(3), multiply(3))

            def wide(dst_ps, terms):
                for lo, hi in ((0, TILE), (TILE, W)):
                    for n, (lhs, rhs) in enumerate(terms):
                        last = mm(dst_ps[:, lo:hi], lhs, rhs(lo, hi - lo), start=(n == 0), stop=(n == len(terms) - 1))
                return last

            def step_view(v, i, rows=slice(0, P)):
                return lambda lo, n: v[rows, bass.ds(i * W + lo, n)]

            def fixed_view(v):
                return lambda lo, n: v[:, lo:lo + n]

            def hidden(i):
                pe.wait_ge(sem("h_in4"), i * 16 + 16)
                pe.wait_ge(sem("r_ready"), i + 1)
                transposes(pA, flat(hs)).then_inc(sem("hT4"), 1)
                pe.wait_ge(sem("hT_s4"), i + 1)
                pe.wait_ge(sem("z_ready"), i + 1)
                wide(pB, [(wt["WinT"][:], fixed_view(hT_s))]).then_inc(sem("hidden"), 1)
                pe.wait_ge(sem("n_in"), i + 1)
                wide(pC, [(wt["WinT"][:], step_view(agg, i)),
                          (bias["b_in_row"][:], step_view(deg_row, i, slice(0, 1)))]).then_inc(sem("hid_sum"), 1)

            def messages(i):
                pe.wait_ge(sem("hid_sum_s"), i + 1)
                wide(pD, [(wt["Wmsg"][:], fixed_view(ah_s))]).then_inc(sem("msg_sum"), 1)

            def gates(i):
                ih, hh = wt["WihT"], wt["WhhT"]
                pe.wait_ge(sem("hidden_s"), i + 1)
                pe.wait_ge(sem("y_ready"), i + 1)
                msg, hid = fixed_view(am_s), step_view(hid2, i % 2)
                halves = ((0, TILE), (TILE, W))
                for lo, hi in halves:
                    mm(pA[:, lo:hi], hh[:, 0:D], hid(lo, hi - lo), start=True, stop=False)
                pe.wait_ge(sem("msg_sum_s"), i + 1)
                for lo, hi in halves:
                    last = mm(pA[:, lo:hi], ih[:, 0:D], msg(lo, hi - lo), start=False, stop=True)
                last.then_inc(sem("r_gate"), 1)
                wide(pB, [(ih[:, D:2 * D], msg), (hh[:, D:2 * D], hid)]).then_inc(sem("z_gate"), 1)
                wide(pC, [(ih[:, 2 * D:], msg)])
                wide(pD, [(hh[:, 2 * D:], hid)]).then_inc(sem("n_gate"), 1)

            def output(i):
                pe.wait_ge(sem("h_new"), i + 1)
                product(pA, [(newT_s, wt["WoutT"][:])]).then_inc(sem("out_rows"), 1)

            pe.wait_ge(sem("agg_done3"), 1)
            pe.wait_ge(sem("deg_row_in"), 16)
            for name in ("r_ready", "z_ready", "n_in", "y_ready"):
                pe.sem_inc(sem(name), 1)
            hidden(0)
            messages(0)
            with pe.Fori(0, NS - 1) as i:
                gates(i)
                hidden(i + 1)
                output(i)
                messages(i + 1)
            gates(NS - 1)
            pe.wait_ge(sem("r_ready"), NS + 1)
            output(NS - 1)

        @block.scalar
        def _(act):
            def ln_std(s, i):
                act.wait_ge(sem("ln_var"), i + 1 + s * NS)
                nc.scalar.activation(rstd[:], rstd[:], ACT.Sqrt).then_inc(sem("ln_std"), 1)

            def stage_agg(s, i):
                nc.scalar.copy(agg_s[:], agg[:, bass.ds(i * W, W)]).then_inc(sem(f"agg_staged{s}"), 1)

            with act.Fori(0, NS) as i:
                ln_std(0, i)
            act.wait_ge(sem("sources_flipped"), 1)
            nc.scalar.copy(slT.rearrange("p k (g e) -> p k g e", g=NGT),
                           ps[:, 0:NKEY].rearrange("p (g k e) -> p k g e", g=NGT, k=K)).then_inc(sem("slT_ready"), 1)
            act.wait_ge(sem("order_known"), 1)
            order = act.value_load(any_order[0:1, 0:1], min_val=0, max_val=1)

            def store_group(blk, sub, g):
                act.wait_ge(sem("cells"), (blk * SUBS + sub) * GS + g + 1 + CELL_RING)
                cells = count_blk[:, bass.ds((blk % 2) * BLK, BLK)].rearrange("p (s d) -> p s d", d=TD)
                nc.scalar.copy(cells[:, :, bass.ds((sub * GS + g) * G, G)],
                               p_cells[:, g % 3, 0:CELLS].rearrange("p (s d) -> p s d", d=G)).then_inc(
                    sem("stored"), 1)

            def copy_flip(b, sub, c):
                act.wait_ge(sem("flips"), b * (2 * SUBS) + sub * 2 + c + 1 + 2 * SUBS)
                act.wait_ge(sem("mixed"), b * (2 * SUBS) + sub * 2 + c + 1)
                nc.scalar.copy(flipped_s[0:HALF, :], p_flip[0:HALF, :]).then_inc(sem("flip_copied"), 1)

            def copy_indices(t, w):
                act.wait_ge(sem("win_mm"), t * WPS + w + 1)
                nc.scalar.copy(idx_slot[:, w * WCH:(w + 1) * WCH],
                               src_i[:, bass.ds(t * CPS + w * WCH, WCH)]).then_inc(sem("indices_ready"), 1)

            def copy_window(t):
                act.wait_ge(sem("win_mm"), t * WPS + WIN_RING)
                act.sem_inc(sem("act_passed"), 1)
                act.wait_ge(sem("win_added"), t + 1)
                nc.scalar.copy(win_sum[:], p_win).then_inc(sem("win_copied"), 1)

            def step(blk, sub, clique):
                t = blk * SUBS + sub
                for g in range(GS):
                    store_group(blk, sub, g)
                    if g == 0:
                        copy_window(t)
                    if clique and g == 1:
                        copy_flip(blk - 1, sub, 0)
                    if clique and g == 3:
                        copy_flip(blk - 1, sub, 1)
                    if g % 2:
                        copy_indices(t + 1, g // 2)

            def slot_free(blk, flips):
                act.wait_ge(sem("flips"), flips)
                act.wait_ge(sem("block_saved"), blk)
                act.sem_inc(sem("block_begun"), 1)

            def count_sorted():
                act.sem_inc(sem("stored"), CELL_RING)
                act.sem_inc(sem("flip_copied"), 1)
                act.wait_ge(sem("edges_in"), 32)
                for w in range(WPS):
                    copy_indices(0, w)
                with act.Fori(0, SUBS) as sub:
                    step(0, sub, False)
                with act.Fori(1, L2B + 1) as blk:
                    slot_free(blk, blk * (2 * SUBS))
                    with act.Fori(0, SUBS) as sub:
                        step(blk, sub, True)
                with act.Fori(L2B + 1, NBLK) as blk:
                    slot_free(blk, (L2B + 1) * 2 * SUBS)
                    with act.Fori(0, SUBS) as sub:
                        step(blk, sub, False)
                with act.Fori(STEPS, STEPS + TAIL - 1) as t:
                    copy_window(t)
                    for w in range(WPS):
                        copy_indices(t + 1, w)
                copy_window(STEPS + TAIL - 1)
                copy_window(STEPS + TAIL)

            def idle():
                act.sem_inc(sem("idle"), 1)

            def count_pieces():
                act.sem_inc(sem("piece_counted_act"), SUBS - KD)
                act.sem_inc(sem("part_added"), 1)
                with act.Fori(0, NBLK) as b:
                    act.wait_ge(sem("part_added"), b + 1)
                    for k in range(KD, SUBS):
                        act.wait_ge(sem(f"piece{k}"), b * 16 + 16)
                        for j in range(SHS):
                            last = nc.scalar.activation(unused[:, j * TD:(j + 1) * TD], piece[:, k, j * TD:(j + 1) * TD], ACT.Copy,
                                                        accum_out=out_part[:, k * SHS + j:k * SHS + j + 1])
                        last.then_inc(sem("piece_counted_act"), 1)
                        act.drain()

            branch(act, order, idle, count_sorted)
            act.wait_ge(sem("agg_done0"), 1)

            def slope(i):
                act.wait_ge(sem("lin1_read"), i + 1)
                nc.scalar.activation(z_s, pB[:, 0:W], ACT.Copy, scale=SLOPE).then_inc(sem("sloped"), 1)

            stage_agg(1, 0)
            with act.Fori(0, NS - 1) as i:
                act.wait_ge(sem("lin1"), i + 1)
                stage_agg(1, i + 1)
                slope(i)
                ln_std(1, i)
            act.wait_ge(sem("lin1"), NS)
            slope(NS - 1)
            ln_std(1, NS - 1)
            branch(act, order, idle, count_pieces)

            def gelu(i):
                act.wait_ge(sem("biased"), i + 2)
                nc.scalar.activation(f_all[:, bass.ds(i * SB, SB), :], blocks(r_s), ACT.Gelu).then_inc(sem("gelu"), 1)

            act.wait_ge(sem("agg_done1"), 1)
            stage_agg(2, 0)
            with act.Fori(0, NS - 1) as i:
                act.wait_ge(sem("lin2"), i + 1)
                stage_agg(2, i + 1)
                gelu(i)
            gelu(NS - 1)
            with act.Fori(0, NS) as i:
                act.wait_ge(sem("centred"), i + 1)
                nc.scalar.activation(sq_all[:, bass.ds(i * SB, SB), :], f_all[:, bass.ds(i * SB, SB), :],
                                     ACT.Square).then_inc(sem("squared"), 1)
            act.wait_ge(sem("var_ready"), 1)
            nc.scalar.activation(gain[:], gain[:], ACT.Sqrt).then_inc(sem("std_ready"), 1)

            def stage_cliques(i):
                act.wait_ge(sem("lin3"), i + 1)
                nc.scalar.copy(agg_s[:], steps_of(clique_sum, i)).then_inc(sem("agg_staged3"), 1)
                act.wait_ge(sem("x_new"), i + NS)
                act.sem_inc(sem("act_passed"), 1)
                for b in range(SB):
                    last = nc.scalar.activation(r_s[:, b * D:(b + 1) * D], clique_out[:], ACT.Copy,
                                                scale=last_share[:, bass.ds(i * SB + b, 1)])
                last.then_inc(sem("beyond"), 1)

            act.wait_ge(sem("gain_ready"), 1)
            stage_cliques(0)
            with act.Fori(0, NS - 1) as i:
                stage_cliques(i + 1)
                ln_std(2, i)
            ln_std(2, NS - 1)
            act.wait_ge(sem("agg_done3"), 1)
            act.wait_ge(sem("b_rz_ready"), 1)
            b_in_gate = b_gates["b_ih"][:, 2:3]

            def copy_rows(i):
                act.wait_ge(sem("hT4"), i + 1)
                nc.scalar.copy(hT_s[:], pA[:, 0:W]).then_inc(sem("hT_s4"), 1)

            def copy_messages(i):
                act.wait_ge(sem("hidden"), i + 1)
                nc.scalar.activation(steps_of(hid2, i % 2), pB[:, 0:W], ACT.Identity, bias=b_in[:]).then_inc(
                    sem("hidden_s"), 1)
                act.wait_ge(sem("hid_sum"), i + 1)
                nc.scalar.copy(ah_s, pC[:, 0:W]).then_inc(sem("hid_sum_s"), 1)
                act.wait_ge(sem("msg_sum"), i + 1)
                nc.scalar.copy(am_s, pD[:, 0:W]).then_inc(sem("msg_sum_s"), 1)

            def sigmoids(i):
                act.wait_ge(sem("r_gate"), i + 1)
                nc.scalar.activation(r_s, pA[:, 0:W], ACT.Sigmoid, bias=b_rz[:, 0:1]).then_inc(sem("r_ready"), 1)
                act.wait_ge(sem("z_gate"), i + 1)
                nc.scalar.activation(z_s, pB[:, 0:W], ACT.Sigmoid, bias=b_rz[:, 1:2]).then_inc(sem("z_ready"), 1)

            def tanh(i):
                act.wait_ge(sem("n_in"), i + 2)
                nc.scalar.activation(n_s, t_s, ACT.Tanh, bias=b_in_gate).then_inc(sem("tanh"), 1)

            copy_rows(0)
            copy_messages(0)
            with act.Fori(0, NS - 1) as i:
                sigmoids(i)
                copy_rows(i + 1)
                tanh(i)
                copy_messages(i + 1)
            sigmoids(NS - 1)
            tanh(NS - 1)

        @block.vector
        def _(dve):
            V = nc.vector
            dve.wait_ge(sem("made"), 5)
            V.tensor_copy(iota16[:], iota_i[:])
            V.tensor_copy(iota_win[:], iota_i[:, 0:WIN])
            V.tensor_copy(tile_off[:], tile_off_i[:])
            V.tensor_copy(ident16[:], ident[:])
            V.tensor_copy(gbase[:], gbase_i[:])
            dve.drain()
            V.tensor_scalar(glast[:], gbase[:], float(G - 1), float(N_NODES - 1), ALU.add, ALU.min)
            dve.wait_ge(sem("ends_in"), 48)
            V.tensor_copy(dmax_f, dmax_i)
            V.tensor_copy(dmin_f, dmin_i)
            dve.drain()
            for g in range(NGT):
                V.tensor_scalar(scr, dmax_f, gbase[:, g:g + 1], None, ALU.is_lt, ALU.add,
                                accum_out=first_chunk[:, g:g + 1])
                dve.drain()
                V.tensor_scalar(first_chunk[:, g:g + 1], first_chunk[:, g:g + 1], float(NCH - 1), None, ALU.min)
                dve.drain()
                V.tensor_copy(chunk_idx[:, g:g + 1], first_chunk[:, g:g + 1]).then_inc(sem("chunk_known"), 1)
            dve.wait_ge(sem("chunk_rows"), 16 * NGT)
            V.tensor_copy(chunk_dst, chunk_dst_i)
            dve.drain()
            V.tensor_tensor(chunk_dst, chunk_dst, gbase[:].rearrange("p (g o) -> p g o", o=1).to_broadcast(
                [P, NGT, P]), ALU.is_lt)
            dve.drain()
            V.tensor_reduce(in_chunk[:], chunk_dst, AX_X, ALU.add)
            dve.drain()
            V.scalar_tensor_tensor(out=in_chunk[:], in0=first_chunk[:], scalar=float(P), in1=in_chunk[:],
                                   op0=ALU.mult, op1=ALU.add)
            dve.drain()
            V.tensor_scalar(edge_idx[:], in_chunk[:], float(NCH * P - GE - 1), None, ALU.min).then_inc(
                sem("edge_known"), 1)
            spans = scr[:, 0:NCH // WCH]
            firsts = dmin_f.rearrange("p (n c) -> p n c", c=WCH)[:, :, 0]
            lasts = dmax_f.rearrange("p (n c) -> p n c", c=WCH)[:, :, WCH - 1]
            V.tensor_tensor(spans, lasts, firsts, ALU.subtract)
            dve.drain()
            V.tensor_scalar(spans, spans, float(WIN - 1), None, ALU.is_gt)
            dve.drain()
            V.tensor_reduce(bad3[:, 1:2], spans, AX_X, ALU.add)
            dve.wait_ge(sem("dst_in"), 16)
            V.tensor_copy(rel, dst_i)
            dve.drain()
            dve.wait_ge(sem("next_in"), 48)
            V.tensor_copy(scr, next_i)
            dve.drain()
            V.tensor_tensor(scr, rel, scr, ALU.is_gt)
            dve.drain()
            V.tensor_reduce(bad3[:, 2:3], scr, AX_X, ALU.add)
            V.tensor_tensor(rel.rearrange("p (n c) -> p n c", c=WCH), rel.rearrange("p (n c) -> p n c", c=WCH),
                            dmin_f.rearrange("p (n c) -> p n c", c=WCH)[:, :, 0:1].to_broadcast(
                                [P, NCH // WCH, WCH]), ALU.subtract)
            dve.drain()

            def slot(t, i):
                return blocks(steps_of(t, i % 2))

            def rows_seen(s, i):
                dve.wait_ge(sem("x_in"), i * 16 + 16 + s * NS * 16)
                dve.sem_inc(sem("x_seen"), 1)

            def layernorm(s, i, split=None):
                x, h = (slot(t, i) for t in row_slots[s])
                for b in range(SB):
                    V.bn_stats(stats[:, b, :], x[:, b, :])
                dve.drain()
                for b in range(SB):
                    V.bn_aggr(mv[:, b, :], stats[:, b, :])
                dve.drain()
                V.tensor_scalar(rstd[:], mv[:, :, 1], EPS, None, ALU.add).then_inc(sem("ln_var"), 1)
                dve.wait_ge(sem("ln_std"), i + 1 + s * NS)
                V.reciprocal(rstd[:], rstd[:])
                dve.drain()
                for b in range(SB):
                    V.tensor_scalar(hT_s[:, b * P:(b + 1) * P], x[:, b, :], mv[:, b, 0:1], rstd[:, b:b + 1],
                                    ALU.subtract, ALU.mult)
                dve.drain()
                V.tensor_scalar(h, blocks(hT_s[:]), 0.0, None, ALU.max).then_inc(sem("h_rows"), 1)
                if split is not None:
                    part = [planes[:, n, bass.ds(i * SB, SB), :] for n in range(2)]
                    V.tensor_scalar(part[0], blocks(hT_s[:]), 0.0, SCALE, ALU.max, ALU.mult)
                    dve.drain()
                    V.scalar_tensor_tensor(out=part[1], in0=h, scalar=SCALE, in1=part[0], op0=ALU.mult,
                                           op1=ALU.subtract).then_inc(sem(f"planes_ready{split}"), 1)
                dve.drain()

            with dve.Fori(0, NS) as i:
                rows_seen(0, i)
                layernorm(0, i)

            by_group = (lambda v: v.rearrange("p (g e) -> p g e", g=NGT))
            dve.wait_ge(sem("group_dst"), 16 * NGT)
            V.tensor_copy(past_group[:], group_dst_i[:, :, GE])
            V.tensor_copy(by_group(key_b), group_dst_i[:, :, 0:GE])
            dve.drain()
            V.tensor_tensor(past_group[:], past_group[:], glast[:], ALU.is_le)
            V.tensor_tensor(by_group(key_b), by_group(key_b), gbase[:].rearrange("p (g o) -> p g o", o=1).to_broadcast(
                [P, NGT, GE]), ALU.subtract)
            dve.drain()
            V.tensor_reduce(bad3[:, 0:1], past_group[:], AX_X, ALU.add)
            V.memset(group_rel[:, NKEY:], -1.0)
            V.tensor_copy(group_rel[:, 0:NKEY], key_b)
            dve.drain()
            V.tensor_reduce(bad[:], bad3[:], AX_X, ALU.add)
            dve.wait_ge(sem("group_src"), 16 * NGT)
            V.tensor_scalar(key_ai, group_src_i, P - 1, None, ALU.bitwise_and)
            dve.drain()
            V.tensor_copy(key_a, key_ai).then_inc(sem("sources_made"), 1)
            dve.drain()
            V.tensor_scalar(key_ai, group_src_i, 7, None, ALU.arith_shift_right)
            dve.drain()
            V.tensor_copy(key_c, key_ai)
            dve.drain()
            V.tensor_scalar(key_c, key_c, float(G), 1.0, ALU.mult, ALU.add)
            dve.drain()
            V.tensor_tensor(key_c, key_c, key_b, ALU.add)
            dve.drain()
            V.scalar_tensor_tensor(out=key_c, in0=key_b, scalar=0.0, in1=key_c, op0=ALU.is_ge, op1=ALU.mult)
            dve.drain()
            V.scalar_tensor_tensor(out=key_c, in0=key_b, scalar=float(G - 1), in1=key_c, op0=ALU.is_le, op1=ALU.mult)
            dve.drain()
            V.tensor_scalar(key_c, key_c, -1.0, None, ALU.add).then_inc(sem("keys_made"), 1)
            dve.wait_ge(sem("rows_written0"), 1)
            V.memset(agg[:], 0.0)
            dve.wait_ge(sem("keys_flipped"), 1)
            V.tensor_copy(keyT.rearrange("p k (g e) -> p k g e", g=NGT),
                          ps[:, 0:NKEY].rearrange("p (g k e) -> p k g e", g=NGT, k=K)).then_inc(sem("keyT_ready"), 1)
            dve.wait_ge(sem("bad_summed"), 1)
            V.tensor_scalar(any_order[:], ps[:, 0:1], 1.0, None, ALU.min)
            dve.drain()
            dve.sem_inc(sem("area_free0"), 1)
            dve.sem_inc(sem("order_known"), 1)
            order = dve.value_load(any_order[0:1, 0:1], min_val=0, max_val=1)

            def sum_any(l):
                _, weighted, counted = GEN[l]

                def f():
                    dve.wait_ge(sem("g_edges"), 48 * (l + 1))
                    V.tensor_copy(g_key, g_src if l == CLIQUES else g_dst)
                    V.tensor_scalar(g_idx, g_dst, N_CLIQUES - 1, None, ALU.min)
                    V.memset(agg[:], 0.0)
                    V.memset(g_iota, 0.0)
                    if counted:
                        V.memset(g_count, 0.0)
                    dve.drain()
                    for n in range(0, TILE, 2 * P):
                        V.tensor_scalar(g_iota[:, n:n + 2 * P], iota16[:, 0:2 * P], float(n), None, ALU.add)
                    dve.drain()
                    dve.sem_inc(sem("g_ready"), 1)
                    dve.sem_inc(sem("g_added"), 2)

                    def add(j, n):
                        t, s = n % NT, n % 2
                        dve.wait_ge(sem("g_mm"), j * (2 * NT) + mm_base(l) + n + 1 + MM_CREDIT)
                        cols, slot = slice(t * TILE, (t + 1) * TILE), slice(s * TILE, (s + 1) * TILE)
                        last = V.tensor_tensor(agg[:, cols], agg[:, cols], pA[:, slot], ALU.add)
                        if counted:
                            last = V.tensor_tensor(g_count[:, cols], g_count[:, cols], pB[:, slot], ALU.add)
                        last.then_inc(sem("g_added"), 1)

                    with dve.Fori(0, NCH // 2) as j:
                        for k in range(2):
                            dve.drain()
                            V.tensor_scalar(tile_key[:], tile_off[:], g_key[:, bass.ds(j * 2 + k, 1)], None, ALU.add)
                            dve.drain()
                            for t in range(NT):
                                n = k * NT + t
                                dve.wait_ge(sem("g_mm"), j * (2 * NT) + mm_base(l) + n - 1 + MM_CREDIT)
                                scale = (g_w[:, bass.ds(j * 2 + k, 1)], ALU.is_equal, ALU.mult) if weighted else (
                                    None, ALU.is_equal)
                                V.tensor_scalar(g_onehot[:, n % 2, :], g_iota, tile_key[:, t:t + 1],
                                                *scale).then_inc(sem("g_onehot"), 1)
                                if n:
                                    add(j, n - 1)
                        add(j, 2 * NT - 1)
                        dve.drain()
                    if l == LAYER_1:
                        dve.sem_inc(sem("g_counted"), 1)
                        dve.wait_ge(sem("deg_out"), 16)
                    if counted:
                        V.tensor_scalar(g_count, g_count, 1.0, None, ALU.max)
                        dve.drain()
                        V.reciprocal(g_count, g_count)
                        dve.drain()
                        V.tensor_tensor(agg[:], agg[:], g_count, ALU.mult)
                        dve.drain()
                    if l == CLIQUES:
                        V.tensor_copy(clique_sum, agg[:, 0:NPAD])
                        V.memset(inv_cnt[:], 1.0)
                        V.memset(out_cnt[:], 0.0)
                        dve.drain()
                        dve.sem_inc(sem("area_free2"), 1)
                    else:
                        dve.sem_inc(sem({LAYER_0: "agg_done0", LAYER_1: "agg_done1", LAYER_3: "agg_done3"}[l]), 1)
                return f

            def window_onehots(t, w):
                dve.wait_ge(sem("win_mm"), t * WPS + w + 1)
                for c in range(w * WCH, (w + 1) * WCH):
                    last = V.tensor_scalar(oh_win[:, c, :], iota_win[:], rel[:, bass.ds(t * CPS + c, 1)],
                                           w_edge[:, bass.ds(t * CPS + c, 1)], ALU.is_equal, ALU.mult)
                last.then_inc(sem("win_onehots"), 1)

            def window_bases(t, regs):
                dve.load(regs, win_base[0:1, bass.ds(t * WPS, WPS)])

            def window_adds(t, regs):
                for w in range(WPS):
                    base = dve.snap(regs[w], min_val=0, max_val=NCOL - WIN)
                    dve.drain()
                    if w == 0:
                        dve.wait_ge(sem("win_copied"), t + 1)
                    last = V.tensor_tensor(agg[:, bass.ds(base, WIN)], agg[:, bass.ds(base, WIN)],
                                           win_sum[:, w * WIN:(w + 1) * WIN], ALU.add)
                last.then_inc(sem("win_added"), 1)

            def group_onehots(t, g):
                dve.wait_ge(sem("cells"), t * GS + g + 1)
                for k in range(K):
                    s = (g % 3) * K + k
                    V.tensor_scalar(oh_src[:, s, :], iota16[:, 0:P], slT[:, k, bass.ds(t * GS + g, 1)], None,
                                    ALU.is_equal)
                    last = V.tensor_scalar(oh_cell[:, s, :], iota16[:], keyT[:, k, bass.ds(t * GS + g, 1)], None,
                                           ALU.is_equal)
                last.then_inc(sem("onehots"), 1)

            def split_cliques(b, part, slot_used=True):
                h = slice(0, HALF)
                rows, r, r2 = (v[h, :].rearrange("p (c d) -> p c d", c=2) for v in (xc_in, xc_r, xc_r2))
                plane = [xc_plane[h, bass.ds(b % 2, 1), :, l, :].rearrange("p s c n -> p (s c) n") for l in range(3)]
                if part == 0:
                    if slot_used:
                        dve.wait_ge(sem("mixed"), (b - 1) * (2 * SUBS) + 1)
                        dve.sem_inc(sem("dve_passed"), 1)
                    dve.wait_ge(sem("xc_loaded"), b * 16 + 16)
                    dve.sem_inc(sem("dve_passed"), 1)
                    V.tensor_copy(plane[0], rows)
                elif part == 1:
                    V.tensor_tensor(r, rows, plane[0], ALU.subtract)
                elif part == 2:
                    V.tensor_copy(plane[1], r)
                elif part == 3:
                    V.tensor_tensor(r2, r, plane[1], ALU.subtract)
                elif part == 4:
                    V.tensor_copy(plane[2], r2).then_inc(sem("xc_split"), 1)

            def add_mix(b, sub):
                dve.wait_ge(sem("mixed"), b * (2 * SUBS) + sub * 2 + 1)
                cols = clique_sum[:, bass.ds((sub + SUBS - 1) % SUBS * W, W)]
                V.tensor_tensor(cols, cols, p_mix, ALU.add).then_inc(sem("mix_added"), 1)

            def step(blk, sub, regs, clique):
                t = blk * SUBS + sub
                group_onehots(t, 0)
                group_onehots(t, 1)
                window_onehots(t, 0)
                group_onehots(t, 2)
                if clique:
                    add_mix(blk - 1, sub)
                group_onehots(t, 3)
                window_onehots(t, 1)
                group_onehots(t, 4)
                window_bases(t, regs)
                window_adds(t, regs)
                group_onehots(t, 5)
                window_onehots(t, 2)

            def count_sorted():
                V.memset(clique_sum, 0.0)
                V.memset(out_cnt[:], 0.0)
                V.memset(p_win, 0.0)
                V.memset(p_mix, 0.0)
                dve.drain()
                dve.sem_inc(sem("win_added"), 1)
                dve.sem_inc(sem("xc_split"), 1)
                dve.wait_ge(sem("edges_in"), 32)
                regs = [dve.alloc_register(f"win_base{w}") for w in range(WPS)]
                with dve.Fori(0, SUBS) as sub:
                    step(0, sub, regs, False)
                for part in range(5):
                    split_cliques(0, part, slot_used=False)
                    dve.drain()
                with dve.Fori(1, L2B) as blk:
                    for sub in range(SUBS):
                        step(blk, sub, regs, True)
                        split_cliques(blk, sub)
                with dve.Fori(0, SUBS) as sub:
                    step(L2B, sub, regs, True)
                add_mix(L2B, 0)
                with dve.Fori(L2B + 1, NBLK) as blk:
                    with dve.Fori(0, SUBS) as sub:
                        step(blk, sub, regs, False)
                dve.wait_ge(sem("cells"), STEPS * GS + CELL_RING)
                with dve.Fori(STEPS, STEPS + TAIL) as t:
                    for r in range(2):
                        g = t * 2 - 2 * STEPS + r
                        for j in range(G):
                            V.tensor_scalar(deg_unused[:, j, :], group_rel[:, bass.ds(g * GE, GE)], float(j), None,
                                            ALU.is_equal, ALU.add, accum_out=deg_g[:, bass.ds(g * G + j, 1)])
                        dve.drain()
                    window_bases(t, regs)
                    for w in range(WPS):
                        window_onehots(t, w)
                    window_adds(t, regs)
                    dve.drain()
                window_bases(STEPS + TAIL, regs)
                window_adds(STEPS + TAIL, regs)
                V.tensor_scalar(inv_deg_g[:], deg_g[:], 1.0, None, ALU.max)
                dve.drain()
                V.reciprocal(inv_deg_g[:], inv_deg_g[:]).then_inc(sem("deg_counted"), 1)
                dve.wait_ge(sem("block_saved"), NBLK + 1)
                dve.drain()
                dve.sem_inc(sem("agg_done0"), 1)

            def multiply(l):
                def f():
                    before = 0 if l == 1 else 1
                    dve.sem_inc(sem("taken"), 2)
                    if l == 1:
                        dve.sem_inc(sem("piece_counted"), KD)

                    def take_out(b, which):
                        slot = (b % 2) * (2 * TILE)
                        if l == 1:
                            for k in range(KD):
                                dve.wait_ge(sem(f"piece{k}"), b * 16 + 16)
                                V.tensor_reduce(out_part[:, k * SHS:(k + 1) * SHS],
                                                piece[:, k, :].rearrange("p (s d) -> p s d", d=TD), AX_X,
                                                ALU.add).then_inc(sem("piece_counted"), 1)
                            dve.wait_ge(sem("deg_in"), b * 16 + 16)
                            dve.sem_inc(sem("dve_passed"), 1)
                            dve.drain()
                            dve.wait_ge(sem("piece_counted_act"), b * (SUBS - KD) + 2 * (SUBS - KD))
                            V.tensor_tensor(out_cnt[:, which, :], out_cnt[:, which, :], out_part[:], ALU.add).then_inc(
                                sem("part_added"), 1)
                            dve.drain()
                        dve.wait_ge(sem("piece_used"), b * SUBS + before * (NBLK + 1) * SUBS + 2 * SUBS)
                        sums, cols = ps[:, bass.ds(slot, TD)], agg[:, bass.ds(b * TD, TD)]
                        if l == 1:
                            V.scalar_tensor_tensor(out=cols, in0=sums, scalar=1.0 / SCALE,
                                                   in1=inv_deg_s[:, bass.ds((b % 2) * TD, TD)], op0=ALU.mult,
                                                   op1=ALU.mult).then_inc(sem("taken"), 1)
                        else:
                            V.tensor_scalar(cols, sums, 1.0 / SCALE, None, ALU.mult).then_inc(sem("taken"), 1)
                        dve.drain()

                    with dve.Fori(0, L2B) as b:
                        take_out(b, 0)
                    with dve.Fori(L2B, NBLK) as b:
                        take_out(b, 1)
                    if l == 1:
                        V.tensor_tensor(inv_cnt[:], out_cnt[:, 0, :], out_cnt[:, 1, :], ALU.add)
                        dve.drain()
                        V.tensor_scalar(inv_cnt[:], inv_cnt[:], 1.0, None, ALU.max)
                        dve.drain()
                        V.reciprocal(inv_cnt[:], inv_cnt[:])
                        dve.drain()
                    dve.sem_inc(sem(f"agg_done{l}"), 1)
                return f

            branch(dve, order, sum_any(0), count_sorted)

            x2 = row_slots[1][0]
            dve.wait_ge(sem("consts_in"), 16 * N_CONST_LOADS)
            V.tensor_copy(last_clique[:], last_col[:].to_broadcast([P, P]))

            def prod1(i):
                dve.wait_ge(sem("hT1"), i + 1)
                dve.wait_ge(sem("agg_staged1"), i + 1)
                V.tensor_tensor(prod_s, pA[:, 0:W], agg_s[:], ALU.mult).then_inc(sem("prod1"), 1)

            def layer_0(i, more):
                dve.wait_ge(sem("lin1"), i + 1)
                if more:
                    prod1(i + 1)
                dve.wait_ge(sem("sloped"), i + 1)
                V.tensor_tensor(r_s, z_s, pB[:, 0:W], ALU.max).then_inc(sem("lin1_read"), 1)
                dve.drain()
                rows_seen(1, i)
                V.tensor_tensor(slot(x2, i), slot(x2, i), blocks(r_s), ALU.add).then_inc(sem("x_new"), 1)
                dve.drain()
                layernorm(1, i, split=1)

            prod1(0)
            with dve.Fori(0, NS - 1) as i:
                layer_0(i, True)
            layer_0(NS - 1, False)
            dve.wait_ge(sem("rows_written1"), 1)
            dve.sem_inc(sem("area_free1"), 1)
            branch(dve, order, both(sum_any(CLIQUES), sum_any(LAYER_1)), multiply(1))

            def over_blocks(t):
                return t[:].rearrange("p (o d) -> p o d", o=1).to_broadcast([P, SB, D])

            def add_bias(i, first=False):
                dve.wait_ge(sem("lin2"), i + 1)
                if not first:
                    dve.wait_ge(sem("gelu"), i)
                V.tensor_tensor(blocks(r_s), blocks(pB[:, 0:W]), over_blocks(bcast["bl"]), ALU.add).then_inc(
                    sem("biased"), 1)

            def copy_rows(i):
                dve.wait_ge(sem("hT2"), i + 1)
                V.tensor_copy(hT_s[:], pA[:, 0:W]).then_inc(sem("hT_s2"), 1)

            copy_rows(0)
            dve.wait_ge(sem("lin2"), 1)
            copy_rows(1)
            add_bias(0, True)
            with dve.Fori(1, NS - 1) as i:
                dve.wait_ge(sem("lin2"), i + 1)
                copy_rows(i + 1)
                add_bias(i)
            add_bias(NS - 1)
            dve.wait_ge(sem("mean_sum"), 1)
            V.scalar_tensor_tensor(out=scaled_mean[:], in0=pC[:, 0:D], scalar=1.0 / N_NODES, in1=bcast["mean_scale"][:],
                                   op0=ALU.mult, op1=ALU.mult)
            dve.drain()
            with dve.Fori(0, NS) as i:
                f = f_all[:, bass.ds(i * SB, SB), :]
                V.tensor_tensor(f, f, over_blocks(scaled_mean), ALU.subtract).then_inc(sem("centred"), 1)
            V.tensor_tensor(shift[:], bcast["gn_bias"][:], bcast["bc"][:], ALU.add)
            V.tensor_tensor(last_share[:], out_cnt[:, 1, :], inv_cnt[:], ALU.mult)
            dve.wait_ge(sem("clique_lin"), 1)
            V.tensor_copy(clique_out[:], pA[:, 0:D])
            V.tensor_scalar(gain[:], pC[:, 0:D], 1.0 / N_NODES, EPS, ALU.mult, ALU.add).then_inc(sem("var_ready"), 1)
            dve.wait_ge(sem("std_ready"), 1)
            V.reciprocal(scaled_mean[:], gain[:])
            dve.drain()
            V.tensor_tensor(gain[:], scaled_mean[:], bcast["gn_weight"][:], ALU.mult)
            dve.drain()
            dve.sem_inc(sem("gain_ready"), 1)

            with dve.Fori(0, NS) as i:
                rows_seen(2, i)
                dve.wait_ge(sem("lin3"), i + 2)
                dve.wait_ge(sem("beyond"), i + 1)
                n3 = blocks(n_s)
                for b in range(SB):
                    V.scalar_tensor_tensor(out=n3[:, b, :], in0=blocks(pB[:, 0:W])[:, b, :],
                                           scalar=inv_cnt[:, bass.ds(i * SB + b, 1)], in1=blocks(r_s)[:, b, :],
                                           op0=ALU.mult, op1=ALU.add)
                dve.drain()
                dve.wait_ge(sem("norm_rows"), i + 1)
                V.tensor_tensor(n_s, n_s, z_s, ALU.add)
                dve.drain()
                V.tensor_tensor(slot(x2, i), slot(x2, i), n3, ALU.add).then_inc(sem("x_new"), 1)
                dve.drain()
                layernorm(2, i, split=3)
            dve.wait_ge(sem("rows_written2"), 1)

            V.tensor_tensor(b_rz[:], b_gates["b_ih"][:, 0:2], b_gates["b_hh"][:, 0:2], ALU.add)
            dve.drain()
            dve.sem_inc(sem("b_rz_ready"), 1)
            dve.sem_inc(sem("area_free3"), 1)
            branch(dve, order, sum_any(3), multiply(3))

            b_hn = b_gates["b_hh"][:, 2:3]
            with dve.Fori(0, NS) as i:
                dve.wait_ge(sem("n_gate"), i + 1)
                dve.wait_ge(sem("r_ready"), i + 2)
                V.scalar_tensor_tensor(out=t_s, in0=pD[:, 0:W], scalar=b_hn, in1=r_s, op0=ALU.add, op1=ALU.mult)
                dve.drain()
                V.tensor_tensor(t_s, t_s, pC[:, 0:W], ALU.add).then_inc(sem("n_in"), 1)
                dve.wait_ge(sem("tanh"), i + 1)
                V.tensor_tensor(r_s, steps_of(hid2, i % 2), n_s, ALU.subtract)
                dve.drain()
                V.tensor_tensor(r_s, r_s, z_s, ALU.mult)
                dve.drain()
                V.tensor_tensor(newT_s, r_s, n_s, ALU.add).then_inc(sem("h_new"), 1)
                dve.wait_ge(sem("out_rows"), i + 1)
                dve.wait_ge(sem("x_biased"), i + 1)
                rows = steps_of(xs2, i % 2)
                V.tensor_tensor(rows, rows, pA[:, 0:W], ALU.add).then_inc(sem("y_ready"), 1)
                dve.drain()


def kernel(**inputs):
    import numpy as np
    import concourse.bacc as bacc
    from concourse.bass_utils import run_bass_kernel_spmd as run

    def edges(name, fill):
        a = np.ascontiguousarray(inputs[name])
        pad = np.full((NCH * P - N_EDGES,), fill, a.dtype)
        return np.concatenate([a, pad]).reshape(NCH, P)

    def wT(name):
        return np.ascontiguousarray(np.asarray(inputs[name]).T)

    def row(*names):
        return np.ascontiguousarray(np.stack([np.asarray(inputs[n]) for n in names]))

    x = np.ascontiguousarray(inputs["x"])
    xc = np.ascontiguousarray(inputs["L2_gnn_x_clique"])
    src, dst, w = edges("src", N_NODES), edges("dst", N_NODES), edges("edge_weight", 0)

    def gates(name):
        return np.ascontiguousarray(np.asarray(inputs[name]).reshape(3, D).T)

    arrays = {
        "x": np.concatenate([x, np.zeros((NPAD - N_NODES, D), x.dtype)]),
        "dst_rows": dst, "src_flat": src.reshape(1, -1), "dst_flat": dst.reshape(1, -1),
        "srcT": np.ascontiguousarray(src.T), "dstT": np.ascontiguousarray(dst.T), "wT": np.ascontiguousarray(w.T),
        "win_base_src": np.concatenate([np.zeros((1, WPS), dst.dtype), dst[::WCH, 0:1].T], axis=1),
        "x_clique": np.concatenate([xc, np.repeat(xc[-1:], N_XC - N_CLIQUES, axis=0)]),
        "last_clique": np.ascontiguousarray(xc[-1:].T),
        "W1T": wT("L0_gnn_W1"), "W2T": wT("L0_gnn_W2"), "WlT": wT("L1_gnn_Wl"), "WrT": wT("L1_gnn_Wr"),
        "WcT": wT("L2_gnn_W"), "WinT": wT("L3_gnn_W_in"), "Wmsg": np.ascontiguousarray(inputs["L3_gnn_W_msg"]),
        "WihT": wT("L3_gnn_W_ih"), "WhhT": wT("L3_gnn_W_hh"), "WoutT": wT("L3_gnn_W_out"),
        "b12": row("L0_gnn_b1", "L0_gnn_b2"), "bl": row("L1_gnn_bl"), "bc": row("L2_gnn_b"),
        "b_ih": gates("L3_gnn_b_ih"), "b_hh": gates("L3_gnn_b_hh"), "b_in_row": row("L3_gnn_b_in"),
        "bout": row("L3_gnn_b_out"), "b_in": np.ascontiguousarray(row("L3_gnn_b_in").T),
        "gn_weight": row("L1_gnn_gn_weight"), "gn_bias": row("L1_gnn_gn_bias"), "mean_scale": row("L1_gnn_mean_scale"),
    }
    nc = bacc.Bacc("TRN2", target_bir_lowering=False, num_devices=1)
    A, fed = {}, {}
    for name, a in arrays.items():
        A[name] = nc.dram_tensor(f"in_{name}", a.shape, mybir.dt.from_np(a.dtype), kind="ExternalInput").ap()
        fed[f"in_{name}"] = a
    out = nc.dram_tensor("out_rows_padded", (NPAD, D), F32, kind="ExternalOutput").ap()
    build_gnn(nc, A, out)
    r = run(nc, [fed], core_ids=[0])
    return r.results[0]["out_rows_padded"][:N_NODES]
```
